# Optimizing a Trainium2 kernel written in Bass

```python
import numpy as np
import jax
import jax.numpy as jnp

def _softmax(x, axis=-1):
    return jax.nn.softmax(x, axis=axis)

def _gelu(x):
    return jax.nn.gelu(x, approximate=True)

def _silu(x):
    return jax.nn.silu(x)

def _sigmoid(x):
    return jax.nn.sigmoid(x)

def _layernorm(x, axis=-1, eps=1e-05):
    m = jnp.mean(x, axis=axis, keepdims=True)
    v = jnp.var(x, axis=axis, keepdims=True)
    return (x - m) / jnp.sqrt(v + eps)

def _scatter_add(tgt, idx, src, axis=0):
    return tgt.at[idx].add(src)

def _segment_sum(src, seg, n):
    return jax.ops.segment_sum(src, seg, n)
kernel_name = 'mk_decoder_preln_d1_seqx_r4_24f6f0'

def setup_inputs(seed: int=0):
    np.random.seed(seed)
    _w = jnp.asarray

    def _rec_inputs():
        import jax
        import jax.numpy as jnp
        _rk = jax.random.key(seed)
        x = 7.22e-05 + 1 * jax.random.normal(jax.random.fold_in(_rk, 1), (2, 1024, 256), jnp.float32)
        _lenS = 1024 - jax.random.randint(jax.random.fold_in(_rk, 7), (2,), 0, max(1, 1024 // 4) + 1, jnp.int32)
        _lenS2 = 77 - jax.random.randint(jax.random.fold_in(_rk, 8), (2,), 0, max(1, 77 // 4) + 1, jnp.int32)
        _ctx_1024P = jax.random.normal(jax.random.fold_in(_rk, 11), (2, 16, 256), jnp.float32)
        _ctx_1024c = jax.random.dirichlet(jax.random.fold_in(_rk, 511), 0.3 * jnp.ones((16,), jnp.float32), (2, 77))
        _ctx_1024t = jnp.einsum('bsk,bkd->bsd', _ctx_1024c, _ctx_1024P)
        _ctx_1024t = _ctx_1024t * jax.lax.rsqrt(jnp.mean(jnp.square(_ctx_1024t)) + 1e-12) * 0.953939
        ctx_1024 = 4.13588e-05 + 0.999923 * (_ctx_1024t + 0.3 * jax.random.normal(jax.random.fold_in(_rk, 611), (2, 77, 256), jnp.float32))
        return (x, ctx_1024)
    x, ctx_1024 = _rec_inputs()

    def _L0_attn_setup():
        import jax, jax.numpy as jnp
        import numpy as np
        B, S, D, H = (2, 512, 256, 16)
        HD = D // H
        FF = 1024
        NUM_ITERS = 8
        DT = 0.1
        LN_EPS = 1e-05

        def _ln(x, g, b):
            m = jnp.mean(x, axis=-1, keepdims=True)
            v = jnp.var(x, axis=-1, keepdims=True)
            return (x - m) * jax.lax.rsqrt(v + LN_EPS) * g + b

        def _forward(x, qkv_w, qkv_b, out_w, out_b, g_attn, b_attn, g1, b1, g2, b2, w_ctx, w_x, b_inl, ff_w1, ff_b1, ff_w2, ff_b2):
            b, s, d = x.shape
            xn = _ln(x, g_attn, b_attn)
            qkv = (xn @ qkv_w + qkv_b).reshape(b, s, 3, H, HD)
            qkv = jnp.transpose(qkv, (2, 0, 3, 1, 4))
            q, k, v = (qkv[0], qkv[1], qkv[2])
            scores = jnp.einsum('bhqd,bhkd->bhqk', q, k) / np.sqrt(HD).astype(np.float32)
            causal = jnp.triu(jnp.ones((s, s), dtype=bool), 1)
            scores = jnp.where(causal[None, None], -jnp.inf, scores)
            attn_w = jax.nn.softmax(scores, axis=-1)
            attn = jnp.einsum('bhqk,bhkd->bhqd', attn_w, v)
            attn = jnp.transpose(attn, (0, 2, 1, 3)).reshape(b, s, d)
            attn = attn @ out_w + out_b
            x = x + attn
            ctx = attn.reshape(b * s, d)
            xs = _ln(x, g1, b1).reshape(b * s, d)
            vs = jnp.zeros_like(xs)

            def step(carry, _):
                xs, vs = carry
                u = jnp.tanh(ctx @ w_ctx + xs @ w_x + b_inl)
                vn = vs + DT * (u - xs - vs)
                xn_ = xs + DT * vn
                return ((xn_, vn), None)
            (xs, vs), _ = jax.lax.scan(step, (xs, vs), None, length=NUM_ITERS)
            x = x + xs.reshape(b, s, d)
            h = _ln(x, g2, b2)
            h = jax.nn.gelu(h @ ff_w1 + ff_b1, approximate=False)
            x = x + (h @ ff_w2 + ff_b2)
            return x
        key = jax.random.key(seed)
        ks = jax.random.split(key, 16)

        def xav(k, shape):
            lim = np.sqrt(6.0 / (shape[0] + shape[1]))
            return jax.random.uniform(k, shape, minval=-lim, maxval=lim, dtype=jnp.float32)
        return {'x': jax.random.normal(ks[0], (B, S, D), dtype=jnp.float32), 'qkv_w': xav(ks[1], (D, 3 * D)), 'qkv_b': jnp.zeros((3 * D,), jnp.float32), 'out_w': xav(ks[2], (D, D)), 'out_b': jnp.zeros((D,), jnp.float32), 'g_attn': jnp.ones((D,), jnp.float32), 'b_attn': jnp.zeros((D,), jnp.float32), 'g1': jnp.ones((D,), jnp.float32), 'b1': jnp.zeros((D,), jnp.float32), 'g2': jnp.ones((D,), jnp.float32), 'b2': jnp.zeros((D,), jnp.float32), 'w_ctx': xav(ks[3], (D, D)), 'w_x': xav(ks[4], (D, D)), 'b_inl': jnp.zeros((D,), jnp.float32), 'ff_w1': xav(ks[5], (D, FF)), 'ff_b1': jnp.zeros((FF,), jnp.float32), 'ff_w2': xav(ks[6], (FF, D)), 'ff_b2': jnp.zeros((D,), jnp.float32)}
    _L0_attn_all = _L0_attn_setup()
    _L0_attn_in = {k: v for k, v in _L0_attn_all.items() if k in ('qkv_w', 'qkv_b', 'out_w', 'out_b', 'g_attn', 'b_attn', 'g1', 'b1', 'g2', 'b2', 'w_ctx', 'w_x', 'b_inl', 'ff_w1', 'ff_b1', 'ff_w2', 'ff_b2')}
    del _L0_attn_all

    def _L0_xattn_setup():
        import jax, jax.numpy as jnp
        import numpy as np
        HEADS = 16
        D_MODEL = 256
        D_K = D_MODEL // HEADS
        key = jax.random.key(seed)
        ks = jax.random.split(key, 12)
        B, S = (4, 512)
        scale = 1.0 / np.sqrt(D_MODEL)
        inp = {'q': jax.random.normal(ks[0], (B, S, D_MODEL), jnp.float32), 'k': jax.random.normal(ks[1], (B, S, D_MODEL), jnp.float32), 'v': jax.random.normal(ks[2], (B, S, D_MODEL), jnp.float32), 'Wq': jax.random.normal(ks[3], (D_MODEL, D_MODEL), jnp.float32) * scale, 'bq': jnp.zeros((D_MODEL,), jnp.float32), 'Wk': jax.random.normal(ks[4], (D_MODEL, D_MODEL), jnp.float32) * scale, 'bk': jnp.zeros((D_MODEL,), jnp.float32), 'Wv': jax.random.normal(ks[5], (D_MODEL, D_MODEL), jnp.float32) * scale, 'bv': jnp.zeros((D_MODEL,), jnp.float32), 'Wo': jax.random.normal(ks[6], (D_MODEL, D_MODEL), jnp.float32) * scale, 'bo': jnp.zeros((D_MODEL,), jnp.float32)}
        return inp
    _L0_xattn_all = _L0_xattn_setup()
    _L0_xattn_in = {k: v for k, v in _L0_xattn_all.items() if k in ('Wq', 'bq', 'Wk', 'bk', 'Wv', 'bv', 'Wo', 'bo')}
    del _L0_xattn_all

    def _L0_ffn_setup():
        import jax, jax.numpy as jnp
        import numpy as np
        DIM = 256
        DEPTH = 7
        PAR = 8
        N_NODES = 2 ** (DEPTH + 1) - 1
        WIDTH = PAR * N_NODES
        key = jax.random.key(seed)
        k1, k2, k3, k4 = jax.random.split(key, 4)
        init_k = float(np.sqrt(1.0 / DIM))
        init_k2 = float(np.sqrt(1.0 / ((DEPTH + 1) * PAR)))
        oldx = jax.random.normal(k1, (4, 512, DIM), dtype=jnp.float32)
        W_in = jax.random.uniform(k2, (WIDTH, DIM), jnp.float32, -init_k, init_k)
        b_in = jax.random.uniform(k3, (WIDTH,), jnp.float32, -init_k, init_k)
        W_out = jax.random.uniform(k4, (DIM, WIDTH), jnp.float32, -init_k2, init_k2)
        return {'oldx': oldx, 'W_in': W_in, 'b_in': b_in, 'W_out': W_out}
    _L0_ffn_all = _L0_ffn_setup()
    _L0_ffn_in = {k: v for k, v in _L0_ffn_all.items() if k in ('W_in', 'b_in', 'W_out')}
    del _L0_ffn_all
    return {'x': x, 'ctx_1024': ctx_1024, 'L0_attn_qkv_w': _L0_attn_in['qkv_w'], 'L0_attn_qkv_b': _L0_attn_in['qkv_b'], 'L0_attn_out_w': _L0_attn_in['out_w'], 'L0_attn_out_b': _L0_attn_in['out_b'], 'L0_attn_g_attn': _L0_attn_in['g_attn'], 'L0_attn_b_attn': _L0_attn_in['b_attn'], 'L0_attn_g1': _L0_attn_in['g1'], 'L0_attn_b1': _L0_attn_in['b1'], 'L0_attn_g2': _L0_attn_in['g2'], 'L0_attn_b2': _L0_attn_in['b2'], 'L0_attn_w_ctx': _L0_attn_in['w_ctx'], 'L0_attn_w_x': _L0_attn_in['w_x'], 'L0_attn_b_inl': _L0_attn_in['b_inl'], 'L0_attn_ff_w1': _L0_attn_in['ff_w1'], 'L0_attn_ff_b1': _L0_attn_in['ff_b1'], 'L0_attn_ff_w2': _L0_attn_in['ff_w2'], 'L0_attn_ff_b2': _L0_attn_in['ff_b2'], 'L0_xattn_Wq': _L0_xattn_in['Wq'], 'L0_xattn_bq': _L0_xattn_in['bq'], 'L0_xattn_Wk': _L0_xattn_in['Wk'], 'L0_xattn_bk': _L0_xattn_in['bk'], 'L0_xattn_Wv': _L0_xattn_in['Wv'], 'L0_xattn_bv': _L0_xattn_in['bv'], 'L0_xattn_Wo': _L0_xattn_in['Wo'], 'L0_xattn_bo': _L0_xattn_in['bo'], 'L0_ffn_W_in': _L0_ffn_in['W_in'], 'L0_ffn_b_in': _L0_ffn_in['b_in'], 'L0_ffn_W_out': _L0_ffn_in['W_out']}

def reference(x, ctx_1024, L0_attn_qkv_w, L0_attn_qkv_b, L0_attn_out_w, L0_attn_out_b, L0_attn_g_attn, L0_attn_b_attn, L0_attn_g1, L0_attn_b1, L0_attn_g2, L0_attn_b2, L0_attn_w_ctx, L0_attn_w_x, L0_attn_b_inl, L0_attn_ff_w1, L0_attn_ff_b1, L0_attn_ff_w2, L0_attn_ff_b2, L0_xattn_Wq, L0_xattn_bq, L0_xattn_Wk, L0_xattn_bk, L0_xattn_Wv, L0_xattn_bv, L0_xattn_Wo, L0_xattn_bo, L0_ffn_W_in, L0_ffn_b_in, L0_ffn_W_out):
    import jax
    import jax.numpy as jnp

    def _L0_attn_ref(x, qkv_w, qkv_b, out_w, out_b, g_attn, b_attn, g1, b1, g2, b2, w_ctx, w_x, b_inl, ff_w1, ff_b1, ff_w2, ff_b2):
        import jax, jax.numpy as jnp
        import numpy as np
        B, S, D, H = (2, 512, 256, 16)
        HD = D // H
        FF = 1024
        NUM_ITERS = 8
        DT = 0.1
        LN_EPS = 1e-05

        def _ln(x, g, b):
            m = jnp.mean(x, axis=-1, keepdims=True)
            v = jnp.var(x, axis=-1, keepdims=True)
            return (x - m) * jax.lax.rsqrt(v + LN_EPS) * g + b

        def _forward(x, qkv_w, qkv_b, out_w, out_b, g_attn, b_attn, g1, b1, g2, b2, w_ctx, w_x, b_inl, ff_w1, ff_b1, ff_w2, ff_b2):
            b, s, d = x.shape
            xn = _ln(x, g_attn, b_attn)
            qkv = (xn @ qkv_w + qkv_b).reshape(b, s, 3, H, HD)
            qkv = jnp.transpose(qkv, (2, 0, 3, 1, 4))
            q, k, v = (qkv[0], qkv[1], qkv[2])
            scores = jnp.einsum('bhqd,bhkd->bhqk', q, k) / np.sqrt(HD).astype(np.float32)
            causal = jnp.triu(jnp.ones((s, s), dtype=bool), 1)
            scores = jnp.where(causal[None, None], -jnp.inf, scores)
            attn_w = jax.nn.softmax(scores, axis=-1)
            attn = jnp.einsum('bhqk,bhkd->bhqd', attn_w, v)
            attn = jnp.transpose(attn, (0, 2, 1, 3)).reshape(b, s, d)
            attn = attn @ out_w + out_b
            x = x + attn
            ctx = attn.reshape(b * s, d)
            xs = _ln(x, g1, b1).reshape(b * s, d)
            vs = jnp.zeros_like(xs)

            def step(carry, _):
                xs, vs = carry
                u = jnp.tanh(ctx @ w_ctx + xs @ w_x + b_inl)
                vn = vs + DT * (u - xs - vs)
                xn_ = xs + DT * vn
                return ((xn_, vn), None)
            (xs, vs), _ = jax.lax.scan(step, (xs, vs), None, length=NUM_ITERS)
            x = x + xs.reshape(b, s, d)
            h = _ln(x, g2, b2)
            h = jax.nn.gelu(h @ ff_w1 + ff_b1, approximate=False)
            x = x + (h @ ff_w2 + ff_b2)
            return x
        return _forward(x, qkv_w, qkv_b, out_w, out_b, g_attn, b_attn, g1, b1, g2, b2, w_ctx, w_x, b_inl, ff_w1, ff_b1, ff_w2, ff_b2)

    def _L0_xattn_ref(q, k, v, Wq, bq, Wk, bk, Wv, bv, Wo, bo):
        import jax, jax.numpy as jnp
        import numpy as np
        HEADS = 16
        D_MODEL = 256
        D_K = D_MODEL // HEADS
        B, S, _ = q.shape

        def proj(x, W, b):
            return (x @ W.T + b).reshape(B, -1, HEADS, D_K).transpose(0, 2, 1, 3)
        qh = proj(q, Wq, bq)
        kh = proj(k, Wk, bk)
        vh = proj(v, Wv, bv)
        scores = jnp.einsum('bhsd,bhtd->bhst', qh, kh) / jnp.sqrt(jnp.float32(D_K))
        attn = jax.nn.softmax(scores, axis=-1)
        ctx = jnp.einsum('bhst,bhtd->bhsd', attn, vh)
        concat = ctx.transpose(0, 2, 1, 3).reshape(B, S, D_MODEL)
        return concat @ Wo.T + bo

    def _L0_ffn_ref(oldx, W_in, b_in, W_out):
        import jax, jax.numpy as jnp
        import numpy as np
        DIM = 256
        DEPTH = 7
        PAR = 8
        N_NODES = 2 ** (DEPTH + 1) - 1
        WIDTH = PAR * N_NODES
        x = oldx.reshape(-1, DIM)
        B = x.shape[0]
        logits = x @ W_in.T + b_in
        decisions = (logits > 0).astype(jnp.int32).reshape(B, PAR, N_NODES)
        acts = jax.nn.silu(logits).reshape(B, PAR, N_NODES)
        current = jnp.zeros((B, PAR), dtype=jnp.int32)
        dmap = jax.nn.one_hot(current, N_NODES, dtype=acts.dtype)
        for d in range(DEPTH):
            cur_platform = 2 ** d - 1
            next_platform = 2 ** (d + 1) - 1
            moves = jnp.take_along_axis(decisions, current[..., None], axis=2)[..., 0]
            current = (current - cur_platform) * 2 + moves + next_platform
            dmap = dmap + jax.nn.one_hot(current, N_NODES, dtype=acts.dtype)
        masked = acts * jax.lax.stop_gradient(dmap)
        out = masked.reshape(B, WIDTH) @ W_out.T
        return out.reshape(oldx.shape)
    x = x + _L0_attn_ref(_layernorm(x, axis=-1), L0_attn_qkv_w, L0_attn_qkv_b, L0_attn_out_w, L0_attn_out_b, L0_attn_g_attn, L0_attn_b_attn, L0_attn_g1, L0_attn_b1, L0_attn_g2, L0_attn_b2, L0_attn_w_ctx, L0_attn_w_x, L0_attn_b_inl, L0_attn_ff_w1, L0_attn_ff_b1, L0_attn_ff_w2, L0_attn_ff_b2)
    x = x + _L0_xattn_ref(_layernorm(x, axis=-1), ctx_1024, ctx_1024, L0_xattn_Wq, L0_xattn_bq, L0_xattn_Wk, L0_xattn_bk, L0_xattn_Wv, L0_xattn_bv, L0_xattn_Wo, L0_xattn_bo)
    x = x + _L0_ffn_ref(_layernorm(x, axis=-1), L0_ffn_W_in, L0_ffn_b_in, L0_ffn_W_out)
    return x

_drawn_inputs = setup_inputs


def setup_inputs(seed=0):
    import zlib

    import numpy as np

    out = dict(_drawn_inputs(seed))
    spreads = {'L0_attn_qkv_b': (0.0, 0.1),
     'L0_attn_out_b': (0.0, 0.1),
     'L0_attn_g_attn': (1.0, 0.6),
     'L0_attn_b_attn': (0.0, 0.1),
     'L0_attn_g1': (1.0, 0.2),
     'L0_attn_b1': (0.0, 0.1),
     'L0_attn_g2': (1.0, 0.2),
     'L0_attn_b2': (0.0, 0.341),
     'L0_attn_b_inl': (0.0, 0.8),
     'L0_attn_ff_b1': (0.0, 0.1),
     'L0_attn_ff_b2': (0.0, 0.1),
     'L0_xattn_bq': (0.0, 0.543),
     'L0_xattn_bk': (0.0, 0.8),
     'L0_xattn_bv': (0.0, 0.1),
     'L0_xattn_bo': (0.0, 0.1)}
    factors = {'L0_attn_w_ctx': 3.586, 'L0_ffn_b_in': 2.777}
    for name, (base, spread) in spreads.items():
        noise = np.random.default_rng([zlib.crc32(name.encode()), seed]).standard_normal(out[name].shape)
        drawn = base * np.exp(spread * noise) if base else spread * noise
        out[name] = jnp.asarray(drawn.astype(out[name].dtype))
    for name, factor in factors.items():
        out[name] = (out[name] * factor).astype(out[name].dtype)
    return out
```

```python
from contextlib import ExitStack

import concourse.bass as bass
from concourse import mybir

F32 = mybir.dt.float32
F32R = mybir.dt.float32r
BF16 = mybir.dt.bfloat16
ALU = mybir.AluOpType
ACT = mybir.ActivationFunctionType
AX_X = mybir.AxisListType.X

P = 128
BATCH, SEQ, D = 2, 1024, 256
TOK = BATCH * SEQ
KT = D // P
CH = 512
NCH = TOK // CH
HEADS, HD = 16, 16
CTX = 77
CTXP = 78
FF = 1024
FT = FF // P
NITER, DT = 8, 0.1
TREES, DEPTH = 8, 7
NODES = 2 ** (DEPTH + 1) - 1
INNER = 2 ** DEPTH - 1
LEAVES = NODES - INNER
EPS = 1e-5
SCALE = HD ** -0.5
LOW = -1e30

VEC = {}
for _name, _n in [("bqk", 4), ("g_attn", 2), ("b_attn", 2), ("bo", 2), ("g1", 2), ("b1", 2), ("binl", 2),
                  ("g2", 2), ("b2", 2), ("ffb1", FT), ("ffb2", 2), ("xbq", 2), ("xbk", 2), ("xbo", 2),
                  ("tin", TREES), ("tleaf", TREES), ("right", 2), ("eps", 1)]:
    VEC[_name] = (sum(n for _, n in VEC.values()), _n)
NVEC = sum(n for _, n in VEC.values())

QUADS = 2
ITS = KT * BATCH


def layer(nc, a, out_t):
    ctx = ExitStack()
    with ctx:
        def sb(name, shape, dt=F32, stack=ctx):
            return stack.enter_context(nc.sbuf_tensor(name, shape, dt))

        def sem(name):
            return ctx.enter_context(nc.semaphore(name))

        psum = ctx.enter_context(nc.psum_tensor("psum", [P, 8, CH], F32))
        pflat = psum[:].rearrange("p b n -> p (b n)")

        def bank(i, n=CH):
            return psum[:, i, 0:n]

        def dbank(i):
            return pflat[:, bass.ds(i * CH, CH)]

        def tok(t, k, c):
            return t[:, k, bass.ds(c * CH, CH)]

        vec = sb("vec", [P, NVEC])
        mean_w = sb("mean_w", [P, P])
        ident = sb("ident", [P, P])
        ident_b = sb("ident_b", [P, P], BF16)
        causal_b = sb("causal_b", [P, P], BF16)
        vbias = sb("vbias", [P, D])
        res = sb("res", [P, KT, TOK])
        nrm = sb("nrm", [P, KT, TOK])
        rstd = sb("rstd", [P, TOK])
        wide = sb("wide", [P, KT, TOK])
        w3 = sb("w3", [P, KT, 3 * D])
        part_max = sb("part_max", [P, 64])
        row_max = sb("row_max", [P, 32])
        neg_max = sb("neg_max", [32, P], F32R)

        def v_(name, i=0, rows=P):
            at = VEC[name][0] + i
            return vec[0:rows, at:at + 1]

        values = wide[:].rearrange("p k t -> p (k t)").rearrange("p (i t f) -> p i t f", i=ITS, f=P)
        stage = rstd[:].rearrange("p (q n) -> p q n", q=2)

        s_first = ExitStack()
        dev1 = sb("dev1", [P, KT, TOK], F32, s_first)
        rstd2 = sb("rstd2", [P, TOK], F32, s_first)
        caus_f = sb("caus_f", [P, P], F32, s_first)
        s_first.close()

        s_self = ExitStack()
        q_hi = sb("q_hi", [P, KT, TOK], F32, s_self)
        q_lo = sb("q_lo", [P, KT, TOK], F32, s_self)
        k_hi = sb("k_hi", [P, KT, TOK], F32, s_self)
        k_lo = sb("k_lo", [P, KT, TOK], F32, s_self)
        q1 = sb("q1", [P, 2, SEQ], F32R, s_self)
        k1 = sb("k1", [P, 2, SEQ], F32R, s_self)
        q2 = sb("q2", [P, 2, 2, SEQ], F32R, s_self)
        k2 = sb("k2", [P, 2, 2, SEQ], F32R, s_self)
        vq = sb("vq", [P, 2, SEQ // P, 4, 32], F32, s_self)
        prob = sb("prob", [P, 2, 2, 2, CH], F32, s_self)
        s_self.close()

        dev = sb("dev", [P, KT, TOK])
        wx4 = sb("wx4", [P, KT, 4 * D])
        win = sb("win", [P, KT, TREES * NODES])
        wout_in = sb("wout_in", [P, TREES, D])
        wout_leaf = sb("wout_leaf", [P, TREES, D])
        ctx_t = sb("ctx_t", [P, KT, BATCH * CTXP])
        sel_f = sb("sel_f", [P, NODES])
        sel = sb("sel", [P, NODES], BF16)
        xvbias = sb("xvbias", [P, D])
        s_mlp = ExitStack()
        wff1 = sb("wff1", [P, KT, FF], F32, s_mlp)
        wff2 = sb("wff2", [P, FT, D], F32, s_mlp)
        s_scan = ExitStack()
        attn_o = sb("attn_o", [P, KT, TOK], F32, s_scan)
        vel = sb("vel", [P, KT, TOK], F32, s_scan)
        act_u = sb("act_u", [P, KT, TOK], F32, s_scan)
        wx01 = sb("wx01", [P, KT, D], F32, s_scan)
        s_scan.close()
        hid = sb("hid", [P, 2, FT, CH], F32, s_mlp)
        x0 = sb("x0", [P, KT, TOK], F32, s_mlp)
        s_mlp.close()
        s_cross = ExitStack()
        xq_hi = sb("xq_hi", [P, KT, TOK], F32, s_cross)
        xq_lo = sb("xq_lo", [P, KT, TOK], F32, s_cross)
        xk_hi = sb("xk_hi", [P, KT, BATCH * CTXP], F32, s_cross)
        xk_lo = sb("xk_lo", [P, KT, BATCH * CTXP], F32, s_cross)
        xvals = sb("xvals", [P, ITS, P], F32, s_cross)
        xq1 = sb("xq1", [P, 2, SEQ], F32R, s_cross)
        xk1 = sb("xk1", [P, 2, CTXP], F32R, s_cross)
        xq2 = sb("xq2", [P, 2, 2, SEQ], F32R, s_cross)
        xk2 = sb("xk2", [P, 2, 2, CTXP], F32R, s_cross)
        xvq = sb("xvq", [P, 2, 1, 4, 32], F32, s_cross)
        xprob = sb("xprob", [P, 2, 2, 2, CH], F32, s_cross)
        s_cross.close()
        s_tree = ExitStack()
        silu = sb("silu", [P, 2, 2, CH], F32, s_tree)
        masked = sb("masked", [P, 2, 2, CH], F32, s_tree)
        decide = sb("decide", [P, 2, CH], BF16, s_tree)
        s_tree.close()

        x_in = [sem(f"x_in{c}") for c in range(NCH)]
        c_in, w_in3, w_out3, w_late, x0_in, out_st = [
            sem(n) for n in ("c_in", "w_in3", "w_out3", "w_late", "x0_in", "out_st")]
        consts, wx01_ready, scan_init = sem("consts"), sem("wx01_ready"), sem("scan_init")

        class Norm:

            def __init__(self, name, src, ready, per, d, mean_bank, var_bank, gain=None):
                self.src, self.ready, self.per, self.d = src, ready, per, d
                self.mean_bank, self.var_bank, self.gain = mean_bank, var_bank, gain
                self.mean, self.d_ready, self.sq, self.var, self.sd, self.rs, self.scaled, self.out = [
                    sem(f"{name}_{s}") for s in ("mean", "d_ready", "sq", "var", "sd", "rs", "scaled", "out")]

        res1, res2, res4, res5 = sem("res1"), sem("res2"), sem("res4"), sem("res5")
        ln1 = Norm("ln1", nrm, None, 0, dev1, lambda c: c, lambda c: c + 4)
        ln2 = Norm("ln2", res, res1, 2, dev, lambda c: 2 * c, lambda c: 2 * c + 1, ("g1", "b1"))
        ln3 = Norm("ln3", res, res2, 2, dev, lambda c: c, lambda c: c + 4, ("g2", "b2"))
        ln4 = Norm("ln4", res, res4, 2, dev, lambda c: c, lambda c: c + 4)
        ln5 = Norm("ln5", res, res5, 2, dev, lambda c: 2 * c, lambda c: 2 * c + 1)
        sd2, rs2, r1sq, v2, xl_ready = sem("sd2"), sem("rs2"), sem("r1sq"), sem("v2"), sem("xl_ready")

        qk_ps, qk_hi, qk_free, v_ps, v_done = [sem(n) for n in ("qk_ps", "qk_hi", "qk_free", "v_ps", "v_done")]
        xq_ps, xq_hi_s, xq_free, xk_ps, xk_hi_s, xk_free, xv_ps, xv_done = [
            sem(n) for n in ("xq_ps", "xq_hi_s", "xq_free", "xk_ps", "xk_hi_s", "xk_free", "xv_ps", "xv_done")]
        attn_ready, op_ps, ctx_ready = sem("attn_ready"), sem("op_ps"), sem("ctx_ready")
        y_ready, z_ps, u_ready, a_ready, vel_ready = [
            sem(n) for n in ("y_ready", "z_ps", "u_ready", "a_ready", "vel_ready")]
        ff1_ps, gelu, ff2_ps, x3 = sem("ff1_ps"), sem("gelu"), sem("ff2_ps"), sem("x3")
        xattn_ready, xo_ps = sem("xattn_ready"), sem("xo_ps")
        lg_ps, silu_ready, dec_ready, cnt_ps, msk_ready, msk_used, tree_out = [
            sem(n) for n in ("lg_ps", "silu_ready", "dec_ready", "cnt_ps", "msk_ready", "msk_used", "tree_out")]

        class Attention:

            def __init__(self, name, steps, units, causal, keys, width, halves, bufs, sched, turn):
                self.steps, self.units, self.causal, self.keys, self.width = steps, units, causal, keys, width
                self.q_hi, self.q_lo, self.k_hi, self.k_lo = halves
                self.q1, self.k1, self.q2, self.k2, self.vq, self.prob, self.out = bufs
                self.sched, self.turn = sched, turn
                self.ld1, self.ld2, self.o_out = [[sem(f"{name}_{s}{qd}") for qd in range(QUADS)]
                                                  for s in ("ld1", "ld2", "o_out")]
                (self.s1_ps, self.s1_free, self.part, self.mx, self.mx_ps, self.neg, self.mrow, self.st_ps,
                 self.prob_ready, self.prob_masked, self.vq_ready, self.pv_ps, self.o_done, self.mask_go,
                 self.store_go) = [sem(f"{name}_{s}") for s in (
                    "s1_ps", "s1_free", "part", "mx", "mx_ps", "neg", "mrow", "st_ps", "prob_ready", "prob_masked",
                    "vq_ready", "pv_ps", "o_done", "mask_go", "store_go")]
                self.nsteps = len(self.steps)
                self.nunits = len(self.units)
                self.ndiag = sum(st[3] for st in self.steps)

        TPC = CH // P
        self_steps = [(c, kt, max(0, (kt - TPC * c) * P), kt >= TPC * c, kt == 0, kt == TPC * (c + 1) - 1)
                      for c in range(SEQ // CH) for kt in range(TPC * (c + 1))]
        self_units = [(2 * p + j, 5 + j, i, h * CH, min(CH, (i + 1) * P - h * CH), i // TPC == h)
                      for p in range(2) for i in range(SEQ // P) for h in range(i // TPC + 1) for j in range(2)]
        cross_steps = [(c, 0, 0, False, True, True) for c in range(SEQ // CH)]
        cross_units = [(2 * p + j, 5 + j, i, 0, CTXP, False)
                       for i in range(0, SEQ // P, 4) for p in range(2) for j in range(2)]
        SA = Attention("sa", self_steps, self_units, True, P, SEQ, (q_hi, q_lo, k_hi, k_lo),
                       (q1, k1, q2, k2, vq, prob, nrm), [5, 5, 5, 5, 5, 5, 5, 5, 4, 4, 0, 0], 10)
        XA = Attention("xa", cross_steps, cross_units, False, CTX, CTXP, (xq_hi, xq_lo, xk_hi, xk_lo),
                       (xq1, xk1, xq2, xk2, xvq, xprob, wide), [8, 0], 1)

        def flat(t):
            return t[:].rearrange("p k t -> p (k t)")

        def over_iterations(eng, body):
            with eng.Fori(0, ITS - 1) as it:
                for qd in range(QUADS):
                    body(it, qd, True)
            for qd in range(QUADS):
                body(ITS - 1, qd, qd < QUADS - 1)

        block = ctx.enter_context(nc.Block())

        @block.sync
        def _(sp):
            for c in range(NCH):
                sp.dma_start(nrm[:, :, c * CH:(c + 1) * CH], a["xT"][:, :, c * CH:(c + 1) * CH]).then_inc(x_in[c], 16)
            sp.dma_start(w3[:], a["wqkv"]).then_inc(w_in3, 16)

            def load_first(A, it, qd):
                sp.wait_ge(A.mx_ps, 2 * it + qd + 1)
                for h in range(4):
                    at = slice(64 * qd + 16 * h, 64 * qd + 16 * h + 16)
                    to = slice(32 * h, 32 * h + 16)
                    sp.dma_start(A.q1[to, qd, :].bitcast(F32), flat(A.q_hi)[at, bass.ds(it * SEQ, SEQ)])\
                        .then_inc(A.ld1[qd], 16)
                    sp.dma_start(A.k1[to, qd, :].bitcast(F32), flat(A.k_hi)[at, bass.ds(it * A.width, A.width)])\
                        .then_inc(A.ld1[qd], 16)

            def load_second(A, it, qd):
                sp.wait_ge(A.pv_ps, 2 * (2 * it + qd) + 2)
                for h in range(4):
                    at = slice(64 * qd + 16 * h, 64 * qd + 16 * h + 16)
                    for r, (qs, ks) in enumerate([(A.q_hi, A.k_hi), (A.q_hi, A.k_lo), (A.q_lo, A.k_hi)]):
                        to = slice(64 * (h % 2) + 16 * r, 64 * (h % 2) + 16 * r + 16)
                        sp.dma_start(A.q2[to, qd, h // 2, :].bitcast(F32), flat(qs)[at, bass.ds(it * SEQ, SEQ)])\
                            .then_inc(A.ld2[qd], 16)
                        sp.dma_start(A.k2[to, qd, h // 2, :].bitcast(F32),
                                     flat(ks)[at, bass.ds(it * A.width, A.width)]).then_inc(A.ld2[qd], 16)

            def load_max(A, it, qd):
                sp.wait_ge(A.neg, 2 * it + qd + 2)
                for h in range(4):
                    row = 64 * (h % 2) + 48
                    sp.dma_start(A.q2[row:row + 1, qd, h // 2, :].bitcast(F32),
                                 neg_max[8 * h:8 * h + 8, :].bitcast(F32)).then_inc(A.mrow, 16)

            def store_out(A, it, qd):
                sp.wait_ge(A.o_done, 2 * (2 * it + qd) + 3)
                sp.sem_inc(A.store_go, 1)
                for h in range(4):
                    to = slice(64 * qd + 16 * h, 64 * qd + 16 * h + 16)
                    sp.dma_start(flat(A.out)[to, bass.ds(it * SEQ, SEQ)], stage[32 * h:32 * h + 16, qd, :])\
                        .then_inc(A.o_out[qd], 16)
                    sp.dma_start(flat(A.q_lo)[to, bass.ds(it * SEQ, SEQ)], stage[32 * h + 16:32 * h + 32, qd, :])\
                        .then_inc(A.o_out[qd], 16)

            def attention(A):
                sp.sem_inc(A.mrow, 64)
                for qd in range(QUADS):
                    sp.sem_inc(A.o_out[qd], 128)
                load_first(A, 0, 0)
                load_second(A, 0, 0)
                load_first(A, 0, 1)

                def quad(it, qd, more):
                    load_max(A, it, qd)
                    if more:
                        load_second(A, it + (qd == 1), 1 - qd)
                    if qd == 0 or more:
                        if isinstance(it, int) and it == ITS - 1:
                            pass
                        else:
                            load_first(A, it + 1, qd)
                    store_out(A, it, qd)

                over_iterations(sp, quad)

            sp.wait_ge(qk_free, 4 + 4 * NCH)
            attention(SA)
            sp.wait_ge(attn_ready, NCH)
            for t, n in ((wff1, "wff1"), (wff2, "wff2"), (wx4, "wx4"), (win, "win"), (ctx_t, "ctxT"),
                         (wout_in[0:INNER], "wout_in"), (wout_leaf, "wout_leaf"), (sel_f[0:INNER], "sel"),
                         (xvbias, "xvbias")):
                sp.dma_start(t[:] if t in (wff1, wff2, wx4, win, ctx_t, wout_leaf, xvbias) else t, a[n])\
                    .then_inc(w_late, 16)
            sp.wait_ge(res2, 2 * NCH)
            sp.dma_start(x0[:], a["xT"]).then_inc(x0_in, 16)
            sp.wait_ge(xq_free, 4 + 2 * NCH)
            sp.wait_ge(xk_free, 2)
            sp.wait_ge(consts, 4)
            attention(XA)
            with sp.Fori(0, NCH) as c:
                sp.wait_ge(tree_out, 2 * c + 2 + 2)
                sp.dma_start(out_t[:, :, bass.ds(c * CH, CH)], res[:, :, bass.ds(c * CH, CH)]).then_inc(out_st, 16)
            sp.wait_ge(out_st, 16 * NCH)

        @block.gpsimd
        def _(pool):
            pool.memset(vq[:], 1.0)
            pool.memset(k2[:].bitcast(F32), 1.0)
            pool.memset(part_max[:], -3e38)
            pool.wait_ge(c_in, 16 * 4)
            pool.tensor_copy(ident_b[:], ident[:])
            pool.tensor_copy(causal_b[:], caus_f[:]).then_inc(consts, 1)

            def attention(A, vals, ready):
                nk = 1 if not A.causal else SEQ // P

                def copy_values(it, qd):
                    pool.wait_ge(A.pv_ps, 2 * (2 * it + qd) + 2)
                    if A.causal:
                        src = vals[:, bass.ds(it, 1), :, 64 * qd:64 * qd + 64]\
                            .rearrange("p o t (h d) -> p (o t) h d", h=4)
                    else:
                        src = vals[0:A.keys, bass.ds(it, 1), 64 * qd:64 * qd + 64]\
                            .rearrange("p o (h d) -> p o h d", h=4)
                    pool.tensor_copy(A.vq[0:A.keys, qd, :, :, 0:HD], src).then_inc(A.vq_ready, 1)

                pool.wait_ge(*ready)
                copy_values(0, 0)

                def quad(it, qd, more):
                    n = 2 * it + qd
                    if more:
                        copy_values(it + (qd == 1), 1 - qd)
                    k = 0
                    for s, (c, kt, q0, diag, first, last) in enumerate(A.steps):
                        if not diag:
                            continue
                        for p in range(2):
                            pool.wait_ge(A.prob_ready, 2 * (n * A.nsteps + s) + p + 3)
                            pool.sem_inc(A.mask_go, 1)
                            blk = A.prob[:, s % 2, p, :, q0:q0 + P]
                            pool.affine_select(out=blk, in_=blk, compare_op=ALU.is_ge, fill=0.0, base=0,
                                               pattern=[[0, 2], [1, P]], channel_multiplier=-1)\
                                .then_inc(A.prob_masked, 1)

                over_iterations(pool, quad)

            attention(SA, values, (v_done, 16))
            pool.wait_ge(w_out3, 48)
            pool.wait_ge(attn_ready, NCH)
            pool.tensor_scalar(wx01[:], w3[:, :, 2 * D:3 * D], DT * DT, None, ALU.mult).then_inc(wx01_ready, 1)
            pool.memset(vel[:], 0.0).then_inc(scan_init, 1)
            for u in range(2 * NCH):
                at = slice((u // 2) * CH, (u // 2 + 1) * CH)
                pool.wait_ge(ln2.out, u + 1)
                pool.tensor_scalar(nrm[:, u % 2, at], nrm[:, u % 2, at], 1 / (DT * DT), None, ALU.mult)\
                    .then_inc(y_ready, 1)
            with pool.Fori(0, NITER) as s:
                for u in range(2 * NCH):
                    at = slice((u // 2) * CH, (u // 2 + 1) * CH)
                    pool.wait_ge(vel_ready, 8 * s + u + 1)
                    pool.tensor_tensor(nrm[:, u % 2, at], nrm[:, u % 2, at], vel[:, u % 2, at], ALU.add)\
                        .then_inc(y_ready, 1)
            pool.wait_ge(w_late, 16 * 9)
            pool.tensor_copy(sel[0:INNER], sel_f[0:INNER]).then_inc(consts, 1)
            pool.wait_ge(x0_in, 16)
            with pool.Fori(0, NCH) as c:
                for m in range(KT):
                    pool.wait_ge(x3, 2 * c + m + 1 + 4)
                    pool.tensor_tensor(tok(res, m, c), tok(res, m, c), tok(x0, m, c), ALU.add).then_inc(res4, 1)
            pool.wait_ge(ln4.out, 2 * NCH)
            pool.memset(xvq[:], 1.0).then_inc(consts, 1)
            pool.memset(xk2[:].bitcast(F32), 1.0).then_inc(consts, 1)
            pool.wait_ge(consts, 4)
            attention(XA, xvals, (xv_done, 2))

        @block.scalar
        def _(act):
            for t, n in ((vec[:], "vec"), (ident[:], "ident"), (caus_f[:], "causal"), (mean_w[:], "mean_w")):
                act.dma_start(t, a[n]).then_inc(c_in, 16)
            act.dma_start(vbias[:], a["vbias"]).then_inc(w_in3, 16)
            act.wait_ge(c_in, 64)

            def square(L):
                with act.Fori(0, NCH) as c:
                    act.wait_ge(L.d_ready, 2 * c + 2)
                    act.activation(wide[:, :, bass.ds(c * CH, CH)], L.d[:, :, bass.ds(c * CH, CH)], ACT.Square)\
                        .then_inc(L.sq, 1)

            def deviation(L):
                with act.Fori(0, NCH) as c:
                    act.wait_ge(L.var, c + 1)
                    act.activation(rstd[:, bass.ds(c * CH, CH)], dbank(L.var_bank(c)), ACT.Sqrt, bias=v_("eps"))\
                        .then_inc(L.sd, 1)

            def add_bias(L):
                with act.Fori(0, NCH) as c:
                    for k in range(KT):
                        act.wait_ge(L.scaled, 2 * c + k + 1)
                        act.activation(tok(nrm, k, c), tok(nrm, k, c), ACT.Identity, bias=v_(L.gain[1], k))\
                            .then_inc(L.out, 1)

            square(ln1)
            deviation(ln1)
            with act.Fori(0, NCH) as c:
                act.wait_ge(v2, c + 1)
                act.activation(rstd2[:, bass.ds(c * CH, CH)], rstd2[:, bass.ds(c * CH, CH)], ACT.Sqrt,
                               bias=v_("eps")).then_inc(sd2, 1)
            with act.Fori(0, NCH) as c:
                for k in range(KT):
                    act.wait_ge(ln1.scaled, 2 * c + k + 1)
                    act.activation(tok(nrm, k, c), tok(nrm, k, c), ACT.Identity, bias=v_("b_attn", k))\
                        .then_inc(ln1.out, 1)
            with act.Fori(0, NCH) as c:
                for m in range(4):
                    act.wait_ge(qk_ps, 4 * c + m + 1)
                    hi = q_hi if m < 2 else k_hi
                    act.activation(tok(hi, m % 2, c).bitcast(F32R), bank(m), ACT.Identity, bias=v_("bqk", m))\
                        .then_inc(qk_hi, 1)

            def attention(A):
                act.sem_inc(A.prob_ready, 2)
                act.sem_inc(A.o_done, 1)

                def quad(it, qd, more):
                    n = 2 * it + qd
                    for s, (c, kt, q0, diag, first, last) in enumerate(A.steps):
                        g = n * A.nsteps + s
                        for p in range(2):
                            act.wait_ge(A.st_ps, 2 * g + p + 1)
                            act.activation(A.prob[0:A.keys, s % 2, p, :, q0:CH],
                                           psum[0:A.keys, 2 * p:2 * p + 2, q0:CH], ACT.Exp, scale=SCALE)\
                                .then_inc(A.prob_ready, 1)
                        if s > 0 and A.steps[s - 1][5]:
                            read_out(it, qd, A.steps[s - 1][0])
                    read_out(it, qd, A.steps[-1][0])

                def read_out(it, qd, c):
                    n = 2 * it + qd
                    act.wait_ge(A.pv_ps, 2 * n + c + 1 + 4)
                    act.wait_ge(A.o_out[qd], 128 * it + 128)
                    act.activation(stage[:, qd, c * CH:(c + 1) * CH], bank(4), ACT.Copy).then_inc(A.o_done, 1)

                over_iterations(act, quad)

            attention(SA)
            act.wait_ge(v_ps, 8)
            for i, n in enumerate(("wo", "wctx", "wx")):
                act.dma_start(w3[:, :, i * D:(i + 1) * D], a[n]).then_inc(w_out3, 16)
            act.wait_ge(attn_ready, NCH)
            with act.Fori(0, NCH) as c:
                for m in range(KT):
                    act.wait_ge(op_ps, 2 * c + m + 1)
                    act.activation(tok(attn_o, m, c), dbank(2 * c + m), ACT.Identity, bias=v_("bo", m))\
                        .then_inc(ctx_ready, 1)
            square(ln2)
            deviation(ln2)
            add_bias(ln2)
            with act.Fori(0, NITER) as s:
                for u in range(2 * NCH):
                    at = slice((u // 2) * CH, (u // 2 + 1) * CH)
                    act.wait_ge(z_ps, 8 * s + 2 * (u // 2) + 2)
                    act.activation(act_u[:, u % 2, at], bank(u), ACT.Tanh, bias=v_("binl", u % 2))\
                        .then_inc(u_ready, 1)
            square(ln3)
            deviation(ln3)
            add_bias(ln3)
            with act.Fori(0, NCH // 2) as cc:
                for half in range(2):
                    for m in range(FT):
                        act.wait_ge(ff1_ps, FT * (2 * cc + half) + m + 1)
                        act.wait_ge(ff2_ps, 2 * (2 * cc + half) + 2 - 2)
                        act.activation(hid[:, half, m, :], bank(m % 4), ACT.Gelu, bias=v_("ffb1", m))\
                            .then_inc(gelu, 1)
            square(ln4)
            deviation(ln4)
            with act.Fori(0, NCH) as c:
                for m in range(KT):
                    act.wait_ge(xq_ps, 2 * c + m + 1)
                    act.activation(tok(xq_hi, m, c).bitcast(F32R), dbank(2 * c + m), ACT.Identity,
                                   bias=v_("xbq", m)).then_inc(xq_hi_s, 1)
            for m in range(KT):
                act.wait_ge(xk_ps, m + 1)
                act.activation(xk_hi[:, m, :].bitcast(F32R), bank(m, BATCH * CTXP), ACT.Identity,
                               bias=v_("xbk", m)).then_inc(xk_hi_s, 1)
            attention(XA)
            square(ln5)
            deviation(ln5)
            act.sem_inc(silu_ready, 4)
            with act.Fori(0, NCH) as c:
                for t in range(TREES):
                    g = c * TREES + t
                    for half, (rows, bias) in enumerate(((INNER, "tin"), (LEAVES, "tleaf"))):
                        act.wait_ge(lg_ps, 2 * g + half + 1)
                        if half == 0:
                            act.wait_ge(dec_ready, g + 1 + 2)
                        act.wait_ge(msk_ready, 2 * g + half + 1)
                        act.activation(silu[0:rows, t % 2, half, :], bank(2 * (t % 2) + half)[0:rows], ACT.Silu,
                                       bias=v_(bias, t, rows)).then_inc(silu_ready, 1)

        @block.vector
        def _(dve):
            dve.sem_inc(qk_free, 4)
            dve.wait_ge(c_in, 64)

            def center(L):
                with dve.Fori(0, NCH) as c:
                    dve.wait_ge(L.mean, c + 1)
                    for k in range(KT):
                        dve.tensor_tensor(tok(L.d, k, c), tok(L.src, k, c), dbank(L.mean_bank(c)), ALU.subtract)\
                            .then_inc(L.d_ready, 1)

            def scale(L):
                with dve.Fori(0, NCH) as c:
                    r = rstd[:, bass.ds(c * CH, CH)]
                    dve.wait_ge(L.sd, c + 1)
                    dve.reciprocal(r, r).then_inc(L.rs, 1)
                    dve.wait_ge(L.rs, c + 1)
                    for k in range(KT):
                        if L.gain:
                            dve.scalar_tensor_tensor(tok(nrm, k, c), tok(L.d, k, c), v_(L.gain[0], k), r,
                                                     ALU.mult, ALU.mult).then_inc(L.scaled, 1)
                        else:
                            dve.tensor_tensor(tok(nrm, k, c), tok(L.d, k, c), r, ALU.mult).then_inc(L.out, 1)

            center(ln1)
            with dve.Fori(0, NCH) as c:
                r = rstd[:, bass.ds(c * CH, CH)]
                r2 = rstd2[:, bass.ds(c * CH, CH)]
                dve.wait_ge(ln1.sd, c + 1)
                dve.reciprocal(r, r).then_inc(ln1.rs, 1)
                dve.wait_ge(ln1.rs, c + 1)
                dve.tensor_tensor(r2, r, r, ALU.mult).then_inc(r1sq, 1)
                dve.wait_ge(r1sq, c + 1)
                dve.tensor_tensor(r2, r2, dbank(ln1.var_bank(c)), ALU.mult).then_inc(v2, 1)
                for k in range(KT):
                    dve.tensor_tensor(tok(res, k, c), tok(dev1, k, c), r, ALU.mult).then_inc(xl_ready, 1)
            with dve.Fori(0, NCH) as c:
                r2 = rstd2[:, bass.ds(c * CH, CH)]
                dve.wait_ge(sd2, c + 1)
                dve.reciprocal(r2, r2).then_inc(rs2, 1)
                dve.wait_ge(rs2, c + 1)
                dve.wait_ge(xl_ready, 2 * c + 2)
                for k in range(KT):
                    dve.scalar_tensor_tensor(tok(nrm, k, c), tok(res, k, c), v_("g_attn", k), r2,
                                             ALU.mult, ALU.mult).then_inc(ln1.scaled, 1)
            dve.wait_ge(consts, 1)
            with dve.Fori(0, NCH) as c:
                for m in range(4):
                    hi, lo = (q_hi, q_lo) if m < 2 else (k_hi, k_lo)
                    dve.wait_ge(qk_hi, 4 * c + m + 1)
                    dve.scalar_tensor_tensor(tok(lo, m % 2, c).bitcast(F32R), bank(m), v_("bqk", m),
                                             tok(hi, m % 2, c), ALU.add, ALU.subtract).then_inc(qk_free, 1)
            dve.wait_ge(w_in3, 32)
            for u in range(8):
                dve.wait_ge(v_ps, u + 1)
                for t in range(2):
                    b, tt = u // 4, 2 * (u % 4) + t
                    dve.tensor_tensor(values[:, b::2, tt, :],
                                      psum[:, 4 + u % 4, t * D:(t + 1) * D].rearrange("p (k f) -> p k f", k=KT),
                                      vbias[:].rearrange("p (k f) -> p k f", k=KT), ALU.add).then_inc(v_done, 1)

            def attention(A):
                dve.sem_inc(A.s1_free, 2)
                dve.sem_inc(A.neg, 1)

                def maxima(it, qd):
                    n = 2 * it + qd
                    for u, (h, b, i, k0, nk, diag) in enumerate(A.units):
                        dve.wait_ge(A.s1_ps, n * A.nunits + u + 1)
                        if A.causal:
                            at = (8 * h + i) * 2 + k0 // CH
                            dve.tensor_reduce(part_max[:, at:at + 1], psum[:, b, 0:nk], AX_X, ALU.max)\
                                .then_inc(A.s1_free, 1)
                        else:
                            at = 8 * h + i
                            dve.tensor_reduce(row_max[:, at:at + 4],
                                              psum[:, b, 0:4 * nk].rearrange("p (i k) -> p i k", i=4), AX_X, ALU.max)\
                                .then_inc(A.s1_free, 1)
                    if A.causal:
                        dve.wait_ge(A.s1_free, (n + 1) * A.nunits + 2)
                        dve.tensor_reduce(row_max[:], part_max[:].rearrange("p (r h) -> p r h", h=2), AX_X, ALU.max)\
                            .then_inc(A.mx, 1)
                    dve.wait_ge(A.mx_ps, n + 1 + 2)
                    dve.wait_ge(A.mrow, 64 * n + 64)
                    dve.tensor_scalar(neg_max[:], psum[0:32, 7, 0:P], -1.0, None, ALU.mult).then_inc(A.neg, 1)

                maxima(0, 0)

                def quad(it, qd, more):
                    if more:
                        maxima(it + (qd == 1), 1 - qd)

                over_iterations(dve, quad)

            def normalize(A, ready):
                for qd in range(QUADS):
                    dve.wait_ge(A.o_out[qd], 128 + 128 * ITS)
                with dve.Fori(0, NCH) as c:
                    num, den = A.out[:, :, bass.ds(c * CH, CH)], A.q_lo[:, :, bass.ds(c * CH, CH)]
                    dve.reciprocal(den, den).then_inc(A.part, 1)
                    dve.wait_ge(A.part, c + 1)
                    dve.tensor_tensor(num, num, den, ALU.mult).then_inc(ready, 1)

            attention(SA)
            normalize(SA, attn_ready)
            with dve.Fori(0, NCH) as c:
                for m in range(KT):
                    dve.wait_ge(ctx_ready, 2 * c + m + 1)
                    dve.tensor_tensor(tok(res, m, c), tok(attn_o, m, c), tok(res, m, c), ALU.add).then_inc(res1, 1)
            center(ln2)
            scale(ln2)
            dve.wait_ge(scan_init, 1)
            with dve.Fori(0, NITER) as s:
                for u in range(2 * NCH):
                    at = slice((u // 2) * CH, (u // 2 + 1) * CH)
                    dve.wait_ge(u_ready, 8 * s + u + 1)
                    dve.wait_ge(y_ready, 8 * s + u + 1)
                    dve.scalar_tensor_tensor(act_u[:, u % 2, at], nrm[:, u % 2, at], -DT * DT, act_u[:, u % 2, at],
                                             ALU.mult, ALU.add).then_inc(a_ready, 1)
                    dve.wait_ge(a_ready, 8 * s + u + 1)
                    dve.scalar_tensor_tensor(vel[:, u % 2, at], vel[:, u % 2, at], 1 - DT, act_u[:, u % 2, at],
                                             ALU.mult, ALU.add).then_inc(vel_ready, 1)
            with dve.Fori(0, NCH) as c:
                for m in range(KT):
                    dve.wait_ge(y_ready, 2 * NCH * NITER + 2 * c + m + 1)
                    dve.scalar_tensor_tensor(tok(res, m, c), tok(nrm, m, c), DT * DT, tok(res, m, c),
                                             ALU.mult, ALU.add).then_inc(res2, 1)
            center(ln3)
            scale(ln3)
            dve.sem_inc(x3, 4)
            with dve.Fori(0, NCH // 2) as cc:
                for half in range(2):
                    for m in range(KT):
                        c = 2 * cc + half
                        dve.wait_ge(ff2_ps, 2 * c + m + 1 + 4)
                        dve.scalar_tensor_tensor(tok(res, m, c), bank(4 + 2 * half + m), v_("ffb2", m),
                                                 tok(res, m, c), ALU.add, ALU.add).then_inc(x3, 1)
            center(ln4)
            scale(ln4)
            with dve.Fori(0, NCH) as c:
                for m in range(KT):
                    dve.wait_ge(xq_hi_s, 2 * c + m + 1)
                    dve.scalar_tensor_tensor(tok(xq_lo, m, c).bitcast(F32R), dbank(2 * c + m), v_("xbq", m),
                                             tok(xq_hi, m, c), ALU.add, ALU.subtract).then_inc(xq_free, 1)
            dve.sem_inc(xq_free, 4)
            for m in range(KT):
                dve.wait_ge(xk_hi_s, m + 1)
                dve.scalar_tensor_tensor(xk_lo[:, m, :].bitcast(F32R), bank(m, BATCH * CTXP), v_("xbk", m),
                                         xk_hi[:, m, :], ALU.add, ALU.subtract).then_inc(xk_free, 1)
            for b in range(BATCH):
                dve.wait_ge(xv_ps, b + 1)
                dve.tensor_tensor(xvals[0:CTX, b::2, :], bank(2 + b, D)[0:CTX].rearrange("p (k f) -> p k f", k=KT),
                                  xvbias[0:CTX, :].rearrange("p (k f) -> p k f", k=KT), ALU.add).then_inc(xv_done, 1)
            attention(XA)
            normalize(XA, xattn_ready)
            with dve.Fori(0, NCH) as c:
                for m in range(KT):
                    dve.wait_ge(xo_ps, 2 * c + m + 1)
                    dve.scalar_tensor_tensor(tok(res, m, c), dbank(2 * c + m), v_("xbo", m), tok(res, m, c),
                                             ALU.add, ALU.add).then_inc(res5, 1)
            center(ln5)
            scale(ln5)
            dve.sem_inc(dec_ready, 2)
            dve.sem_inc(msk_ready, 4)
            dve.sem_inc(tree_out, 2)
            with dve.Fori(0, NCH) as c:
                for st in range(TREES + 1):
                    if st < TREES:
                        g = c * TREES + st
                        dve.wait_ge(lg_ps, 2 * g + 1)
                        dve.wait_ge(cnt_ps, 2 * g + 2)
                        dve.tensor_scalar(decide[0:INNER, st % 2, :], bank(2 * (st % 2))[0:INNER],
                                          v_("tin", st, INNER), 0.0, ALU.add, ALU.is_gt).then_inc(dec_ready, 1)
                    if st >= 1:
                        t = st - 1
                        g = c * TREES + t
                        dve.wait_ge(msk_used, g + 1)
                        for half, rows in enumerate((INNER, LEAVES)):
                            dve.wait_ge(cnt_ps, 2 * g + half + 1 + 4)
                            dve.wait_ge(silu_ready, 2 * g + half + 1 + 4)
                            dve.scalar_tensor_tensor(masked[0:rows, t % 2, half, :], bank(4 + half)[0:rows],
                                                     v_("right", half, rows), silu[0:rows, t % 2, half, :],
                                                     ALU.is_equal, ALU.mult).then_inc(msk_ready, 1)
                dve.wait_ge(msk_used, TREES * (c + 1) + 2)
                for m in range(KT):
                    dve.tensor_tensor(tok(res, m, c), bank(6 + m), tok(res, m, c), ALU.add).then_inc(tree_out, 1)

        @block.tensor
        def _(pe):
            pe.wait_ge(c_in, 64)

            def mean(L):
                with pe.Fori(0, NCH) as c:
                    pe.wait_ge(L.ready, L.per * (c + 1))
                    for k in range(KT):
                        mm = pe.matmul(dbank(L.mean_bank(c)), mean_w[:], tok(L.src, k, c), start=k == 0, stop=k == 1)
                    mm.then_inc(L.mean, 1)

            def variance(L):
                with pe.Fori(0, NCH) as c:
                    pe.wait_ge(L.sq, c + 1)
                    for k in range(KT):
                        mm = pe.matmul(dbank(L.var_bank(c)), mean_w[:], tok(wide, k, c), start=k == 0, stop=k == 1)
                    mm.then_inc(L.var, 1)

            for c in range(NCH):
                pe.wait_ge(x_in[c], 16)
                for k in range(KT):
                    mm = pe.matmul(bank(c), mean_w[:], nrm[:, k, c * CH:(c + 1) * CH], start=k == 0, stop=k == 1)
                mm.then_inc(ln1.mean, 1)
            variance(ln1)
            pe.wait_ge(w_in3, 32)
            pe.wait_ge(ln1.d_ready, 2 * NCH)
            with pe.Fori(0, NCH) as c:
                pe.wait_ge(ln1.out, 2 * c + 2)
                for m in range(4):
                    pe.wait_ge(qk_free, 4 * c + m + 1)
                    for k in range(KT):
                        mm = pe.matmul(bank(m), w3[:, k, m * P:(m + 1) * P], tok(nrm, k, c), start=k == 0, stop=k == 1)
                    mm.then_inc(qk_ps, 1)
            for u in range(8):
                if u >= 4:
                    pe.wait_ge(v_done, 2 * (u - 3))
                for t in range(2):
                    for k in range(KT):
                        at = (2 * u + t) * P
                        mm = pe.matmul(psum[:, 4 + u % 4, t * D:(t + 1) * D], nrm[:, k, at:at + P],
                                       w3[:, k, 2 * D:3 * D], start=k == 0, stop=k == 1)
                mm.then_inc(v_ps, 1)

            def attention(A):
                pe.sem_inc(A.mx_ps, 2)
                pe.sem_inc(A.pv_ps, 4)

                def unit(it, qd, u):
                    n = 2 * it + qd
                    h, b, i, k0, nk, diag = A.units[u]
                    rows = slice(32 * h, 32 * h + HD)
                    pe.wait_ge(A.s1_free, n * A.nunits + u + 1)
                    if A.causal:
                        mm = pe.matmul(psum[:, b, 0:nk], A.q1[rows, qd, i * P:(i + 1) * P],
                                       A.k1[rows, qd, k0:k0 + nk], start=True, stop=not diag)
                        if diag:
                            mm = pe.matmul(psum[:, b, nk - P:nk], ident_b[:], causal_b[:], start=False, stop=True)
                    else:
                        for ii in range(4):
                            mm = pe.matmul(psum[:, b, ii * nk:(ii + 1) * nk],
                                           A.q1[rows, qd, (i + ii) * P:(i + ii + 1) * P], A.k1[rows, qd, 0:nk],
                                           start=True, stop=True)
                    mm.then_inc(A.s1_ps, 1)

                def first_pass_ready(it, qd):
                    pe.wait_ge(A.ld1[qd], 128 * (it + 1))

                def turn(it, qd):
                    n = 2 * it + qd
                    if A.causal:
                        pe.wait_ge(A.mx, n + 1)
                    else:
                        pe.wait_ge(A.s1_free, (n + 1) * A.nunits + 2)
                    pe.wait_ge(A.neg, n + 1)
                    pe.transpose(psum[0:32, 7, 0:P], row_max[:], ident[:]).then_inc(A.mx_ps, 1)

                def scores(it, qd, s):
                    n = 2 * it + qd
                    c, kt, q0, diag, first, last = A.steps[s]
                    g = n * A.nsteps + s
                    for p in range(2):
                        pe.wait_ge(A.prob_ready, 2 * g + p + 1)
                        for j in range(2):
                            rows = slice(64 * j, 64 * j + 3 * HD + 1)
                            mm = pe.matmul(psum[0:A.keys, 2 * p + j, q0:CH],
                                           A.k2[rows, qd, p, kt * P:kt * P + A.keys],
                                           A.q2[rows, qd, p, c * CH + q0:(c + 1) * CH], start=True, stop=True)
                        mm.then_inc(A.st_ps, 1)

                def weigh(it, qd, s):
                    n = 2 * it + qd
                    c, kt, q0, diag, first, last = A.steps[s]
                    g = n * A.nsteps + s
                    if first:
                        pe.wait_ge(A.o_done, 2 * n + c + 1)
                    if diag:
                        k = sum(st[3] for st in A.steps[:s + 1])
                        pe.wait_ge(A.prob_masked, 2 * (n * A.ndiag + k))
                    pe.wait_ge(A.prob_ready, 2 * g + 2 + 2)
                    for h in range(4):
                        mm = pe.matmul(psum[32 * h:32 * h + 32, 4, q0:CH], A.vq[0:A.keys, qd, kt, h, :],
                                       A.prob[0:A.keys, s % 2, h // 2, h % 2, q0:CH], start=first, stop=last)
                    if last:
                        mm.then_inc(A.pv_ps, 1)

                first_pass_ready(0, 0)
                for u in range(A.nunits):
                    unit(0, 0, u)
                turn(0, 0)

                def quad(it, qd, more):
                    n = 2 * it + qd
                    nxt = (it + (qd == 1), 1 - qd)
                    pe.wait_ge(A.ld2[qd], 384 * (it + 1))
                    pe.wait_ge(A.mrow, 64 * (n + 1) + 64)
                    pe.wait_ge(A.vq_ready, n + 1)
                    if more:
                        first_pass_ready(*nxt)
                    u = 0
                    for s in range(A.nsteps):
                        scores(it, qd, s)
                        if more:
                            for _ in range(A.sched[s]):
                                unit(*nxt, u)
                                u += 1
                            if s == A.turn:
                                turn(*nxt)
                        if s > 0:
                            weigh(it, qd, s - 1)
                    weigh(it, qd, A.nsteps - 1)

                over_iterations(pe, quad)

            pe.wait_ge(qk_free, 4 + 4 * NCH)
            pe.wait_ge(v_done, 16)
            pe.wait_ge(consts, 1)
            attention(SA)

            def project(w, at, src, ready, per, done):
                with pe.Fori(0, NCH) as c:
                    pe.wait_ge(ready, per * (c + 1))
                    for m in range(KT):
                        for k in range(KT):
                            mm = pe.matmul(dbank(2 * c + m), w[:, k, at + m * P:at + (m + 1) * P], tok(src, k, c),
                                           start=k == 0, stop=k == 1)
                        mm.then_inc(done, 1)

            pe.wait_ge(w_out3, 48)
            project(w3, 0, nrm, attn_ready, 1, op_ps)
            pe.wait_ge(ctx_ready, 2 * NCH)
            mean(ln2)
            variance(ln2)
            pe.wait_ge(wx01_ready, 1)
            for c in range(NCH):
                at = slice(c * CH, (c + 1) * CH)
                pe.wait_ge(y_ready, 2 * c + 2)
                for m in range(KT):
                    mo = slice(m * P, (m + 1) * P)
                    for k in range(KT):
                        pe.matmul(bank(2 * c + m), w3[:, k, D + m * P:D + (m + 1) * P], attn_o[:, k, at],
                                  start=k == 0, stop=False, skip_group_check=True)
                    for k in range(KT):
                        mm = pe.matmul(bank(2 * c + m), wx01[:, k, mo], nrm[:, k, at], start=False, stop=k == 1,
                                       skip_group_check=True)
                    mm.then_inc(z_ps, 1)
            with pe.Fori(0, NITER - 1) as s:
                for c in range(NCH):
                    at = slice(c * CH, (c + 1) * CH)
                    pe.wait_ge(vel_ready, 8 * s + 2 * c + 2)
                    for m in range(KT):
                        for k in range(KT):
                            mm = pe.matmul(bank(2 * c + m), wx01[:, k, m * P:(m + 1) * P], vel[:, k, at],
                                           start=False, stop=k == 1, skip_group_check=True)
                        mm.then_inc(z_ps, 1)
            pe.wait_ge(u_ready, 2 * NCH * NITER)
            mean(ln3)
            variance(ln3)
            pe.sem_inc(ff2_ps, 4)
            pe.wait_ge(w_late, 16 * 9)
            pe.wait_ge(ln3.out, 2 * NCH)
            with pe.Fori(0, NCH // 2) as cc:
                for half in range(2):
                    c = 2 * cc + half
                    for m in range(FT):
                        if m >= 4:
                            pe.wait_ge(gelu, FT * c + m - 3)
                        for k in range(KT):
                            mm = pe.matmul(bank(m % 4), wff1[:, k, m * P:(m + 1) * P], tok(nrm, k, c),
                                           start=k == 0, stop=k == 1)
                        mm.then_inc(ff1_ps, 1)
                    pe.wait_ge(gelu, FT * (c + 1))
                    for m in range(KT):
                        pe.wait_ge(x3, 2 * c + m + 1)
                        for k in range(FT):
                            mm = pe.matmul(bank(4 + 2 * half + m), wff2[:, k, m * P:(m + 1) * P], hid[:, half, k, :],
                                           start=k == 0, stop=k == FT - 1)
                        mm.then_inc(ff2_ps, 1)
            mean(ln4)
            pe.wait_ge(res4, 2 * NCH)
            variance(ln4)
            pe.wait_ge(ln4.out, 2 * NCH)
            project(wx4, 0, nrm, ln4.out, 2, xq_ps)
            pe.wait_ge(xq_free, 4 + 2 * NCH)
            for m in range(KT):
                for k in range(KT):
                    mm = pe.matmul(bank(m, BATCH * CTXP), wx4[:, k, D + m * P:D + (m + 1) * P], ctx_t[:, k, :],
                                   start=k == 0, stop=k == 1)
                mm.then_inc(xk_ps, 1)
            for b in range(BATCH):
                for k in range(KT):
                    mm = pe.matmul(bank(2 + b, D)[0:CTX], ctx_t[:, k, b * CTXP:b * CTXP + CTX], wx4[:, k, 2 * D:3 * D],
                                   start=k == 0, stop=k == 1)
                mm.then_inc(xv_ps, 1)
            pe.wait_ge(xk_free, 2)
            pe.wait_ge(xv_done, 2)
            attention(XA)
            project(wx4, 3 * D, wide, xattn_ready, 1, xo_ps)
            mean(ln5)
            variance(ln5)
            pe.wait_ge(consts, 2)
            pe.wait_ge(ln5.out, 2 * NCH)
            pe.sem_inc(cnt_ps, 4)
            pe.sem_inc(msk_used, 2)
            with pe.Fori(0, NCH) as c:
                for st in range(TREES + 2):
                    if st < TREES:
                        g = c * TREES + st
                        for half, (at, rows) in enumerate(((0, INNER), (INNER, LEAVES))):
                            if half == 0:
                                pe.wait_ge(dec_ready, g + 1)
                            pe.wait_ge(silu_ready, 2 * g + half + 1)
                            for k in range(KT):
                                o = st * NODES + at
                                mm = pe.matmul(bank(2 * (st % 2) + half)[0:rows], win[:, k, o:o + rows],
                                               tok(nrm, k, c), start=k == 0, stop=k == 1)
                            mm.then_inc(lg_ps, 1)
                    if 1 <= st <= TREES:
                        g = c * TREES + st - 1
                        pe.wait_ge(dec_ready, g + 1 + 2)
                        for half, (at, rows) in enumerate(((0, INNER), (INNER, LEAVES))):
                            pe.wait_ge(msk_ready, 2 * g + half + 1 + 2)
                            pe.matmul(bank(4 + half)[0:rows], sel[0:INNER, at:at + rows],
                                      decide[0:INNER, (st - 1) % 2, :], start=True, stop=True).then_inc(cnt_ps, 1)
                    if st >= 2:
                        t = st - 2
                        g = c * TREES + t
                        if t == 0:
                            pe.wait_ge(tree_out, 2 * c + 2)
                        pe.wait_ge(msk_ready, 2 * g + 2 + 4)
                        for m in range(KT):
                            mo = slice(m * P, (m + 1) * P)
                            pe.matmul(bank(6 + m), wout_in[0:INNER, t, mo], masked[0:INNER, t % 2, 0, :],
                                      start=t == 0, stop=False)
                            mm = pe.matmul(bank(6 + m), wout_leaf[:, t, mo], masked[:, t % 2, 1, :],
                                           start=False, stop=t == TREES - 1)
                        mm.then_inc(msk_used, 1)


INS = ["xT", "vec", "ident", "causal", "mean_w", "wqkv", "vbias", "wo", "wctx", "wx", "wff1", "wff2", "wx4", "win",
       "wout_in", "wout_leaf", "sel", "ctxT", "xvbias"]


def kernel(**inp):
    import numpy as np
    import concourse.bacc as bacc
    from concourse.bass_utils import run_bass_kernel_spmd

    f = {k: np.asarray(v) for k, v in inp.items()}

    def tiles(w):
        return w.reshape(-1, P, w.shape[1]).transpose(1, 0, 2)

    def cols(v):
        return v.reshape(-1, P).T

    A, X, T = "L0_attn_", "L0_xattn_", "L0_ffn_"
    bin2 = f[T + "b_in"].reshape(TREES, NODES)
    tin = np.zeros((P, TREES), np.float32)
    tin[:INNER] = bin2[:, :INNER].T
    turn = np.zeros((INNER, NODES), np.float32)
    for node in range(NODES):
        child = node
        while child:
            turn[(child - 1) // 2, node] = 1.0 if child % 2 == 0 else -1.0
            child = (child - 1) // 2
    rights = (turn > 0).sum(0).astype(np.float32)
    right = np.zeros((P, 2), np.float32)
    right[:INNER, 0] = rights[:INNER]
    right[:, 1] = rights[INNER:]
    qkv_b = f[A + "qkv_b"]
    vec = {"bqk": cols(qkv_b[:2 * D]), "bo": cols(f[A + "out_b"]), "binl": cols(f[A + "b_inl"]),
           "ffb1": cols(f[A + "ff_b1"]), "ffb2": cols(f[A + "ff_b2"]), "xbq": cols(f[X + "bq"]),
           "xbk": cols(f[X + "bk"]), "xbo": cols(f[X + "bo"]), "tin": tin, "tleaf": bin2[:, INNER:].T,
           "right": right, "eps": np.full((P, 1), EPS, np.float32)}
    for n in ("g_attn", "b_attn", "g1", "b1", "g2", "b2"):
        vec[n] = cols(f[A + n])
    wout = f[T + "W_out"].T.reshape(TREES, NODES, D).transpose(1, 0, 2)
    context = np.concatenate([f["ctx_1024"], f["ctx_1024"][:, -1:]], 1).reshape(BATCH * CTXP, D)
    q, k = np.arange(P)[:, None], np.arange(P)[None]
    arrays = {
        "xT": tiles(f["x"].reshape(TOK, D).T),
        "vec": np.concatenate([vec[n] for n in VEC], 1),
        "ident": np.eye(P, dtype=np.float32),
        "causal": np.where(k <= q, 0.0, LOW).astype(np.float32),
        "mean_w": np.full((P, P), 1.0 / D, np.float32),
        "wqkv": tiles(f[A + "qkv_w"]),
        "vbias": np.tile(qkv_b[None, 2 * D:], (P, 1)),
        "wo": tiles(f[A + "out_w"]), "wctx": tiles(f[A + "w_ctx"]), "wx": tiles(f[A + "w_x"]),
        "wff1": tiles(f[A + "ff_w1"]), "wff2": tiles(f[A + "ff_w2"]),
        "wx4": np.concatenate([tiles(f[X + n].T) for n in ("Wq", "Wk", "Wv", "Wo")], 2),
        "win": tiles(f[T + "W_in"].T),
        "wout_in": wout[:INNER], "wout_leaf": wout[INNER:],
        "sel": turn, "ctxT": tiles(context.T), "xvbias": np.tile(f[X + "bv"][None], (P, 1)),
    }
    nc = bacc.Bacc("TRN2", target_bir_lowering=False, num_devices=1)
    aps, feed = {}, {}
    for n in INS:
        arr = np.ascontiguousarray(arrays[n])
        feed[f"in_{n}"] = arr
        aps[n] = nc.dram_tensor(f"in_{n}", arr.shape, mybir.dt.from_np(arr.dtype), kind="ExternalInput").ap()
    out = nc.dram_tensor("out_t", (P, KT, TOK), F32, kind="ExternalOutput").ap()
    layer(nc, aps, out)
    r = run_bass_kernel_spmd(nc, [feed], core_ids=[0])
    return np.ascontiguousarray(r.results[0]["out_t"].transpose(2, 1, 0).reshape(BATCH, SEQ, D))
```

```python
from contextlib import ExitStack

import concourse.bass as bass
from concourse import mybir

F32 = mybir.dt.float32
F32R = mybir.dt.float32r
BF16 = mybir.dt.bfloat16
ALU = mybir.AluOpType
ACT = mybir.ActivationFunctionType
AX_X = mybir.AxisListType.X

P = 128
BATCH, SEQ, D = 2, 1024, 256
TOK = BATCH * SEQ
KT = D // P
CH = 512
NCH = TOK // CH
TPC = CH // P
HEADS, HD = 16, 16
CTX = 77
CTXP = 78
FF = 1024
FT = FF // P
NITER, DT = 8, 0.1
TREES, DEPTH = 8, 7
NODES = 2 ** (DEPTH + 1) - 1
INNER = 2 ** DEPTH - 1
LEAVES = NODES - INNER
EPS = 1e-5
SCALE = HD ** -0.5
R2 = 3 * HD
LOW = -1e30

VEC = {}
for _name, _n in [("bqk", 4), ("g_attn", 2), ("b_attn", 2), ("bo", 2), ("g1", 2), ("b1", 2), ("binl", 2),
                  ("g2", 2), ("b2", 2), ("ffb1", FT), ("ffb2", 2), ("xbq", 2), ("xbk", 2), ("xbo", 2),
                  ("tin", TREES), ("tleaf", TREES), ("right", 2), ("eps", 1)]:
    VEC[_name] = (sum(n for _, n in VEC.values()), _n)
NVEC = sum(n for _, n in VEC.values())

HT = P // HD
QUADS = HT // 4
ITS = KT * BATCH


def layer(nc, a, out_t):
    q3, xq3 = [nc.dram_tensor(n, (HT, 3, HD, KT * TOK), F32).ap() for n in ("q3", "xq3")]
    k3 = nc.dram_tensor("k3", (HT, 3, HD, KT * TOK), F32).ap()
    xk3 = nc.dram_tensor("xk3", (HT, 3, HD, KT * BATCH * CTXP), F32).ap()
    o3, xo3 = [nc.dram_tensor(n, (ITS, HT, 2, HD, SEQ), F32).ap() for n in ("o3", "xo3")]
    r3, xr3 = [nc.dram_tensor(n, (ITS, HT, SEQ), F32).ap() for n in ("r3", "xr3")]

    ctx = ExitStack()
    with ctx:
        def sb(name, shape, dt=F32, stack=ctx):
            return stack.enter_context(nc.sbuf_tensor(name, shape, dt))

        def sem(name):
            return ctx.enter_context(nc.semaphore(name))

        psum = ctx.enter_context(nc.psum_tensor("psum", [P, 8, CH], F32))
        pflat = psum[:].rearrange("p b n -> p (b n)")

        def bank(i, n=CH):
            return psum[:, i, 0:n]

        def dbank(i):
            return pflat[:, bass.ds(i * CH, CH)]

        def tok(t, k, c):
            return t[:, k, bass.ds(c * CH, CH)]

        vec = sb("vec", [P, NVEC])
        mean_w = sb("mean_w", [P, P])
        ident = sb("ident", [P, P])
        ident_b = sb("ident_b", [P, P], BF16)
        caus_f = sb("caus_f", [P, P])
        causal_b = sb("causal_b", [P, P], BF16)
        vbias = sb("vbias", [P, D])
        res = sb("res", [P, KT, TOK])
        nrm = sb("nrm", [P, KT, TOK])
        stage = sb("stage", [P, QUADS, SEQ])
        sd = sb("sd", [P, 2, 2, TPC])
        rs = sb("rs", [P, 2, 2, TPC])
        wide = sb("wide", [P, KT, TOK])
        w3 = sb("w3", [P, KT, 3 * D])
        part_max = sb("part_max", [P, 64])
        row_max = sb("row_max", [P, 32])
        neg_max = sb("neg_max", [32, P], F32R)

        def v_(name, i=0, rows=P):
            at = VEC[name][0] + i
            return vec[0:rows, at:at + 1]

        values = wide[:].rearrange("p k t -> p (k t)").rearrange("p (i t f) -> p i t f", i=ITS, f=P)
        square = wide[:, :, 0:2 * CH]

        s_first = ExitStack()
        dev1 = sb("dev1", [P, KT, TOK], F32, s_first)
        s_first.close()

        s_self = ExitStack()
        s_part = ExitStack()
        part_hi = sb("part_hi", [P, 2, 4, CH], F32, s_part)
        part_lo = sb("part_lo", [P, 2, 4, CH], F32, s_part)
        s_part.close()
        den = sb("den", [P, KT, TOK], F32, s_self)
        prob = sb("prob", [P, 2, 2, 2, CH], F32, s_self)
        q2 = sb("q2", [P, 2, 2, SEQ], F32R, s_self)
        q1 = sb("q1", [P, 2, SEQ], F32R, s_self)
        k1 = sb("k1", [P, 2, 4, SEQ], F32R, s_self)
        k2 = sb("k2", [P, 2, 2, 2, SEQ], F32R, s_self)
        vq = sb("vq", [P, 2, SEQ // P, 4, 32], F32, s_self)
        sums = sb("sums", [P, SEQ // HD], F32, s_self)
        recip = sb("recip", [P, SEQ // HD], F32, s_self)
        s_self.close()

        dev = sb("dev", [P, KT, TOK])
        wx4 = sb("wx4", [P, KT, 4 * D])
        win = sb("win", [P, KT, TREES * NODES])
        wout_in = sb("wout_in", [P, TREES, D])
        wout_leaf = sb("wout_leaf", [P, TREES, D])
        ctx_t = sb("ctx_t", [P, KT, BATCH * CTXP])
        sel_f = sb("sel_f", [P, NODES])
        sel = sb("sel", [P, NODES], BF16)
        xvbias = sb("xvbias", [P, D])
        s_mlp = ExitStack()
        wff1 = sb("wff1", [P, KT, FF], F32, s_mlp)
        wff2 = sb("wff2", [P, FT, D], F32, s_mlp)
        s_scan = ExitStack()
        attn_o = sb("attn_o", [P, KT, TOK], F32, s_scan)
        vel = sb("vel", [P, KT, TOK], F32, s_scan)
        act_u = sb("act_u", [P, KT, TOK], F32, s_scan)
        wx01 = sb("wx01", [P, KT, D], F32, s_scan)
        s_scan.close()
        hid = sb("hid", [P, 2, FT, CH], F32, s_mlp)
        x0 = sb("x0", [P, KT, TOK], F32, s_mlp)
        s_mlp.close()
        s_cross = ExitStack()
        xq2 = sb("xq2", [P, 2, 2, SEQ], F32R, s_cross)
        xq1 = sb("xq1", [P, 2, SEQ], F32R, s_cross)
        xk1 = sb("xk1", [P, QUADS, 4, ITS * CTXP], F32R, s_cross)
        xk2_all = sb("xk2_all", [P, QUADS, 2, 2, ITS * CTXP], F32R, s_cross)
        xk2 = sb("xk2", [P, 2, 2, 2, CTXP], F32R, s_cross)
        xvq = sb("xvq", [P, 2, 1, 4, 32], F32, s_cross)
        xvals = sb("xvals", [P, ITS, P], F32, s_cross)
        xsums = sb("xsums", [P, SEQ // HD], F32, s_cross)
        xrecip = sb("xrecip", [P, SEQ // HD], F32, s_cross)
        s_xpart = ExitStack()
        xk_hi = sb("xk_hi", [P, KT, BATCH * CTXP], F32, s_xpart)
        xk_lo = sb("xk_lo", [P, KT, BATCH * CTXP], F32, s_xpart)
        xpart_hi = sb("xpart_hi", [P, 2, KT, CH], F32, s_xpart)
        xpart_lo = sb("xpart_lo", [P, 2, KT, CH], F32, s_xpart)
        s_xpart.close()
        xden = sb("xden", [P, KT, TOK], F32, s_cross)
        xprob = sb("xprob", [P, 2, 2, 2, CH], F32, s_cross)
        s_cross.close()
        s_tree = ExitStack()
        silu = sb("silu", [P, 2, 2, CH], F32, s_tree)
        masked = sb("masked", [P, 2, 2, CH], F32, s_tree)
        decide = sb("decide", [P, 2, CH], BF16, s_tree)
        s_tree.close()

        x_in = [sem(f"x_in{c}") for c in range(NCH)]
        c_in, w_in3, w_out3, w_late, x0_in, out_st = [
            sem(n) for n in ("c_in", "w_in3", "w_out3", "w_late", "x0_in", "out_st")]
        passed = sem("passed")
        zeros_set, ones_set = sem("zeros_set"), sem("ones_set")
        consts, wx01_ready, scan_init = sem("consts"), sem("wx01_ready"), sem("scan_init")

        class Norm:
            mean, d_ready, sq, var, sd, rs, bc = [
                sem(f"ln_{s}") for s in ("mean", "d_ready", "sq", "var", "sd", "rs", "bc")]

            def __init__(self, at, src, ready, per, d, mean_bank, var_bank, gain=None):
                self.src, self.ready, self.per, self.d = src, ready, per, d
                self.mean_bank, self.var_bank, self.gain = mean_bank, var_bank, gain
                self.at = at * NCH
                self.out = sem(f"ln{at + 1}_out")
                if gain or at == 0:
                    self.scaled = sem(f"ln{at + 1}_scaled")

        res1, res2, res4, res5 = sem("res1"), sem("res2"), sem("res4"), sem("res5")
        ln1 = Norm(0, nrm, None, 0, dev1, lambda c: c, lambda c: c + 4)
        ln2 = Norm(1, res, res1, 2, dev, lambda c: 2 * c, lambda c: 2 * c + 1, ("g1", "b1"))
        ln3 = Norm(2, res, res2, 2, dev, lambda c: c, lambda c: c + 4, ("g2", "b2"))
        ln4 = Norm(3, res, res4, 2, dev, lambda c: c, lambda c: c + 4)
        ln5 = Norm(4, res, res5, 2, dev, lambda c: 2 * c, lambda c: 2 * c + 1)
        sd2, rs2, bc2, r1sq, v2, xl_ready = [sem(n) for n in ("sd2", "rs2", "bc2", "r1sq", "v2", "xl_ready")]

        qk_ps, qk_hi, qk_free, v_ps, v_done = [sem(n) for n in ("qk_ps", "qk_hi", "qk_free", "v_ps", "v_done")]
        qk_st, xq_st = [[sem(f"{n}{half}") for half in range(2)] for n in ("qk_st", "xq_st")]
        xk_st, xk_in = sem("xk_st"), sem("xk_in")
        xq_ps, xq_hi_s, xq_free, xk_ps, xk_hi_s, xk_free, xv_ps, xv_done = [
            sem(n) for n in ("xq_ps", "xq_hi_s", "xq_free", "xk_ps", "xk_hi_s", "xk_free", "xv_ps", "xv_done")]
        attn_ready, op_ps, ctx_ready = sem("attn_ready"), sem("op_ps"), sem("ctx_ready")
        y_ready, z_ps, u_ready, a_ready, vel_ready = [
            sem(n) for n in ("y_ready", "z_ps", "u_ready", "a_ready", "vel_ready")]
        ff1_ps, gelu, ff2_ps, x3 = sem("ff1_ps"), sem("gelu"), sem("ff2_ps"), sem("x3")
        xattn_ready, xo_ps = sem("xattn_ready"), sem("xo_ps")
        lg_ps, silu_ready, dec_ready, cnt_ps, msk_ready, msk_used, tree_out = [
            sem(n) for n in ("lg_ps", "silu_ready", "dec_ready", "cnt_ps", "msk_ready", "msk_used", "tree_out")]

        class Attention:

            def __init__(self, name, steps, units, lead, causal, keys, width, scratch, bufs, recip_qd):
                self.steps, self.units, self.causal, self.keys, self.width = steps, units, causal, keys, width
                self.q3, self.o3, self.r3 = scratch
                (self.q1, self.k1, self.q2, self.k2, self.vq, self.prob, self.sums, self.recip, self.den,
                 self.out) = bufs
                self.recip_qd = recip_qd
                self.ld1, self.ld2, self.o_st, self.stage_free = [[sem(f"{name}_{s}{qd}") for qd in range(QUADS)]
                                                           for s in ("ld1", "ld2", "o_st", "stage_free")]
                (self.s1_ps, self.s1_free, self.mx, self.mx_ps, self.neg, self.mrow, self.st_ps,
                 self.prob_ready, self.prob_masked, self.vq_ready, self.pv_ps, self.o_done,
                 self.sums_in, self.rec, self.rec_st, self.den_in, self.num, self.num_last) = [sem(f"{name}_{s}") for s in (
                    "s1_ps", "s1_free", "mx", "mx_ps", "neg", "mrow", "st_ps", "prob_ready", "prob_masked",
                    "vq_ready", "pv_ps", "o_done","sums_in", "rec", "rec_st", "den_in", "num", "num_last")]
                self.ld1_n = 16 * 5 if causal else 16
                self.ld2_n = 16 * 3 if causal else 16
                self.nsteps = len(self.steps)
                self.nunits = len(self.units)
                self.ndiag = sum(st[3] for st in self.steps)
                self.nbanks = 3 if self.nunits % 3 == 0 else 2
                todo = [(1, u) for u in range(lead, self.nunits)] + [(2, u) for u in range(lead)]
                cols = [self.units[u][3] + 64 for _, u in todo]
                size = [CH - st[2] + 64 for st in self.steps]
                self.plan, at = [[] for _ in steps], 0
                for s in range(self.nsteps):
                    while at < len(todo) and (s == self.nsteps - 1 or
                                              sum(cols[:at]) * sum(size) < sum(cols) * sum(size[:s + 1])):
                        self.plan[s].append(todo[at])
                        at += 1
                self.lead = lead

            def share(self, s, quarter):
                n = len(self.plan[s])
                return self.plan[s][n * quarter // 4:n * (quarter + 1) // 4]

        self_steps = [(c, kt, max(0, (kt - TPC * c) * P), kt >= TPC * c, kt == 0, kt == TPC * (c + 1) - 1)
                      for c in range(SEQ // CH) for kt in range(TPC * (c + 1))]
        self_units = [(h, i, kh * CH, min(CH, (i + 1) * P - kh * CH), i // TPC == kh)
                      for h in range(4) for i in range(SEQ // P) for kh in range(i // TPC + 1)]
        cross_steps = [(c, 0, 0, False, True, True) for c in range(SEQ // CH)]
        cross_units = [(0, i, 0, 4 * CTXP, False) for i in range(SEQ // P)]
        SA = Attention("sa", self_steps, self_units, 8, True, P, SEQ, (q3, o3, r3),
                       (q1, k1, q2, k2, vq, prob, sums, recip, den, nrm), 0)
        XA = Attention("xa", cross_steps, cross_units, 8, False, CTX, CTXP, (xq3, xo3, xr3),
                       (xq1, xk1, xq2, xk2, xvq, xprob, xsums, xrecip, xden, wide), 1)

        def chunk_pairs(eng, body):
            with eng.Fori(0, NCH // 2) as cc:
                for half in range(2):
                    body(2 * cc + half, half)

        def flat(t):
            return t[:].rearrange("p k t -> p (k t)")

        def over_iterations(eng, body, peel_first=False):
            if peel_first:
                for qd in range(QUADS):
                    body(0, qd, 2)
            with eng.Fori(int(peel_first), ITS - 1) as it:
                for qd in range(QUADS):
                    body(it, qd, 2)
            for qd in range(QUADS):
                body(ITS - 1, qd, QUADS - 1 - qd)

        def after(it, qd, d):
            return it + (qd + d) // QUADS, (qd + d) % QUADS

        def store_parts(sp, out3, part_hi, part_lo, m_of, half, at, done, r_lo):
            for r in range(3):
                part = part_lo if r == r_lo else part_hi
                sp.dma_start(out3[:, r, :, at], part[:, half, m_of, :]).then_inc(done, 16)

        def pack(eng, A, it, qd):
            eng.wait_ge(A.o_done, 2 * (2 * it + qd) + 3)
            eng.sem_inc(passed, 1)
            eng.dma_start(A.o3[bass.ds(it, 1), 4 * qd:4 * qd + 4].rearrange("o h s d n -> (o h s d) n"),
                          stage[:, qd, :]).then_inc(A.o_st[qd], 16)
            eng.wait_ge(A.o_st[qd], 16 * it + 16)
            eng.sem_inc(A.stage_free[qd], 1)
            eng.dma_start(flat(A.out)[64 * qd:64 * qd + 64, bass.ds(it * SEQ, SEQ)],
                          A.o3[bass.ds(it, 1), 4 * qd:4 * qd + 4, 0].rearrange("o h d n -> (o h) d n"))\
                .then_inc(A.num_last if isinstance(it, int) and it == ITS - 1 else A.num, 16)
            if qd == QUADS - 1:
                eng.wait_ge(A.rec, it + 1)
                eng.sem_inc(passed, 1)
                eng.dma_start(A.sums[:], A.o3[bass.ds(it, 1), :, 1, 0].rearrange("o h (s n) -> (o h) s n", s=HD))\
                    .then_inc(A.sums_in, 16)

        def spread(eng, A, it):
            eng.wait_ge(A.rec, it + 2)
            eng.sem_inc(passed, 1)
            eng.dma_start(A.r3[bass.ds(it, 1)].rearrange("o h (s n) -> (o h s) n", s=HD), A.recip[:])\
                .then_inc(A.rec_st, 16)
            eng.wait_ge(A.rec_st, 16 * it + 48)
            eng.sem_inc(passed, 1)
            eng.dma_start(flat(A.den)[:, bass.ds(it * SEQ, SEQ)],
                          A.r3[bass.ds(it, 1)].rearrange("o h (u n) -> (o h) u n", u=1).to_broadcast([HT, HD, SEQ]))\
                .then_inc(A.den_in, 16)

        block = ctx.enter_context(nc.Block())

        @block.sync
        def _(sp):
            for c in range(NCH):
                sp.dma_start(nrm[:, :, c * CH:(c + 1) * CH], a["xT"][:, :, c * CH:(c + 1) * CH]).then_inc(x_in[c], 16)
            sp.dma_start(w3[:], a["wqkv"]).then_inc(w_in3, 16)

            with sp.Fori(0, NCH // 2) as cc:
                for half in range(2):
                    c = 2 * cc + half
                    for m in range(4):
                        sp.wait_ge(qk_free, 4 * c + m + 1 + 4)
                        sp.sem_inc(passed, 1)
                        store_parts(sp, q3 if m < 2 else k3, part_hi, part_lo, m, half,
                                    bass.ds(c * CH + m % 2 * TOK, CH), qk_st[half], 2 if m < 2 else 1)

            def load_first(A, it, qd):
                sp.wait_ge(A.mx_ps, 2 * it + qd + 1)
                sp.sem_inc(passed, 1)
                sp.dma_start(A.q1[0:4 * HD, qd, :].bitcast(F32),
                             A.q3[4 * qd:4 * qd + 4, 0, :, bass.ds(it * SEQ, SEQ)].rearrange("h d t -> d h t"))\
                    .then_inc(A.ld1[qd], 16)
                if A.causal:
                    for h in range(4):
                        sp.dma_start(A.k1[h:4 * HD:4, qd, h, :].bitcast(F32),
                                     k3[4 * qd + h, 0, :, bass.ds(it * SEQ, SEQ)]).then_inc(A.ld1[qd], 16)

            def load_second(A, it, qd):
                sp.wait_ge(A.pv_ps, 2 * (2 * it + qd) + 2)
                sp.sem_inc(passed, 1)
                at = bass.ds(it * SEQ, SEQ)
                sp.dma_start(A.q2[0:2 * R2, qd, :, :].bitcast(F32),
                             A.q3[4 * qd:4 * qd + 4, :, :, at].rearrange("(p j) r d t -> (j r d) p t", p=2))\
                    .then_inc(A.ld2[qd], 16)
                if A.causal:
                    for j in range(2):
                        sp.dma_start(A.k2[R2 * j:R2 * j + R2, qd, :, j, :].bitcast(F32),
                                     k3[4 * qd + j:4 * qd + 4:2, :, :, at].rearrange("p r d t -> (r d) p t"))\
                            .then_inc(A.ld2[qd], 16)

            def load_max(A, it, qd):
                sp.wait_ge(A.neg, 2 * it + qd + 2)
                sp.sem_inc(passed, 1)
                sp.dma_start(A.q2[2 * R2:2 * R2 + 2, qd, :, :].bitcast(F32), neg_max[:].bitcast(F32))\
                    .then_inc(A.mrow, 16)

            def attention(A, packs, stored, per):
                sp.sem_inc(A.mrow, 16)
                for half in range(2):
                    sp.wait_ge(stored[half], 2 * per)
                load_first(A, 0, 0)
                load_second(A, 0, 0)
                load_first(A, 0, 1)
                load_max(A, 0, 0)
                for half in range(2):
                    sp.wait_ge(stored[half], (NCH // 2 + 1) * per)

                def quad(it, qd, more):
                    first = isinstance(it, int) and it == 0
                    if more == 2:
                        load_first(A, *after(it, qd, 2))
                    if more >= 1:
                        load_second(A, *after(it, qd, 1))
                    if packs and not (first and qd == 0):
                        pack(sp, A, *after(it, qd, -1))
                    if qd == 1 and not first:
                        spread(sp, A, it - 1)
                    if more >= 1:
                        load_max(A, *after(it, qd, 1))

                over_iterations(sp, quad, True)
                if packs:
                    pack(sp, A, ITS - 1, QUADS - 1)
                spread(sp, A, ITS - 1)

            sp.wait_ge(consts, 1)
            attention(SA, True, qk_st, 16 * 12)
            sp.wait_ge(attn_ready, NCH)
            for t, n in ((wff1, "wff1"), (wff2, "wff2"), (wx4, "wx4"), (win, "win"), (ctx_t, "ctxT"),
                         (wout_in[0:INNER], "wout_in"), (wout_leaf, "wout_leaf"), (sel_f[0:INNER], "sel"),
                         (xvbias, "xvbias")):
                sp.dma_start(t[:] if t in (wff1, wff2, wx4, win, ctx_t, wout_leaf, xvbias) else t, a[n])\
                    .then_inc(w_late, 16)
            sp.wait_ge(res2, 2 * NCH)
            sp.dma_start(x0[:], a["xT"]).then_inc(x0_in, 16)
            with sp.Fori(0, NCH // 2) as cc:
                for half in range(2):
                    c = 2 * cc + half
                    for m in range(KT):
                        sp.wait_ge(xq_free, 2 * c + m + 1)
                        sp.sem_inc(passed, 1)
                        store_parts(sp, xq3, xpart_hi, xpart_lo, m, half, bass.ds(c * CH + m * TOK, CH),
                                    xq_st[half], 2)
            sp.wait_ge(xk_free, KT)
            for m in range(KT):
                for r in range(3):
                    part = xk_lo if r == 1 else xk_hi
                    sp.dma_start(xk3[:, r, :, m * BATCH * CTXP:(m + 1) * BATCH * CTXP], part[:, m, :])\
                        .then_inc(xk_st, 16)
            sp.wait_ge(consts, 3)
            sp.wait_ge(xk_st, 16 * 3 * KT)
            for qd in range(QUADS):
                for h in range(4):
                    sp.dma_start(xk1[h:4 * HD:4, qd, h, :].bitcast(F32), xk3[4 * qd + h, 0]).then_inc(xk_in, 16)
                for j in range(2):
                    sp.dma_start(xk2_all[R2 * j:R2 * j + R2, qd, :, j, :].bitcast(F32),
                                 xk3[4 * qd + j:4 * qd + 4:2].rearrange("p r d t -> (r d) p t")).then_inc(xk_in, 16)
            attention(XA, False, xq_st, 16 * 6)
            with sp.Fori(0, NCH) as c:
                sp.wait_ge(tree_out, 2 * c + 2 + 2)
                sp.dma_start(out_t[:, :, bass.ds(c * CH, CH)], res[:, :, bass.ds(c * CH, CH)]).then_inc(out_st, 16)
            sp.wait_ge(out_st, 16 * NCH)

        @block.gpsimd
        def _(pool):
            def preset(q1, k1, q2, k2, vq, sums, nth):
                pool.memset(k1[:].bitcast(F32), 0.0)
                pool.memset(q1[:].bitcast(F32), 0.0)
                pool.memset(k2[:].bitcast(F32), 0.0)
                pool.memset(vq[:], 1.0)
                pool.memset(sums[:], 1.0).then_inc(zeros_set, 1)
                pool.wait_ge(zeros_set, nth)
                pool.memset(q2[2 * R2:P].bitcast(F32), 0.0)
                pool.memset(k2[2 * R2:2 * R2 + 2].bitcast(F32), 1.0).then_inc(ones_set, 1)
                pool.wait_ge(ones_set, 3 * nth - 2)
                for j in range(2):
                    row = k2[2 * R2:2 * R2 + 2, :, :, j, :].rearrange("r b p n -> r (b p) n")
                    pool.tensor_scalar(row, row.bitcast(F32), ident[2 * R2:2 * R2 + 2, 2 * R2 + j:2 * R2 + j + 1],
                                       None, ALU.mult).then_inc(ones_set, 1)
                pool.wait_ge(ones_set, 3 * nth)
                pool.sem_inc(consts, 1)

            pool.memset(part_max[:], -3e38)
            pool.wait_ge(c_in, 16 * 4)
            pool.tensor_copy(ident_b[:], ident[:])
            pool.tensor_copy(causal_b[:], caus_f[:])
            preset(q1, k1, q2, k2, vq, sums, 1)

            def attention(A, vals, ready):

                def copy_values(it, qd):
                    pool.wait_ge(A.pv_ps, 2 * (2 * it + qd) + 2)
                    if A.causal:
                        src = vals[:, bass.ds(it, 1), :, 64 * qd:64 * qd + 64]\
                            .rearrange("p o t (h d) -> p (o t) h d", h=4)
                    else:
                        src = vals[0:A.keys, bass.ds(it, 1), 64 * qd:64 * qd + 64]\
                            .rearrange("p o (h d) -> p o h d", h=4)
                    if not A.causal:
                        pool.tensor_copy(A.k2[:, qd], xk2_all[:, qd, :, :, bass.ds(it * CTXP, CTXP)].bitcast(F32))
                    pool.tensor_copy(A.vq[0:A.keys, qd, :, :, 0:HD], src).then_inc(A.vq_ready, 1)

                pool.wait_ge(*ready)
                copy_values(0, 0)

                def quad(it, qd, more):
                    n = 2 * it + qd
                    first = isinstance(it, int) and it == 0
                    if more >= 1:
                        copy_values(*after(it, qd, 1))
                    if not A.causal and not (first and qd == 0):
                        pack(pool, A, *after(it, qd, -1))
                    for s, (c, kt, q0, diag, first, last) in enumerate(A.steps):
                        if not diag:
                            continue
                        for p in range(2):
                            pool.wait_ge(A.prob_ready, 2 * (n * A.nsteps + s) + p + 3)
                            pool.sem_inc(passed, 1)
                            blk = A.prob[:, s % 2, p, :, q0:q0 + P]
                            pool.affine_select(out=blk, in_=blk, compare_op=ALU.is_ge, fill=0.0, base=0,
                                               pattern=[[0, 2], [1, P]], channel_multiplier=-1)\
                                .then_inc(A.prob_masked, 1)

                over_iterations(pool, quad, not A.causal)
                if not A.causal:
                    pack(pool, A, ITS - 1, QUADS - 1)

            attention(SA, values, (v_done, 16))
            pool.wait_ge(w_out3, 48)
            pool.wait_ge(attn_ready, NCH)
            pool.tensor_scalar(wx01[:], w3[:, :, 2 * D:3 * D], DT * DT, None, ALU.mult).then_inc(wx01_ready, 1)
            pool.memset(vel[:], 0.0).then_inc(scan_init, 1)
            for u in range(2 * NCH):
                at = slice((u // 2) * CH, (u // 2 + 1) * CH)
                pool.wait_ge(ln2.out, u + 1)
                pool.tensor_scalar(nrm[:, u % 2, at], nrm[:, u % 2, at], 1 / (DT * DT), None, ALU.mult)\
                    .then_inc(y_ready, 1)
            with pool.Fori(0, NITER) as s:
                for u in range(2 * NCH):
                    at = slice((u // 2) * CH, (u // 2 + 1) * CH)
                    pool.wait_ge(vel_ready, 8 * s + u + 1)
                    pool.tensor_tensor(nrm[:, u % 2, at], nrm[:, u % 2, at], vel[:, u % 2, at], ALU.add)\
                        .then_inc(y_ready, 1)
            pool.wait_ge(w_late, 16 * 9)
            pool.tensor_copy(sel[0:INNER], sel_f[0:INNER]).then_inc(consts, 1)
            pool.wait_ge(x0_in, 16)
            with pool.Fori(0, NCH) as c:
                for m in range(KT):
                    pool.wait_ge(x3, 2 * c + m + 1 + 4)
                    pool.tensor_tensor(tok(res, m, c), tok(res, m, c), tok(x0, m, c), ALU.add).then_inc(res4, 1)
            pool.wait_ge(ln4.out, 2 * NCH)
            preset(xq1, xk1, xq2, xk2_all, xvq, xsums, 2)
            pool.wait_ge(xk_in, 16 * 6 * QUADS)
            attention(XA, xvals, (xv_done, 2))

        @block.scalar
        def _(act):
            for t, n in ((vec[:], "vec"), (ident[:], "ident"), (caus_f[:], "causal"), (mean_w[:], "mean_w")):
                act.dma_start(t, a[n]).then_inc(c_in, 16)
            act.dma_start(vbias[:], a["vbias"]).then_inc(w_in3, 16)
            act.wait_ge(c_in, 64)

            def squares(L):
                def chunk(c, half):
                    act.wait_ge(L.d_ready, 2 * (L.at + c) + 2)
                    act.wait_ge(L.var, L.at + c + 1)
                    act.activation(square[:, :, half * CH:(half + 1) * CH], L.d[:, :, bass.ds(c * CH, CH)],
                                   ACT.Square).then_inc(L.sq, 1)
                chunk_pairs(act, chunk)

            def deviation(L):
                def chunk(c, half):
                    act.wait_ge(L.var, L.at + c + 3)
                    act.wait_ge(L.rs, L.at + c + 1)
                    act.activation(sd[:, half, 0, :], dbank(L.var_bank(c))[:, 0:TPC], ACT.Sqrt, bias=v_("eps"))\
                        .then_inc(L.sd, 1)
                chunk_pairs(act, chunk)

            def add_bias(L):
                with act.Fori(0, NCH) as c:
                    for k in range(KT):
                        act.wait_ge(L.scaled, 2 * c + k + 1)
                        act.activation(tok(nrm, k, c), tok(nrm, k, c), ACT.Identity, bias=v_(L.gain[1], k))\
                            .then_inc(L.out, 1)

            squares(ln1)

            def both_deviations(c, half):
                act.wait_ge(ln1.var, c + 3)
                act.wait_ge(ln1.rs, c + 1)
                act.activation(sd[:, half, 0, :], dbank(ln1.var_bank(c))[:, 0:TPC], ACT.Sqrt, bias=v_("eps"))\
                    .then_inc(ln1.sd, 1)
                act.wait_ge(v2, c + 1)
                act.activation(sd[:, half, 1, :], sd[:, half, 1, :], ACT.Sqrt, bias=v_("eps")).then_inc(sd2, 1)
            chunk_pairs(act, both_deviations)
            with act.Fori(0, NCH) as c:
                for k in range(KT):
                    act.wait_ge(ln1.scaled, 2 * c + k + 1)
                    act.activation(tok(nrm, k, c), tok(nrm, k, c), ACT.Identity, bias=v_("b_attn", k))\
                        .then_inc(ln1.out, 1)
            for half in range(2):
                act.sem_inc(qk_st[half], 16 * 12)
                act.sem_inc(xq_st[half], 16 * 6)
            with act.Fori(0, NCH // 2) as cc:
                for half in range(2):
                    act.wait_ge(qk_st[half], 16 * 12 * cc + 16 * 12)
                    for m in range(4):
                        act.wait_ge(qk_ps, 4 * (2 * cc + half) + m + 1)
                        act.activation(part_hi[:, half, m, :].bitcast(F32R), bank(m), ACT.Identity,
                                       bias=v_("bqk", m)).then_inc(qk_hi, 1)

            def attention(A):
                act.sem_inc(A.prob_ready, 2)
                act.sem_inc(A.o_done, 1)
                for qd in range(QUADS):
                    act.sem_inc(A.stage_free[qd], 1)

                def quad(it, qd, more):
                    n = 2 * it + qd
                    for s, (c, kt, q0, diag, first, last) in enumerate(A.steps):
                        g = n * A.nsteps + s
                        for p in range(2):
                            act.wait_ge(A.st_ps, 2 * g + p + 1)
                            act.activation(A.prob[0:A.keys, s % 2, p, :, q0:CH],
                                           psum[0:A.keys, 2 * p:2 * p + 2, q0:CH], ACT.Exp, scale=SCALE)\
                                .then_inc(A.prob_ready, 1)
                        if s > 0 and A.steps[s - 1][5]:
                            read_out(it, qd, A.steps[s - 1][0])
                    read_out(it, qd, A.steps[-1][0])

                def read_out(it, qd, c):
                    n = 2 * it + qd
                    act.wait_ge(A.pv_ps, 2 * n + c + 1 + 4)
                    act.wait_ge(A.stage_free[qd], it + 1)
                    act.activation(stage[:, qd, c * CH:(c + 1) * CH], bank(4), ACT.Copy).then_inc(A.o_done, 1)

                over_iterations(act, quad)

            attention(SA)
            act.wait_ge(v_ps, 8)
            for i, n in enumerate(("wo", "wctx", "wx")):
                act.dma_start(w3[:, :, i * D:(i + 1) * D], a[n]).then_inc(w_out3, 16)
            act.wait_ge(attn_ready, NCH)
            with act.Fori(0, NCH) as c:
                for m in range(KT):
                    act.wait_ge(op_ps, 2 * c + m + 1)
                    act.activation(tok(attn_o, m, c), dbank(2 * c + m), ACT.Identity, bias=v_("bo", m))\
                        .then_inc(ctx_ready, 1)
            squares(ln2)
            deviation(ln2)
            add_bias(ln2)
            with act.Fori(0, NITER) as s:
                for u in range(2 * NCH):
                    at = slice((u // 2) * CH, (u // 2 + 1) * CH)
                    act.wait_ge(z_ps, 8 * s + 2 * (u // 2) + 2)
                    act.activation(act_u[:, u % 2, at], bank(u), ACT.Tanh, bias=v_("binl", u % 2))\
                        .then_inc(u_ready, 1)
            squares(ln3)
            deviation(ln3)
            add_bias(ln3)
            with act.Fori(0, NCH // 2) as cc:
                for half in range(2):
                    for m in range(FT):
                        act.wait_ge(ff1_ps, FT * (2 * cc + half) + m + 1)
                        act.wait_ge(ff2_ps, 2 * (2 * cc + half) + 2)
                        act.activation(hid[:, half, m, :], bank(m % 4), ACT.Gelu, bias=v_("ffb1", m))\
                            .then_inc(gelu, 1)
            squares(ln4)
            deviation(ln4)
            with act.Fori(0, NCH // 2) as cc:
                for half in range(2):
                    c = 2 * cc + half
                    act.wait_ge(xq_st[half], 16 * 6 * cc + 16 * 6)
                    for m in range(KT):
                        act.wait_ge(xq_ps, 2 * c + m + 1)
                        act.activation(xpart_hi[:, half, m, :].bitcast(F32R), dbank(2 * c + m), ACT.Identity,
                                       bias=v_("xbq", m)).then_inc(xq_hi_s, 1)
            for m in range(KT):
                act.wait_ge(xk_ps, m + 1)
                act.activation(xk_hi[:, m, :].bitcast(F32R), bank(m, BATCH * CTXP), ACT.Identity,
                               bias=v_("xbk", m)).then_inc(xk_hi_s, 1)
            attention(XA)
            squares(ln5)
            deviation(ln5)
            act.sem_inc(silu_ready, 4)
            with act.Fori(0, NCH) as c:
                for t in range(TREES):
                    g = c * TREES + t
                    for half, (rows, bias) in enumerate(((INNER, "tin"), (LEAVES, "tleaf"))):
                        act.wait_ge(lg_ps, 2 * g + half + 1)
                        if half == 0:
                            act.wait_ge(dec_ready, g + 1 + 2)
                        act.wait_ge(msk_ready, 2 * g + half + 1)
                        act.activation(silu[0:rows, t % 2, half, :], bank(2 * (t % 2) + half)[0:rows], ACT.Silu,
                                       bias=v_(bias, t, rows)).then_inc(silu_ready, 1)

        @block.vector
        def _(dve):
            dve.sem_inc(qk_free, 4)
            dve.wait_ge(c_in, 64)

            def center(L):
                with dve.Fori(0, NCH) as c:
                    dve.wait_ge(L.mean, L.at + c + 1)
                    for k in range(KT):
                        dve.tensor_tensor(tok(L.d, k, c), tok(L.src, k, c), dbank(L.mean_bank(c)), ALU.subtract)\
                            .then_inc(L.d_ready, 1)

            def scale(L):
                def invert(c, half):
                    dve.wait_ge(L.sd, L.at + c + 1)
                    dve.wait_ge(L.bc, L.at + c + 1)
                    dve.reciprocal(rs[:, half, 0, :], sd[:, half, 0, :]).then_inc(L.rs, 1)
                chunk_pairs(dve, invert)
                with dve.Fori(0, NCH) as c:
                    dve.wait_ge(L.bc, L.at + c + 3)
                    r = dbank(L.var_bank(c))
                    for k in range(KT):
                        if L.gain:
                            dve.scalar_tensor_tensor(tok(nrm, k, c), tok(L.d, k, c), v_(L.gain[0], k), r,
                                                     ALU.mult, ALU.mult).then_inc(L.scaled, 1)
                        else:
                            dve.tensor_tensor(tok(nrm, k, c), tok(L.d, k, c), r, ALU.mult).then_inc(L.out, 1)

            center(ln1)
            dve.sem_inc(ln1.rs, 2)

            def invert_both(c, half):
                r, r2 = rs[:, half, 0, :], rs[:, half, 1, :]
                dve.wait_ge(ln1.sd, c + 1)
                dve.wait_ge(ln1.bc, c + 1)
                dve.reciprocal(r, sd[:, half, 0, :]).then_inc(xl_ready, 1)
                dve.wait_ge(xl_ready, c + 1)
                dve.tensor_tensor(r2, r, r, ALU.mult).then_inc(r1sq, 1)
                dve.wait_ge(r1sq, c + 1)
                dve.tensor_tensor(sd[:, half, 1, :], r2, dbank(ln1.var_bank(c))[:, 0:TPC], ALU.mult).then_inc(v2, 1)
                dve.wait_ge(sd2, c + 1)
                dve.reciprocal(r2, sd[:, half, 1, :]).then_inc(ln1.rs, 1)
            chunk_pairs(dve, invert_both)
            with dve.Fori(0, NCH) as c:
                dve.wait_ge(ln1.bc, c + 3)
                for k in range(KT):
                    dve.tensor_tensor(tok(res, k, c), tok(dev1, k, c), dbank(ln1.var_bank(c)), ALU.mult)\
                        .then_inc(rs2, 1)
                dve.wait_ge(rs2, 2 * c + 2)
                for k in range(KT):
                    dve.scalar_tensor_tensor(tok(nrm, k, c), tok(res, k, c), v_("g_attn", k), dbank(ln1.mean_bank(c)),
                                             ALU.mult, ALU.mult).then_inc(ln1.scaled, 1)
            with dve.Fori(0, NCH // 2) as cc:
                for half in range(2):
                    c = 2 * cc + half
                    dve.wait_ge(qk_st[half], 16 * 12 * cc + 16 * 12)
                    for m in range(4):
                        dve.wait_ge(qk_hi, 4 * c + m + 1)
                        dve.scalar_tensor_tensor(part_lo[:, half, m, :].bitcast(F32R), bank(m), v_("bqk", m),
                                                 part_hi[:, half, m, :], ALU.add, ALU.subtract).then_inc(qk_free, 1)
            dve.wait_ge(w_in3, 32)
            for u in range(8):
                dve.wait_ge(v_ps, u + 1)
                for t in range(2):
                    b, tt = u // 4, 2 * (u % 4) + t
                    dve.tensor_tensor(values[:, b::2, tt, :],
                                      psum[:, 4 + u % 4, t * D:(t + 1) * D].rearrange("p (k f) -> p k f", k=KT),
                                      vbias[:].rearrange("p (k f) -> p k f", k=KT), ALU.add).then_inc(v_done, 1)

            def attention(A, ready):
                dve.sem_inc(A.s1_free, A.nbanks)
                dve.sem_inc(A.neg, 1)

                dve.sem_inc(A.rec_st, 32)
                if A.causal:
                    dve.sem_inc(A.sums_in, 16)
                dve.wait_ge(consts, 1 if A.causal else 3)

                def maximum(it, qd, u):
                    n = 2 * it + qd
                    h, i, k0, nk, diag = A.units[u]
                    row = 16 * (h % 2) + 8 * (h // 2) + i
                    dve.wait_ge(A.s1_ps, n * A.nunits + u + 1)
                    if A.causal and u == 0 and not (isinstance(n, int) and n == 0):
                        dve.wait_ge(A.mx, n)
                    if A.causal:
                        at = 2 * row + k0 // CH
                        dve.tensor_reduce(part_max[:, at:at + 1], psum[:, 5 + u % A.nbanks, 0:nk], AX_X, ALU.max)\
                            .then_inc(A.s1_free, 1)
                    else:
                        dve.tensor_reduce(row_max[:].rearrange("q (j p i) -> q p j i", j=2, p=2)[:, :, :, i],
                                          psum[:, 5 + u % A.nbanks, 0:nk].rearrange("q (p j k) -> q p j k", p=2, j=2),
                                          AX_X, ALU.max).then_inc(A.s1_free, 1)

                def gather(it, qd):
                    n = 2 * it + qd
                    if A.causal:
                        dve.wait_ge(A.s1_free, (n + 1) * A.nunits + A.nbanks)
                        dve.wait_ge(A.mx_ps, n + 2)
                        dve.tensor_reduce(row_max[:], part_max[:].rearrange("p (r h) -> p r h", h=2), AX_X, ALU.max)\
                            .then_inc(A.mx, 1)

                def negate(it, qd):
                    n = 2 * it + qd
                    dve.wait_ge(A.mx_ps, n + 1 + 2)
                    dve.wait_ge(A.mrow, 16 * n + 16)
                    dve.tensor_scalar(neg_max[:], psum[0:32, 7, 0:P], -1.0, None, ALU.mult).then_inc(A.neg, 1)

                def invert(it):
                    if A.causal:
                        dve.wait_ge(A.sums_in, 16 * it + 16)
                    elif not (isinstance(it, int) and it == 0):
                        dve.wait_ge(A.sums_in, 16 * it)
                    dve.wait_ge(A.rec_st, 16 * it + 16)
                    dve.reciprocal(A.recip[:], A.sums[:]).then_inc(A.rec, 1)

                for u in range(A.nunits):
                    maximum(0, 0, u)
                gather(0, 0)
                negate(0, 0)
                for u in range(A.lead):
                    maximum(0, 1, u)
                if A.lead == A.nunits:
                    negate(0, 1)

                def quad(it, qd, more):
                    todo = [(d, u) for step in A.plan for d, u in step]
                    if more == 0 and qd == A.recip_qd:
                        invert(it)
                    for k, (d, u) in enumerate(todo):
                        if d <= more:
                            maximum(*after(it, qd, d), u)
                        if k == len(todo) // 2 and qd == A.recip_qd and more:
                            invert(it)
                        if (d, u) == (1, A.nunits - 1) and more:
                            gather(*after(it, qd, 1))
                        if (d, u) == (2, 1) and A.causal and more:
                            negate(*after(it, qd, 1))
                    if not A.causal and more == 2:
                        negate(*after(it, qd, 2))

                over_iterations(dve, quad, not A.causal)

                def normalize(its, chunks):
                    dve.wait_ge(A.num, 16 * QUADS * (ITS - 1))
                    if its == ITS:
                        dve.wait_ge(A.num_last, 16 * QUADS)
                    dve.wait_ge(A.den_in, 16 * its)
                    for c in chunks:
                        num, den = A.out[:, :, c * CH:(c + 1) * CH], A.den[:, :, c * CH:(c + 1) * CH]
                        dve.tensor_tensor(num, num, den, ALU.mult).then_inc(ready, 1)

                normalize(ITS - 1, range(NCH // BATCH))
                invert(ITS)
                normalize(ITS, range(NCH // BATCH, NCH))

            attention(SA, attn_ready)
            with dve.Fori(0, NCH) as c:
                for m in range(KT):
                    dve.wait_ge(ctx_ready, 2 * c + m + 1)
                    dve.tensor_tensor(tok(res, m, c), tok(attn_o, m, c), tok(res, m, c), ALU.add).then_inc(res1, 1)
            center(ln2)
            scale(ln2)
            dve.wait_ge(scan_init, 1)
            with dve.Fori(0, NITER) as s:
                for u in range(2 * NCH):
                    at = slice((u // 2) * CH, (u // 2 + 1) * CH)
                    dve.wait_ge(u_ready, 8 * s + u + 1)
                    dve.wait_ge(y_ready, 8 * s + u + 1)
                    dve.scalar_tensor_tensor(act_u[:, u % 2, at], nrm[:, u % 2, at], -DT * DT, act_u[:, u % 2, at],
                                             ALU.mult, ALU.add).then_inc(a_ready, 1)
                    dve.wait_ge(a_ready, 8 * s + u + 1)
                    dve.scalar_tensor_tensor(vel[:, u % 2, at], vel[:, u % 2, at], 1 - DT, act_u[:, u % 2, at],
                                             ALU.mult, ALU.add).then_inc(vel_ready, 1)
            with dve.Fori(0, NCH) as c:
                for m in range(KT):
                    dve.wait_ge(y_ready, 2 * NCH * NITER + 2 * c + m + 1)
                    dve.scalar_tensor_tensor(tok(res, m, c), tok(nrm, m, c), DT * DT, tok(res, m, c),
                                             ALU.mult, ALU.add).then_inc(res2, 1)
            center(ln3)
            scale(ln3)
            dve.sem_inc(x3, 4)
            with dve.Fori(0, NCH // 2) as cc:
                for half in range(2):
                    for m in range(KT):
                        c = 2 * cc + half
                        dve.wait_ge(ff2_ps, 2 * c + m + 1 + 4)
                        dve.scalar_tensor_tensor(tok(res, m, c), bank(4 + 2 * half + m), v_("ffb2", m),
                                                 tok(res, m, c), ALU.add, ALU.add).then_inc(x3, 1)
            center(ln4)
            scale(ln4)
            with dve.Fori(0, NCH // 2) as cc:
                for half in range(2):
                    c = 2 * cc + half
                    dve.wait_ge(xq_st[half], 16 * 6 * cc + 16 * 6)
                    for m in range(KT):
                        dve.wait_ge(xq_hi_s, 2 * c + m + 1)
                        dve.scalar_tensor_tensor(xpart_lo[:, half, m, :].bitcast(F32R), dbank(2 * c + m),
                                                 v_("xbq", m), xpart_hi[:, half, m, :], ALU.add, ALU.subtract)\
                            .then_inc(xq_free, 1)
            for m in range(KT):
                dve.wait_ge(xk_hi_s, m + 1)
                dve.scalar_tensor_tensor(xk_lo[:, m, :].bitcast(F32R), bank(m, BATCH * CTXP), v_("xbk", m),
                                         xk_hi[:, m, :], ALU.add, ALU.subtract).then_inc(xk_free, 1)
            for b in range(BATCH):
                dve.wait_ge(xv_ps, b + 1)
                dve.tensor_tensor(xvals[0:CTX, b::2, :], bank(2 + b, D)[0:CTX].rearrange("p (k f) -> p k f", k=KT),
                                  xvbias[0:CTX, :].rearrange("p (k f) -> p k f", k=KT), ALU.add).then_inc(xv_done, 1)
            attention(XA, xattn_ready)
            with dve.Fori(0, NCH) as c:
                for m in range(KT):
                    dve.wait_ge(xo_ps, 2 * c + m + 1)
                    dve.scalar_tensor_tensor(tok(res, m, c), dbank(2 * c + m), v_("xbo", m), tok(res, m, c),
                                             ALU.add, ALU.add).then_inc(res5, 1)
            center(ln5)
            scale(ln5)
            dve.sem_inc(dec_ready, 2)
            dve.sem_inc(msk_ready, 4)
            dve.sem_inc(tree_out, 2)
            with dve.Fori(0, NCH) as c:
                for st in range(TREES + 1):
                    if st < TREES:
                        g = c * TREES + st
                        dve.wait_ge(lg_ps, 2 * g + 1)
                        dve.wait_ge(cnt_ps, 2 * g + 2)
                        dve.tensor_scalar(decide[0:INNER, st % 2, :], bank(2 * (st % 2))[0:INNER],
                                          v_("tin", st, INNER), 0.0, ALU.add, ALU.is_gt).then_inc(dec_ready, 1)
                    if st >= 1:
                        t = st - 1
                        g = c * TREES + t
                        dve.wait_ge(msk_used, g + 1)
                        for half, rows in enumerate((INNER, LEAVES)):
                            dve.wait_ge(cnt_ps, 2 * g + half + 1 + 4)
                            dve.wait_ge(silu_ready, 2 * g + half + 1 + 4)
                            dve.scalar_tensor_tensor(masked[0:rows, t % 2, half, :], bank(4 + half)[0:rows],
                                                     v_("right", half, rows), silu[0:rows, t % 2, half, :],
                                                     ALU.is_equal, ALU.mult).then_inc(msk_ready, 1)
                dve.wait_ge(msk_used, TREES * (c + 1) + 2)
                for m in range(KT):
                    dve.tensor_tensor(tok(res, m, c), bank(6 + m), tok(res, m, c), ALU.add).then_inc(tree_out, 1)

        @block.tensor
        def _(pe):
            pe.wait_ge(c_in, 64)

            def mean(L):
                with pe.Fori(0, NCH) as c:
                    pe.wait_ge(L.ready, L.per * (c + 1))
                    for k in range(KT):
                        mm = pe.matmul(dbank(L.mean_bank(c)), mean_w[:], tok(L.src, k, c), start=k == 0, stop=k == 1)
                    mm.then_inc(L.mean, 1)

            def variance(L, n=1):
                def sums(c, half):
                    pe.wait_ge(L.sq, L.at + c + 1)
                    for t in range(TPC):
                        for k in range(KT):
                            at = half * CH + t * P
                            mm = pe.matmul(dbank(L.var_bank(c))[:, t:t + 1], square[:, k, at:at + P], mean_w[:, 0:1],
                                           start=k == 0, stop=k == 1)
                    mm.then_inc(L.var, 1)

                def spread_out(c, half):
                    pe.wait_ge(L.rs, L.at + c + 3)
                    for i in range(n):
                        bank_of = (L.var_bank, L.mean_bank)[i]
                        for t in range(TPC):
                            mm = pe.matmul(dbank(bank_of(c))[:, t * P:(t + 1) * P],
                                           rs[:, half, i, t:t + 1].to_broadcast([P, P]), ident[:],
                                           start=True, stop=True)
                    mm.then_inc(L.bc, 1)

                chunk_pairs(pe, sums)
                chunk_pairs(pe, spread_out)

            pe.sem_inc(ln1.var, 2)
            pe.sem_inc(ln1.bc, 2)
            for c in range(NCH):
                pe.wait_ge(x_in[c], 16)
                for k in range(KT):
                    mm = pe.matmul(bank(c), mean_w[:], nrm[:, k, c * CH:(c + 1) * CH], start=k == 0, stop=k == 1)
                mm.then_inc(ln1.mean, 1)
            variance(ln1, 2)
            pe.wait_ge(w_in3, 32)
            pe.wait_ge(ln1.scaled, 2 * NCH)
            with pe.Fori(0, NCH) as c:
                pe.wait_ge(ln1.out, 2 * c + 2)
                for m in range(4):
                    pe.wait_ge(qk_free, 4 * c + m + 1)
                    for k in range(KT):
                        mm = pe.matmul(bank(m), w3[:, k, m * P:(m + 1) * P], tok(nrm, k, c), start=k == 0, stop=k == 1)
                    mm.then_inc(qk_ps, 1)
            for u in range(8):
                if u >= 4:
                    pe.wait_ge(v_done, 2 * (u - 3))
                for t in range(2):
                    for k in range(KT):
                        at = (2 * u + t) * P
                        mm = pe.matmul(psum[:, 4 + u % 4, t * D:(t + 1) * D], nrm[:, k, at:at + P],
                                       w3[:, k, 2 * D:3 * D], start=k == 0, stop=k == 1)
                mm.then_inc(v_ps, 1)

            def attention(A):
                pe.sem_inc(A.mx_ps, 2)
                pe.sem_inc(A.pv_ps, 4)

                def unit(it, qd, u):
                    n = 2 * it + qd
                    h, i, k0, nk, diag = A.units[u]
                    if u == 0:
                        pe.wait_ge(A.ld1[qd], A.ld1_n * (it + 1))
                    pe.wait_ge(A.s1_free, n * A.nunits + u + 1)
                    if A.nbanks == 3 and u == 2:
                        pe.wait_ge(A.neg, n + 1)
                    if A.causal:
                        mm = pe.matmul(psum[:, 5 + u % A.nbanks, 0:nk], A.q1[:, qd, i * P:(i + 1) * P],
                                       A.k1[:, qd, h, k0:k0 + nk], start=True, stop=not diag)
                        if diag:
                            mm = pe.matmul(psum[:, 5 + u % A.nbanks, nk - P:nk], ident_b[:], causal_b[:], start=False, stop=True)
                    else:
                        pe.sem_inc(passed, 1)
                        mm = pe.matmul(psum[:, 5 + u % A.nbanks, 0:nk].rearrange("q (h k) -> q h k", h=4),
                                       A.q1[:, qd, i * P:(i + 1) * P], A.k1[:, qd, :, bass.ds(it * CTXP, CTXP)],
                                       start=True, stop=True)
                    mm.then_inc(A.s1_ps, 1)

                def turn(it, qd):
                    n = 2 * it + qd
                    if A.causal:
                        pe.wait_ge(A.mx, n + 1)
                    else:
                        pe.wait_ge(A.s1_free, (n + 1) * A.nunits + A.nbanks)
                    pe.wait_ge(A.neg, n + 1)
                    pe.transpose(psum[0:32, 7, 0:P], row_max[:], ident[:]).then_inc(A.mx_ps, 1)

                def scores(it, qd, s, p):
                    n = 2 * it + qd
                    c, kt, q0, diag, first, last = A.steps[s]
                    g = n * A.nsteps + s
                    pe.wait_ge(A.prob_ready, 2 * g + p + 1)
                    for j in range(2):
                        mm = pe.matmul(psum[0:A.keys, 2 * p + j, q0:CH],
                                       A.k2[:, qd, p, j, kt * P:kt * P + A.keys],
                                       A.q2[:, qd, p, c * CH + q0:(c + 1) * CH], start=True, stop=True)
                    mm.then_inc(A.st_ps, 1)

                def weigh(it, qd, s):
                    n = 2 * it + qd
                    c, kt, q0, diag, first, last = A.steps[s]
                    g = n * A.nsteps + s
                    if first:
                        pe.wait_ge(A.o_done, 2 * n + c + 1)
                    if diag:
                        k = sum(st[3] for st in A.steps[:s + 1])
                        pe.wait_ge(A.prob_masked, 2 * (n * A.ndiag + k))
                    pe.wait_ge(A.prob_ready, 2 * g + 2 + 2)
                    for h in range(4):
                        mm = pe.matmul(psum[32 * h:32 * h + 32, 4, q0:CH], A.vq[0:A.keys, qd, kt, h, :],
                                       A.prob[0:A.keys, s % 2, h // 2, h % 2, q0:CH], start=first, stop=last)
                    if last:
                        mm.then_inc(A.pv_ps, 1)

                for u in range(A.nunits):
                    unit(0, 0, u)
                turn(0, 0)
                for u in range(A.lead):
                    unit(0, 1, u)
                if A.lead == A.nunits:
                    turn(0, 1)

                def ahead(it, qd, units, more):
                    for d, u in units:
                        if d <= more:
                            unit(*after(it, qd, d), u)
                        if (d, u) == (2, 1) and A.causal and more:
                            turn(*after(it, qd, 1))

                def quad(it, qd, more):
                    n = 2 * it + qd
                    pe.wait_ge(A.ld2[qd], A.ld2_n * (it + 1))
                    pe.wait_ge(A.mrow, 16 * (n + 1) + 16)
                    pe.wait_ge(A.vq_ready, n + 1)
                    for s in range(A.nsteps):
                        scores(it, qd, s, 0)
                        ahead(it, qd, A.share(s, 0), more)
                        scores(it, qd, s, 1)
                        ahead(it, qd, A.share(s, 1), more)
                        if s > 0:
                            weigh(it, qd, s - 1)
                        ahead(it, qd, A.share(s, 2) + A.share(s, 3), more)
                    weigh(it, qd, A.nsteps - 1)
                    if not A.causal and more == 2:
                        turn(*after(it, qd, 2))

                over_iterations(pe, quad)

            pe.wait_ge(qk_free, 4 + 4 * NCH)
            pe.wait_ge(v_done, 16)
            pe.wait_ge(consts, 1)
            attention(SA)

            def project(w, at, src, ready, per, done):
                with pe.Fori(0, NCH) as c:
                    pe.wait_ge(ready, per * (c + 1))
                    for m in range(KT):
                        for k in range(KT):
                            mm = pe.matmul(dbank(2 * c + m), w[:, k, at + m * P:at + (m + 1) * P], tok(src, k, c),
                                           start=k == 0, stop=k == 1)
                        mm.then_inc(done, 1)

            pe.wait_ge(w_out3, 48)
            project(w3, 0, nrm, attn_ready, 1, op_ps)
            pe.wait_ge(ctx_ready, 2 * NCH)
            mean(ln2)
            variance(ln2)
            pe.wait_ge(wx01_ready, 1)
            for c in range(NCH):
                at = slice(c * CH, (c + 1) * CH)
                pe.wait_ge(y_ready, 2 * c + 2)
                for m in range(KT):
                    mo = slice(m * P, (m + 1) * P)
                    for k in range(KT):
                        pe.matmul(bank(2 * c + m), w3[:, k, D + m * P:D + (m + 1) * P], attn_o[:, k, at],
                                  start=k == 0, stop=False, skip_group_check=True)
                    for k in range(KT):
                        mm = pe.matmul(bank(2 * c + m), wx01[:, k, mo], nrm[:, k, at], start=False, stop=k == 1,
                                       skip_group_check=True)
                    mm.then_inc(z_ps, 1)
            with pe.Fori(0, NITER - 1) as s:
                for c in range(NCH):
                    at = slice(c * CH, (c + 1) * CH)
                    pe.wait_ge(vel_ready, 8 * s + 2 * c + 2)
                    for m in range(KT):
                        for k in range(KT):
                            mm = pe.matmul(bank(2 * c + m), wx01[:, k, m * P:(m + 1) * P], vel[:, k, at],
                                           start=False, stop=k == 1, skip_group_check=True)
                        mm.then_inc(z_ps, 1)
            pe.wait_ge(u_ready, 2 * NCH * NITER)
            mean(ln3)
            variance(ln3)
            pe.sem_inc(ff2_ps, 4)
            pe.wait_ge(w_late, 16 * 9)
            pe.wait_ge(ln3.out, 2 * NCH)
            with pe.Fori(0, NCH // 2) as cc:
                for half in range(2):
                    c = 2 * cc + half
                    for m in range(FT):
                        if m >= 4:
                            pe.wait_ge(gelu, FT * c + m - 3)
                        for k in range(KT):
                            mm = pe.matmul(bank(m % 4), wff1[:, k, m * P:(m + 1) * P], tok(nrm, k, c),
                                           start=k == 0, stop=k == 1)
                        mm.then_inc(ff1_ps, 1)
                    pe.wait_ge(gelu, FT * (c + 1))
                    for m in range(KT):
                        pe.wait_ge(x3, 2 * c + m + 1)
                        for k in range(FT):
                            mm = pe.matmul(bank(4 + 2 * half + m), wff2[:, k, m * P:(m + 1) * P], hid[:, half, k, :],
                                           start=k == 0, stop=k == FT - 1)
                        mm.then_inc(ff2_ps, 1)
            mean(ln4)
            pe.wait_ge(res4, 2 * NCH)
            variance(ln4)
            pe.wait_ge(ln4.out, 2 * NCH)
            project(wx4, 0, nrm, ln4.out, 2, xq_ps)
            pe.wait_ge(xq_free, 2 * NCH)
            for m in range(KT):
                for k in range(KT):
                    mm = pe.matmul(bank(m, BATCH * CTXP), wx4[:, k, D + m * P:D + (m + 1) * P], ctx_t[:, k, :],
                                   start=k == 0, stop=k == 1)
                mm.then_inc(xk_ps, 1)
            for b in range(BATCH):
                for k in range(KT):
                    mm = pe.matmul(bank(2 + b, D)[0:CTX], ctx_t[:, k, b * CTXP:b * CTXP + CTX], wx4[:, k, 2 * D:3 * D],
                                   start=k == 0, stop=k == 1)
                mm.then_inc(xv_ps, 1)
            pe.wait_ge(xk_free, 2)
            pe.wait_ge(xv_done, 2)
            attention(XA)
            project(wx4, 3 * D, wide, xattn_ready, 1, xo_ps)
            mean(ln5)
            variance(ln5)
            pe.wait_ge(consts, 2)
            pe.wait_ge(ln5.out, 2 * NCH)
            pe.sem_inc(cnt_ps, 4)
            pe.sem_inc(msk_used, 2)
            with pe.Fori(0, NCH) as c:
                for st in range(TREES + 2):
                    if st < TREES:
                        g = c * TREES + st
                        for half, (at, rows) in enumerate(((0, INNER), (INNER, LEAVES))):
                            if half == 0:
                                pe.wait_ge(dec_ready, g + 1)
                            pe.wait_ge(silu_ready, 2 * g + half + 1)
                            for k in range(KT):
                                o = st * NODES + at
                                mm = pe.matmul(bank(2 * (st % 2) + half)[0:rows], win[:, k, o:o + rows],
                                               tok(nrm, k, c), start=k == 0, stop=k == 1)
                            mm.then_inc(lg_ps, 1)
                    if 1 <= st <= TREES:
                        g = c * TREES + st - 1
                        pe.wait_ge(dec_ready, g + 1 + 2)
                        for half, (at, rows) in enumerate(((0, INNER), (INNER, LEAVES))):
                            pe.wait_ge(msk_ready, 2 * g + half + 1 + 2)
                            pe.matmul(bank(4 + half)[0:rows], sel[0:INNER, at:at + rows],
                                      decide[0:INNER, (st - 1) % 2, :], start=True, stop=True).then_inc(cnt_ps, 1)
                    if st >= 2:
                        t = st - 2
                        g = c * TREES + t
                        if t == 0:
                            pe.wait_ge(tree_out, 2 * c + 2)
                        pe.wait_ge(msk_ready, 2 * g + 2 + 4)
                        for m in range(KT):
                            mo = slice(m * P, (m + 1) * P)
                            pe.matmul(bank(6 + m), wout_in[0:INNER, t, mo], masked[0:INNER, t % 2, 0, :],
                                      start=t == 0, stop=False)
                            mm = pe.matmul(bank(6 + m), wout_leaf[:, t, mo], masked[:, t % 2, 1, :],
                                           start=False, stop=t == TREES - 1)
                        mm.then_inc(msk_used, 1)


INS = ["xT", "vec", "ident", "causal", "mean_w", "wqkv", "vbias", "wo", "wctx", "wx", "wff1", "wff2", "wx4", "win",
       "wout_in", "wout_leaf", "sel", "ctxT", "xvbias"]


def kernel(**inp):
    import numpy as np
    import concourse.bacc as bacc
    from concourse.bass_utils import run_bass_kernel_spmd

    f = {k: np.asarray(v) for k, v in inp.items()}

    def tiles(w):
        return w.reshape(-1, P, w.shape[1]).transpose(1, 0, 2)

    def cols(v):
        return v.reshape(-1, P).T

    A, X, T = "L0_attn_", "L0_xattn_", "L0_ffn_"
    bin2 = f[T + "b_in"].reshape(TREES, NODES)
    tin = np.zeros((P, TREES), np.float32)
    tin[:INNER] = bin2[:, :INNER].T
    turn = np.zeros((INNER, NODES), np.float32)
    for node in range(NODES):
        child = node
        while child:
            turn[(child - 1) // 2, node] = 1.0 if child % 2 == 0 else -1.0
            child = (child - 1) // 2
    rights = (turn > 0).sum(0).astype(np.float32)
    right = np.zeros((P, 2), np.float32)
    right[:INNER, 0] = rights[:INNER]
    right[:, 1] = rights[INNER:]
    qkv_b = f[A + "qkv_b"]
    vec = {"bqk": cols(qkv_b[:2 * D]), "bo": cols(f[A + "out_b"]), "binl": cols(f[A + "b_inl"]),
           "ffb1": cols(f[A + "ff_b1"]), "ffb2": cols(f[A + "ff_b2"]), "xbq": cols(f[X + "bq"]),
           "xbk": cols(f[X + "bk"]), "xbo": cols(f[X + "bo"]), "tin": tin, "tleaf": bin2[:, INNER:].T,
           "right": right, "eps": np.full((P, 1), EPS, np.float32)}
    for n in ("g_attn", "b_attn", "g1", "b1", "g2", "b2"):
        vec[n] = cols(f[A + n])
    wout = f[T + "W_out"].T.reshape(TREES, NODES, D).transpose(1, 0, 2)
    context = np.concatenate([f["ctx_1024"], f["ctx_1024"][:, -1:]], 1).reshape(BATCH * CTXP, D)
    q, k = np.arange(P)[:, None], np.arange(P)[None]
    arrays = {
        "xT": tiles(f["x"].reshape(TOK, D).T),
        "vec": np.concatenate([vec[n] for n in VEC], 1),
        "ident": np.eye(P, dtype=np.float32),
        "causal": np.where(k <= q, 0.0, LOW).astype(np.float32),
        "mean_w": np.full((P, P), 1.0 / D, np.float32),
        "wqkv": tiles(f[A + "qkv_w"]),
        "vbias": np.tile(qkv_b[None, 2 * D:], (P, 1)),
        "wo": tiles(f[A + "out_w"]), "wctx": tiles(f[A + "w_ctx"]), "wx": tiles(f[A + "w_x"]),
        "wff1": tiles(f[A + "ff_w1"]), "wff2": tiles(f[A + "ff_w2"]),
        "wx4": np.concatenate([tiles(f[X + n].T) for n in ("Wq", "Wk", "Wv", "Wo")], 2),
        "win": tiles(f[T + "W_in"].T),
        "wout_in": wout[:INNER], "wout_leaf": wout[INNER:],
        "sel": turn, "ctxT": tiles(context.T), "xvbias": np.tile(f[X + "bv"][None], (P, 1)),
    }
    nc = bacc.Bacc("TRN2", target_bir_lowering=False, num_devices=1)
    aps, feed = {}, {}
    for n in INS:
        arr = np.ascontiguousarray(arrays[n])
        feed[f"in_{n}"] = arr
        aps[n] = nc.dram_tensor(f"in_{n}", arr.shape, mybir.dt.from_np(arr.dtype), kind="ExternalInput").ap()
    out = nc.dram_tensor("out_t", (P, KT, TOK), F32, kind="ExternalOutput").ap()
    layer(nc, aps, out)
    r = run_bass_kernel_spmd(nc, [feed], core_ids=[0])
    return np.ascontiguousarray(r.results[0]["out_t"].transpose(2, 1, 0).reshape(BATCH, SEQ, D))
```

```python
from contextlib import ExitStack

import concourse.bass as bass
from concourse import mybir

F32 = mybir.dt.float32
F32R = mybir.dt.float32r
BF16 = mybir.dt.bfloat16
ALU = mybir.AluOpType
ACT = mybir.ActivationFunctionType
AX_X = mybir.AxisListType.X

P = 128
BATCH, SEQ, D = 2, 1024, 256
TOK = BATCH * SEQ
KT = D // P
CH = 512
NCH = TOK // CH
TPC = CH // P
HEADS, HD = 16, 16
CTX = 77
CTXP = 78
FF = 1024
FT = FF // P
NITER, DT = 8, 0.1
WPIECE = (KT * FF + FT * D) // NITER
TREES, DEPTH = 8, 7
NODES = 2 ** (DEPTH + 1) - 1
INNER = 2 ** DEPTH - 1
LEAVES = NODES - INNER
WT = 2 * P * KT + 2 * D
EPS = 1e-5
SCALE = HD ** -0.5
R2 = 3 * HD
LOW = -1e30

VEC = {}
for _name, _n in [("bqk", 4), ("g_attn", 2), ("b_attn", 2), ("bo", 2), ("g1", 2), ("b1", 2), ("binl", 2),
                  ("g2", 2), ("b2", 2), ("ffb1", FT), ("ffb2", 2), ("xbq", 2), ("xbk", 2), ("xbo", 2),
                  ("eps", 1)]:
    VEC[_name] = (sum(n for _, n in VEC.values()), _n)
NVEC = sum(n for _, n in VEC.values())

HT = P // HD
QUADS = HT // 4
ITS = KT * BATCH


def layer(nc, a, out_t):
    q3, xq3 = [nc.dram_tensor(n, (HT, 3, HD, KT * TOK), F32).ap() for n in ("q3", "xq3")]
    k3 = nc.dram_tensor("k3", (HT, 3, HD, KT * TOK), F32).ap()
    xk3 = nc.dram_tensor("xk3", (HT, 3, HD, KT * BATCH * CTXP), F32).ap()
    o3, xo3 = [nc.dram_tensor(n, (ITS, HT, 2, HD, SEQ), F32).ap() for n in ("o3", "xo3")]
    r3, xr3 = [nc.dram_tensor(n, (ITS, HT, SEQ), F32).ap() for n in ("r3", "xr3")]

    ctx = ExitStack()
    with ctx:
        def sb(name, shape, dt=F32, stack=ctx):
            return stack.enter_context(nc.sbuf_tensor(name, shape, dt))

        def with_low(name, shape, stack=ctx):
            with ExitStack() as low_stack:
                low = sb(f"{name}_lo", shape, F32, low_stack)
            return sb(name, shape, F32, stack), low

        def sem(name):
            return ctx.enter_context(nc.semaphore(name))

        psum = ctx.enter_context(nc.psum_tensor("psum", [P, 8, CH], F32))
        pflat = psum[:].rearrange("p b n -> p (b n)")

        def bank(i, n=CH):
            return psum[:, i, 0:n]

        def tok(t, k, c):
            return t[:, k, bass.ds(c * CH, CH)]

        vec = sb("vec", [P, NVEC])
        mean_w = sb("mean_w", [P, P])
        ident = sb("ident", [P, P])
        ident_b = sb("ident_b", [P, P], BF16)
        caus_f = sb("caus_f", [P, P])
        causal_b = sb("causal_b", [P, P], BF16)
        vbias = sb("vbias", [P, D])
        b1_scaled = sb("b1_scaled", [P, KT])
        res = sb("res", [P, KT, TOK])
        nrm, nrm_lo = with_low("nrm", [P, KT, TOK])
        stage = sb("stage", [P, QUADS, SEQ])
        sd = sb("sd", [P, 2, 2, TPC])
        rs = sb("rs", [P, 2, 2, TPC])
        wide = sb("wide", [P, KT, TOK])
        w3 = sb("w3", [P, KT, 3 * D])
        part_max = sb("part_max", [P, 64])
        row_max = sb("row_max", [P, 32])
        neg_max = sb("neg_max", [32, 2, P], F32R)

        def v_(name, i=0, rows=P):
            at = VEC[name][0] + i
            return vec[0:rows, at:at + 1]

        values = wide[:].rearrange("p k t -> p (k t)").rearrange("p (i t f) -> p i t f", i=ITS, f=P)
        scratch = wide

        s_self = ExitStack()
        sums = sb("sums", [P, SEQ // HD], F32, s_self)
        recip = sb("recip", [P, SEQ // HD], F32, s_self)
        s_part = ExitStack()
        part_hi = sb("part_hi", [P, 2, 4, CH], F32, s_part)
        part_lo = sb("part_lo", [P, 2, 4, CH], F32, s_part)
        s_part.close()
        den = sb("den", [P, KT, TOK], F32, s_self)
        prob = sb("prob", [P, 2, 2, 2, CH], F32, s_self)
        q2 = sb("q2", [P, 2, 2, SEQ], F32R, s_self)
        q1 = sb("q1", [P, 2, SEQ], F32R, s_self)
        k1 = sb("k1", [P, 2, 4, SEQ], F32R, s_self)
        k2 = sb("k2", [P, 2, 2, 2, SEQ], F32R, s_self)
        vq = sb("vq", [P, 2, SEQ // P, 4, 32], F32, s_self)
        s_self.close()

        wx4 = sb("wx4", [P, KT, 4 * D])
        wt, wt_lo = with_low("wt", [P, 2, WT + 2])
        wt_hi = sb("wt_hi", [P, 2, WT])
        ctx_t = sb("ctx_t", [P, KT, BATCH * CTXP])
        sel_f = sb("sel_f", [P, 2 * P])
        sel = sb("sel", [P, 2 * P], BF16)
        xvbias = sb("xvbias", [P, D])
        xk1 = sb("xk1", [P, QUADS, 4, ITS * CTXP], F32R)
        xk2 = sb("xk2", [P, 2, 2, 2, CTXP], F32R)
        xvals = sb("xvals", [P, ITS, P])
        s_mlp = ExitStack()
        wff, wff_lo = with_low("wff", [P, KT * FF + FT * D], s_mlp)
        wff_hi = sb("wff_hi", [P, KT * FF + FT * D], F32, s_mlp)
        s_wx = ExitStack()
        wx01 = sb("wx01", [P, KT, D], F32, s_wx)
        s_wx.close()
        xk_hi = sb("xk_hi", [P, KT, BATCH * CTXP], F32, s_mlp)
        xk_lo = sb("xk_lo", [P, KT, BATCH * CTXP], F32, s_mlp)
        x0 = sb("x0", [P, KT, TOK], F32, s_mlp)
        s_scan = ExitStack()
        attn_o = sb("attn_o", [P, KT, TOK], F32, s_scan)
        vel = sb("vel", [P, KT, TOK], F32, s_scan)
        act_u = sb("act_u", [P, KT, TOK], F32, s_scan)
        s_scan.close()
        hid_hi = sb("hid_hi", [P, FT, CH], F32, s_mlp)
        nrm_hi = sb("nrm_hi", [P, KT, TOK], F32, s_mlp)
        hid, hid_lo = with_low("hid", [P, FT, CH], s_mlp)
        s_mlp.close()
        s_cross = ExitStack()
        xq2 = sb("xq2", [P, 2, 2, SEQ], F32R, s_cross)
        xq1 = sb("xq1", [P, 2, SEQ], F32R, s_cross)
        xvq = sb("xvq", [P, 2, 1, 4, 32], F32, s_cross)
        xsums = sb("xsums", [P, SEQ // HD], F32, s_cross)
        xrecip = sb("xrecip", [P, SEQ // HD], F32, s_cross)
        xprob = sb("xprob", [P, 2, 2, 2, CH], F32, s_cross)
        s_xpart = ExitStack()
        xpart_hi = sb("xpart_hi", [P, 2, KT, CH], F32, s_xpart)
        xpart_lo = sb("xpart_lo", [P, 2, KT, CH], F32, s_xpart)
        s_xpart.close()
        xden = sb("xden", [P, KT, TOK], F32, s_cross)
        scratch5 = sb("scratch5", [P, KT, 4 * CH], F32, s_cross)
        s_cross.close()
        s_tree = ExitStack()
        silu = sb("silu", [P, 2, 2, CH], F32, s_tree)
        masked, masked_lo = with_low("masked", [P, 2, 2, CH], s_tree)
        masked_hi = sb("masked_hi", [P, 2, 2, CH], F32, s_tree)
        decide = sb("decide", [P, 2, CH], BF16, s_tree)
        tree_hi = sb("tree_hi", [P, KT, TOK], F32, s_tree)
        s_tree.close()

        x_in = [sem(f"x_in{c}") for c in range(NCH)]
        c_in, w_in3, w_out3, w_late, x0_in, out_st = [
            sem(n) for n in ("c_in", "w_in3", "w_out3", "w_late", "x0_in", "out_st")]
        passed = sem("passed")
        zeros_set, ones_set = sem("zeros_set"), sem("ones_set")
        consts, wx01_ready, scan_init = sem("consts"), sem("wx01_ready"), sem("scan_init")

        class Norm:
            total, mean, d_ready, sq, sqs, var, sd, rs, bc = [
                sem(f"ln_{s}") for s in ("total", "mean", "d_ready", "sq", "sqs", "var", "sd", "rs", "bc")]

            def __init__(self, at, src, ready, per, d, bank, signals, gain=None, plus=0,
                         scratch=scratch):
                self.src, self.ready, self.per, self.plus, self.d = src, ready, per, plus, d
                self.bank, self.gain, self.scratch = bank, gain, scratch
                self.at = at * NCH
                self.out, self.scaled, self.hi = [sem(f"ln{at + 1}_{n}") if n in signals else None
                                                  for n in ("out", "scaled", "hi")]

            def square(self, c):
                return self.scratch[:, :, c % 2 * CH:(c % 2 + 1) * CH]

            def sum_of(self, what, c):
                return self.scratch[:, what, (2 + c % 2) * CH:(3 + c % 2) * CH]

        res1, res2, res4, res5 = sem("res1"), sem("res2"), sem("res4"), sem("res5")
        ln1 = Norm(0, nrm, None, 0, res, lambda c: c, ("out", "scaled"))
        ln2 = Norm(1, res, res1, 1, nrm, lambda c: (5, 6, 4, 7)[c], ("scaled",), "g1")
        ln3 = Norm(2, res, res2, 2, nrm, lambda c: 6 + c % 2, ("out", "scaled", "hi"), "g2")
        ln4 = Norm(3, res, res4, 2, nrm, lambda c: 6 + c % 2, ("out",), plus=2)
        ln5 = Norm(4, res, res5, 2, nrm, lambda c: (5, 6, 4, 7)[c], ("out", "scaled", "hi"), scratch=scratch5)
        rs2, r1sq, v2, sd2, xl_ready, b1_set = [
            sem(n) for n in ("rs2", "r1sq", "v2", "sd2", "xl_ready", "b1_set")]

        qk_ps, qk_hi, qk_free, v_ps, v_done = [sem(n) for n in ("qk_ps", "qk_hi", "qk_free", "v_ps", "v_done")]
        qk_st, xq_st = [[sem(f"{n}{half}") for half in range(2)] for n in ("qk_st", "xq_st")]
        xk_st, xk_in = sem("xk_st"), sem("xk_in")
        xq_ps, xq_hi_s, xq_free, xk_ps, xk_hi_s, xk_free, xv_ps, xv_done = [
            sem(n) for n in ("xq_ps", "xq_hi_s", "xq_free", "xk_ps", "xk_hi_s", "xk_free", "xv_ps", "xv_done")]
        attn_ready, op_ps, ctx_ready = sem("attn_ready"), sem("op_ps"), sem("ctx_ready")
        y_ready, z_ps, u_ready, a_ready, vel_ready = [
            sem(n) for n in ("y_ready", "z_ps", "u_ready", "a_ready", "vel_ready")]
        wff_in, wff_h, wff_l, ff1_ps, gelu, hid_h, hid_l, ff2_ps, x0_added = [sem(n) for n in (
            "wff_in", "wff_h", "wff_l", "ff1_ps", "gelu", "hid_h", "hid_l", "ff2_ps", "x0_added")]
        xattn_ready, xo_ps = sem("xattn_ready"), sem("xo_ps")
        lg_ps, silu_ready, dec_ready, cnt_ps, msk_ready, msk_h, msk_l, out_ps, tree_out, wt_h, wt_l = [
            sem(n) for n in ("lg_ps", "silu_ready", "dec_ready", "cnt_ps", "msk_ready", "msk_h", "msk_l", "out_ps",
                             "tree_out", "wt_h", "wt_l")]
        wt_in = [sem(f"wt_in{i}") for i in range(2)]

        class Attention:

            def __init__(self, name, steps, units, lead, causal, keys, width, scratch, bufs, recip_qd):
                self.steps, self.units, self.causal, self.keys, self.width = steps, units, causal, keys, width
                self.q3, self.k3, self.o3, self.r3 = scratch
                (self.q1, self.k1, self.q2, self.k2, self.vq, self.prob, self.sums, self.recip, self.den,
                 self.out) = bufs
                self.recip_qd = recip_qd
                self.ld1, self.ld2, self.mrow, self.o_st, self.stage_free = [[sem(f"{name}_{s}{qd}") for qd in range(QUADS)]
                                                           for s in ("ld1", "ld2", "mrow", "o_st", "stage_free")]
                (self.s1_ps, self.s1_free, self.mx, self.mx_ps, self.neg, self.st_ps,
                 self.prob_ready, self.prob_masked, self.vq_ready, self.pv_ps, self.o_done,
                 self.sums_in, self.rec, self.rec_st, self.rec_free, self.den_in, self.num, self.num_last) = [
                    sem(f"{name}_{s}") if causal or s not in ("mx", "prob_masked") else None for s in (
                    "s1_ps", "s1_free", "mx", "mx_ps", "neg", "st_ps", "prob_ready", "prob_masked",
                    "vq_ready", "pv_ps", "o_done","sums_in", "rec", "rec_st", "rec_free", "den_in", "num", "num_last")]
                self.late_from = {} if causal else {"num1": ITS - 2,
                                                    "sums_in": ITS - 2, "rec_st": ITS - 2, "den_in": ITS - 2}
                self.late = {n: sem(f"{name}_{n}_late") for n in self.late_from}
                self.usual = {"num0": self.num, "num1": self.num, "sums_in": self.sums_in,
                              "rec_st": self.rec_st, "den_in": self.den_in}
                self.ld1_n = 16 * 5 if causal else 16
                self.ld2_n = 16 * 3
                self.nsteps = len(self.steps)
                self.nunits = len(self.units)
                self.ndiag = sum(st[3] for st in self.steps)
                self.nbanks = 3 if self.nunits % 3 == 0 else 2
                todo = [(1, u) for u in range(lead, self.nunits)] + [(2, u) for u in range(lead)]
                cols = [self.units[u][3] + 64 for _, u in todo]
                size = [CH - st[2] + 64 for st in self.steps]
                self.plan, at = [[] for _ in steps], 0
                for s in range(self.nsteps):
                    while at < len(todo) and (s == self.nsteps - 1 or
                                              sum(cols[:at]) * sum(size) < sum(cols) * sum(size[:s + 1])):
                        self.plan[s].append(todo[at])
                        at += 1
                self.lead = lead

            def nth(self, what, it):
                if what in self.late and isinstance(it, int) and it >= self.late_from[what]:
                    return self.late[what], it - self.late_from[what]
                return self.usual[what], it

            def share(self, s, quarter):
                n = len(self.plan[s])
                return self.plan[s][n * quarter // 4:n * (quarter + 1) // 4]

        self_steps = [(c, kt, max(0, (kt - TPC * c) * P), kt >= TPC * c, kt == 0, kt == TPC * (c + 1) - 1)
                      for c in range(SEQ // CH) for kt in range(TPC * (c + 1))]
        self_units = [(h, i, kh * CH, min(CH, (i + 1) * P - kh * CH), i // TPC == kh)
                      for h in range(4) for i in range(SEQ // P) for kh in range(i // TPC + 1)]
        cross_steps = [(c, 0, 0, False, True, True) for c in range(SEQ // CH)]
        cross_units = [(0, i, 0, 4 * CTXP, False) for i in range(SEQ // P)]
        SA = Attention("sa", self_steps, self_units, 8, True, P, SEQ, (q3, k3, o3, r3),
                       (q1, k1, q2, k2, vq, prob, sums, recip, den, nrm), 0)
        XA = Attention("xa", cross_steps, cross_units, 8, False, CTX, CTXP, (xq3, xk3, xo3, xr3),
                       (xq1, xk1, xq2, xk2, xvq, xprob, xsums, xrecip, xden, wide), 1)

        def skewed(*stages, chunks=NCH):
            for step in range(chunks + max(lag for _, lag in stages)):
                for stage, lag in stages:
                    if 0 <= step - lag < chunks:
                        stage(step - lag)

        def cols_of(c):
            return slice(c * CH, (c + 1) * CH)

        def rounded(t):
            return t.bitcast(F32R)

        def three(pe, out, w_hi, w_lo, x_hi, x_lo, start, stop):
            pe.matmul(out, rounded(w_hi), rounded(x_hi), start=start, stop=False)
            pe.matmul(out, rounded(w_hi), rounded(x_lo), start=False, stop=False)
            return pe.matmul(out, rounded(w_lo), rounded(x_hi), start=False, stop=stop)

        class Step:

            def __init__(self, tt, off):
                self.g, self.trees = tt * 2 * NCH + off, 2 * tt + off // NCH
                self.tree, self.chunk, self.buf = (off // NCH) % 2, off % NCH, off % 2
                self.at = slice(self.chunk * CH, (self.chunk + 1) * CH)

        STEPS = TREES * NCH
        by_batch = [range(b * NCH // BATCH, (b + 1) * NCH // BATCH) for b in range(BATCH)]

        def qk_bank(c, m):
            return bank(5 + (4 * c + m) % 3 if c in by_batch[0] else m)

        def norm_beside(c):
            return (ln3, 2) if c == 0 else (ln4, c - 1)

        def xq_bank(c):
            return 2 * (c % 2)

        def tree_steps(eng, first, second, third):
            first(Step(0, 0))
            first(Step(0, 1))
            second(Step(0, 0))
            with eng.Fori(0, TREES // 2 - 1) as tt:
                for i in range(2 * NCH):
                    first(Step(tt, i + 2))
                    second(Step(tt, i + 1))
                    third(Step(tt, i))
            for i in range(2 * NCH):
                last = TREES // 2 - 1
                if i + 2 < 2 * NCH:
                    first(Step(last, i + 2))
                if i + 1 < 2 * NCH:
                    second(Step(last, i + 1))
                third(Step(last, i))

        def flat(t):
            return t[:].rearrange("p k t -> p (k t)")

        def over_iterations(eng, body, peel_first=False):
            if peel_first:
                for qd in range(QUADS):
                    body(0, qd, 2)
            with eng.Fori(int(peel_first), ITS - 1) as it:
                for qd in range(QUADS):
                    body(it, qd, 2)
            for qd in range(QUADS):
                body(ITS - 1, qd, QUADS - 1 - qd)

        def after(it, qd, d):
            return it + (qd + d) // QUADS, (qd + d) % QUADS

        def store_parts(sp, out3, part_hi, part_lo, m_of, half, at, done, r_lo):
            for r in range(3):
                part = part_lo if r == r_lo else part_hi
                sp.dma_start(out3[:, r, :, at], part[:, half, m_of, :]).then_inc(done, 16)

        def store_out(eng, A, it, qd):
            eng.wait_ge(A.o_done, 2 * (2 * it + qd) + 3)
            eng.sem_inc(passed, 1)
            eng.dma_start(A.o3[bass.ds(it, 1), 4 * qd:4 * qd + 4].rearrange("o h s d n -> (o h s d) n"),
                          stage[:, qd, :]).then_inc(A.o_st[qd], 16)

        def pack(eng, A, it, qd):
            if A.causal:
                store_out(eng, A, it, qd)
            eng.wait_ge(A.o_st[qd], 16 * it + 16)
            eng.sem_inc(A.stage_free[qd], 1)
            eng.dma_start(flat(A.out)[64 * qd:64 * qd + 64, bass.ds(it * SEQ, SEQ)],
                          A.o3[bass.ds(it, 1), 4 * qd:4 * qd + 4, 0].rearrange("o h d n -> (o h) d n"))\
                .then_inc(A.num_last if isinstance(it, int) and it == ITS - 1 and (qd or not A.late)
                          else A.nth(f"num{qd}", it)[0], 16)
            if qd == QUADS - 1:
                eng.wait_ge(A.rec, it + 1)
                eng.wait_ge(A.o_st[0], 16 * it + 16)
                eng.sem_inc(passed, 1)
                eng.dma_start(A.sums[:], A.o3[bass.ds(it, 1), :, 1, 0].rearrange("o h (s n) -> (o h) s n", s=HD))\
                    .then_inc(A.nth("sums_in", it)[0], 16)

        def spread(eng, A, it):
            rec_done, before = A.nth("rec_st", it)
            eng.wait_ge(A.rec, it + 2)
            eng.sem_inc(passed, 1)
            eng.dma_start(A.r3[bass.ds(it, 1)].rearrange("o h (s n) -> (o h s) n", s=HD), A.recip[:])\
                .then_inc(rec_done, 16)
            eng.wait_ge(rec_done, 16 * before + 16)
            eng.sem_inc(A.rec_free, 1)
            eng.dma_start(flat(A.den)[:, bass.ds(it * SEQ, SEQ)],
                          A.r3[bass.ds(it, 1)].rearrange("o h (u n) -> (o h) u n", u=1).to_broadcast([HT, HD, SEQ]))\
                .then_inc(A.nth("den_in", it)[0], 16)

        block = ctx.enter_context(nc.Block())

        @block.sync
        def _(sp):
            for c in range(NCH):
                if c == 1:
                    sp.wait_ge(c_in, 16 * 4)
                sp.dma_start(nrm[:, :, c * CH:(c + 1) * CH], a["xT"][:, :, c * CH:(c + 1) * CH]).then_inc(x_in[c], 16)
            sp.dma_start(w3[:], a["wqkv"]).then_inc(w_in3, 16)

            def store_qk(batch):
                for c in by_batch[batch]:
                    for m in range(4):
                        sp.wait_ge(qk_free, 4 * c + m + 1 + 3)
                        store_parts(sp, q3 if m < 2 else k3, part_hi, part_lo, m, c % 2,
                                    slice(m % 2 * TOK + c * CH, m % 2 * TOK + (c + 1) * CH), qk_st[c % 2],
                                    2 if m < 2 else 1)

            def load_first(A, it, qd):
                n = 2 * it + qd
                if not (isinstance(n, int) and n < 2):
                    sp.wait_ge(A.mx_ps, n + 1)
                    sp.sem_inc(passed, 1)
                sp.dma_start(A.q1[0:4 * HD, qd, :].bitcast(F32),
                             A.q3[4 * qd:4 * qd + 4, 0, :, bass.ds(it * SEQ, SEQ)].rearrange("h d t -> d h t"))\
                    .then_inc(A.ld1[qd], 16)
                if A.causal:
                    for h in range(4):
                        sp.dma_start(A.k1[h:4 * HD:4, qd, h, :].bitcast(F32),
                                     k3[4 * qd + h, 0, :, bass.ds(it * SEQ, SEQ)]).then_inc(A.ld1[qd], 16)

            def load_second(A, it, qd):
                n = 2 * it + qd
                if not (isinstance(n, int) and n < 2):
                    sp.wait_ge(A.prob_ready, 2 * A.nsteps * (n - 1) + 2)
                    sp.sem_inc(passed, 1)
                at = bass.ds(it * SEQ, SEQ)
                sp.dma_start(A.q2[0:2 * R2, qd, :, :].bitcast(F32),
                             A.q3[4 * qd:4 * qd + 4, :, :, at].rearrange("(p j) r d t -> (j r d) p t", p=2))\
                    .then_inc(A.ld2[qd], 16)
                for j in range(2):
                    sp.dma_start(A.k2[R2 * j:R2 * j + R2, qd, :, j, :].bitcast(F32),
                                 A.k3[4 * qd + j:4 * qd + 4:2, :, :, bass.ds(it * A.width, A.width)]
                                 .rearrange("p r d t -> (r d) p t")).then_inc(A.ld2[qd], 16)

            def load_max(A, it, qd):
                sp.wait_ge(A.neg, 2 * it + qd + 2)
                sp.sem_inc(passed, 1)
                sp.dma_start(A.q2[2 * R2:2 * R2 + 2, qd, :, :].bitcast(F32), neg_max[:, qd, :].bitcast(F32))\
                    .then_inc(A.mrow[qd], 16)

            def attention(A, packs, stored, per, store):
                for qd in range(QUADS):
                    sp.sem_inc(A.mrow[qd], 16)
                for half in range(2):
                    sp.wait_ge(stored[half], 2 * per)
                load_first(A, 0, 0)
                load_second(A, 0, 0)
                load_first(A, 0, 1)
                store(1)
                load_max(A, 0, 0)
                for half in range(2):
                    sp.wait_ge(stored[half], (NCH // 2 + 1) * per)

                def quad(it, qd, more):
                    first = isinstance(it, int) and it == 0
                    if more == 2:
                        load_first(A, *after(it, qd, 2))
                    if more >= 1:
                        load_second(A, *after(it, qd, 1))
                    if more >= 1 and not A.causal:
                        load_max(A, *after(it, qd, 1))
                    if packs and not (first and qd == 0):
                        pack(sp, A, *after(it, qd, -1))
                    if packs and qd == 1 and not first:
                        spread(sp, A, it - 1)
                    if more >= 1 and A.causal:
                        load_max(A, *after(it, qd, 1))

                over_iterations(sp, quad, True)
                if not packs:
                    pack(sp, A, ITS - 2, QUADS - 1)
                    spread(sp, A, ITS - 2)
                pack(sp, A, ITS - 1, QUADS - 1)
                spread(sp, A, ITS - 1)

            store_qk(0)
            sp.wait_ge(consts, 1)
            attention(SA, True, qk_st, 16 * 12, store_qk)
            sp.wait_ge(attn_ready, NCH)
            sp.dma_start(wff[:], a["wff"]).then_inc(wff_in, 16)
            for t, n in ((wx4, "wx4"), (ctx_t, "ctxT"), (sel_f, "sel"), (xvbias, "xvbias")):
                sp.dma_start(t[:], a[n]).then_inc(w_late, 16)
            for i in range(2):
                sp.dma_start(wt[:, i, :], a["wt"][i]).then_inc(wt_in[i], 16)
            sp.dma_start(x0[:], a["xT"]).then_inc(x0_in, 16)
            sp.wait_ge(xk_free, KT)
            for m in range(KT):
                for r in range(3):
                    part = xk_lo if r == 1 else xk_hi
                    sp.dma_start(xk3[:, r, :, m * BATCH * CTXP:(m + 1) * BATCH * CTXP], part[:, m, :])\
                        .then_inc(xk_st, 16)
            sp.wait_ge(consts, 2)
            sp.wait_ge(xk_st, 16 * 3 * KT)
            for qd in range(QUADS):
                for h in range(4):
                    sp.dma_start(xk1[h:4 * HD:4, qd, h, :].bitcast(F32), xk3[4 * qd + h, 0]).then_inc(xk_in, 16)

            def store_xq(batch):
                for c in by_batch[batch]:
                    for m in range(KT):
                        sp.wait_ge(xq_free, 2 * c + m + 1)
                        store_parts(sp, xq3, xpart_hi, xpart_lo, m, c % 2, slice(m * TOK + c * CH, m * TOK + (c + 1) * CH),
                                    xq_st[c % 2], 2)

            store_xq(0)
            sp.wait_ge(consts, 4)
            attention(XA, False, xq_st, 16 * 6, store_xq)
            with sp.Fori(0, TREES // 2 - 1) as tt:
                for i in range(2):
                    sp.wait_ge(out_ps, NCH * (2 * tt + i + 1))
                    sp.sem_inc(passed, 1)
                    sp.dma_start(wt[:, i, :], a["wt"][bass.ds(2 * tt + i + 2, 1)].rearrange("o p n -> (o p) n"))\
                        .then_inc(wt_in[i], 16)
            for c in range(NCH):
                sp.wait_ge(tree_out, STEPS - NCH + c + 1 + 1)
                sp.dma_start(out_t[:, :, c * CH:(c + 1) * CH], res[:, :, c * CH:(c + 1) * CH]).then_inc(out_st, 16)
            sp.wait_ge(out_st, 16 * NCH)

        @block.gpsimd
        def _(pool):
            def preset_keys(k1, k2, nth):
                pool.memset(k1[:].bitcast(F32), 0.0)
                pool.memset(k2[:].bitcast(F32), 0.0).then_inc(zeros_set, 1)
                pool.wait_ge(zeros_set, 3 * nth - 2)
                pool.memset(k2[2 * R2:2 * R2 + 2].bitcast(F32), 1.0).then_inc(ones_set, 1)
                pool.wait_ge(ones_set, 3 * nth - 2)
                for j in range(2):
                    row = k2[2 * R2:2 * R2 + 2, :, :, j, :].rearrange("r b p n -> r (b p) n")
                    pool.tensor_scalar(row, row.bitcast(F32), ident[2 * R2:2 * R2 + 2, 2 * R2 + j:2 * R2 + j + 1],
                                       None, ALU.mult).then_inc(ones_set, 1)
                pool.wait_ge(ones_set, 3 * nth)

            def preset_rest(q1, q2, vq, sums, nth, prob=None):
                pool.memset(q1[:].bitcast(F32), 0.0)
                pool.memset(vq[:], 1.0)
                if prob is not None:
                    pool.memset(prob[:], 0.0)
                pool.memset(sums[:], 1.0).then_inc(zeros_set, 1)
                pool.wait_ge(zeros_set, 3 * nth - 1)
                pool.memset(q2[2 * R2:P].bitcast(F32), 0.0).then_inc(zeros_set, 1)
                pool.wait_ge(zeros_set, 3 * nth)
                pool.sem_inc(consts, 1)

            pool.memset(part_max[:], -3e38)
            pool.wait_ge(c_in, 16 * 4)
            pool.tensor_copy(ident_b[:], ident[:])
            pool.tensor_copy(causal_b[:], caus_f[:])
            preset_keys(k1, k2, 1)
            preset_rest(q1, q2, vq, sums, 1)

            def attention(A, vals, ready):

                def copy_values(it, qd):
                    pool.wait_ge(A.pv_ps, 2 * (2 * it + qd) + 2)
                    src = vals[:, bass.ds(it, 1), :, 64 * qd:64 * qd + 64].rearrange("p o t (h d) -> p (o t) h d", h=4)
                    pool.tensor_copy(A.vq[0:A.keys, qd, :, :, 0:HD], src).then_inc(A.vq_ready, 1)

                if A.causal:
                    pool.wait_ge(*ready)
                    copy_values(0, 0)

                def quad(it, qd, more):
                    n = 2 * it + qd
                    first = isinstance(it, int) and it == 0
                    if more >= 1 and A.causal:
                        copy_values(*after(it, qd, 1))
                    if not A.causal and more > 1 and not (first and qd == 0):
                        pack(pool, A, *after(it, qd, -1))
                    if not A.causal and more > 1 and qd == 1 and not first:
                        spread(pool, A, it - 1)
                    for s, (c, kt, q0, diag, first, last) in enumerate(A.steps):
                        if not diag:
                            continue
                        for p in range(2):
                            pool.wait_ge(A.prob_ready, 2 * (n * A.nsteps + s) + p + 3)
                            pool.sem_inc(passed, 1)
                            blk = A.prob[:, s % 2, p, :, q0:q0 + P]
                            pool.affine_select(out=blk, in_=blk, compare_op=ALU.is_ge, fill=0.0, base=0,
                                               pattern=[[0, 2], [1, P]], channel_multiplier=-1)\
                                .then_inc(A.prob_masked, 1)

                over_iterations(pool, quad, not A.causal)
                if not A.causal:
                    pool.wait_ge(A.num, 16 * (QUADS * (ITS - 1) - 1))
                    pack(pool, A, ITS - 1, 0)

            attention(SA, values, (v_done, 16))
            pool.wait_ge(w_out3, 48)
            pool.wait_ge(attn_ready, NCH)
            pool.tensor_scalar(wx01[:], w3[:, :, 2 * D:3 * D], DT * DT, None, ALU.mult).then_inc(wx01_ready, 1)
            pool.memset(vel[:], 0.0).then_inc(scan_init, 1)
            preset_keys(xk1, xk2, 2)
            pool.sem_inc(consts, 1)
            with pool.Fori(0, NITER) as s:
                for u in range(2 * NCH):
                    at = slice((u // 2) * CH, (u // 2 + 1) * CH)
                    pool.wait_ge(vel_ready, 8 * s + u + 1)
                    pool.tensor_tensor(nrm[:, u % 2, at], nrm[:, u % 2, at], vel[:, u % 2, at], ALU.add)\
                        .then_inc(y_ready, 1)
            pool.wait_ge(w_late, 16 * 4)
            pool.tensor_copy(sel[:], sel_f[:]).then_inc(consts, 1)

            def split_weights(tt, i):
                pool.wait_ge(wt_in[i], 16 * tt + 16)
                pool.sem_inc(passed, 1)
                pool.tensor_copy(rounded(wt_hi[:, i, :]), wt[:, i, 0:WT]).then_inc(wt_h, 1)
                pool.wait_ge(wt_h, 2 * tt + i + 1)
                pool.tensor_tensor(rounded(wt_lo[:, i, 0:WT]), wt[:, i, 0:WT], wt_hi[:, i, :], ALU.subtract).then_inc(wt_l, 1)

            pool.wait_ge(x0_in, 16)
            with pool.Fori(0, NCH) as c:
                pool.wait_ge(ln3.d_ready, 2 * (ln3.at + c) + 2)
                for m in range(KT):
                    pool.tensor_tensor(tok(res, m, c), tok(res, m, c), tok(x0, m, c), ALU.add).then_inc(x0_added, 1)
            for i in range(2):
                split_weights(0, i)
            pool.wait_ge(res4, 2 * NCH + 2)
            pool.wait_ge(xk_st, 16 * 3 * KT)
            preset_rest(xq1, xq2, xvq, xsums, 2, xprob)
            attention(XA, xvals, (xv_done, 2))
            with pool.Fori(1, TREES // 2) as tt:
                for i in range(2):
                    split_weights(tt, i)

        @block.scalar
        def _(act):
            for t, n in ((vec[:], "vec"), (ident[:], "ident"), (caus_f[:], "causal"), (mean_w[:], "mean_w")):
                act.dma_start(t, a[n]).then_inc(c_in, 16)
            act.dma_start(vbias[:], a["vbias"]).then_inc(w_in3, 16)
            act.wait_ge(c_in, 64)

            def square(L):
                def chunk(c):
                    act.wait_ge(L.d_ready, 2 * (L.at + c) + 2)
                    if L.at + c >= 2:
                        act.wait_ge(L.sqs, L.at + c - 1)
                    act.activation(L.square(c), L.d[:, :, cols_of(c)], ACT.Square).then_inc(L.sq, 1)
                return chunk

            def deviation(L):
                def chunk(c):
                    act.wait_ge(L.var, L.at + c + 1)
                    if L.at + c >= 2:
                        act.wait_ge(L.rs, L.at + c - 1)
                    act.activation(sd[:, c % 2, 0, :], bank(L.bank(c), TPC), ACT.Sqrt, bias=v_("eps"))\
                        .then_inc(L.sd, 1)
                return chunk

            def second_deviation(c):
                act.wait_ge(v2, c + 1)
                act.activation(sd[:, c % 2, 1, :], sd[:, c % 2, 1, :], ACT.Sqrt, bias=v_("eps")).then_inc(sd2, 1)

            def first_bias(c):
                for k in range(KT):
                    act.wait_ge(ln1.scaled, 2 * c + k + 1)
                    act.activation(nrm[:, k, cols_of(c)], nrm[:, k, cols_of(c)], ACT.Identity, bias=v_("b_attn", k))\
                        .then_inc(ln1.out, 1)

            def qk_high(c):
                act.wait_ge(qk_st[c % 2], 16 * 12 * (c // 2) + 16 * 12)
                for m in range(4):
                    act.wait_ge(qk_ps, 4 * c + m + 1)
                    act.activation(part_hi[:, c % 2, m, :].bitcast(F32R), qk_bank(c, m), ACT.Identity,
                                   bias=v_("bqk", m)).then_inc(qk_hi, 1)

            for half in range(2):
                act.sem_inc(qk_st[half], 16 * 12)
                act.sem_inc(xq_st[half], 16 * 6)
            skewed((first_bias, 5), (second_deviation, 3), (deviation(ln1), 2), (square(ln1), 1))
            for c in range(NCH):
                qk_high(c)

            def attention(A):
                act.sem_inc(A.prob_ready, 2)
                act.sem_inc(A.o_done, 1)
                for qd in range(QUADS):
                    act.sem_inc(A.stage_free[qd], 1)

                def quad(it, qd, more):
                    n = 2 * it + qd
                    begins = isinstance(n, int) and n == 0
                    for s, (c, kt, q0, diag, first, last) in enumerate(A.steps):
                        g = n * A.nsteps + s
                        for p in range(2):
                            act.wait_ge(A.st_ps, 2 * g + p + 1)
                            act.activation(A.prob[0:A.keys, s % 2, p, :, q0:CH],
                                           psum[0:A.keys, 2 * p:2 * p + 2, q0:CH], ACT.Exp, scale=SCALE)\
                                .then_inc(A.prob_ready, 1)
                        if s == 0 and not begins:
                            read_out(*after(it, qd, -1), A.steps[-1][0])
                        if s == 0 and not A.causal and more:
                            copy_values(*after(it, qd, 1))
                        if s > 0 and A.steps[s - 1][5]:
                            read_out(it, qd, A.steps[s - 1][0])

                def read_out(it, qd, c):
                    n = 2 * it + qd
                    act.wait_ge(A.pv_ps, 2 * n + c + 1 + 4)
                    act.wait_ge(A.stage_free[qd], it + 1)
                    act.activation(stage[:, qd, c * CH:(c + 1) * CH], bank(4), ACT.Copy).then_inc(A.o_done, 1)
                    if not A.causal and c == A.steps[-1][0]:
                        store_out(act, A, it, qd)

                def copy_values(it, qd):
                    act.activation(A.vq[0:A.keys, qd, 0, :, 0:HD], xvals[0:A.keys, bass.ds(it, 1), 64 * qd:64 * qd + 64]
                                   .rearrange("p o (h d) -> p (o h) d", h=4), ACT.Copy).then_inc(A.vq_ready, 1)

                if not A.causal:
                    act.wait_ge(xv_done, 2)
                    act.wait_ge(consts, 4)
                    copy_values(0, 0)
                over_iterations(act, quad, True)
                read_out(ITS - 1, QUADS - 1, A.steps[-1][0])

            act.wait_ge(v_ps, 8)
            for i, n in enumerate(("wo", "wctx", "wx")):
                act.dma_start(w3[:, :, i * D:(i + 1) * D], a[n]).then_inc(w_out3, 16)
            for half in range(2):
                act.wait_ge(qk_st[half], 16 * 12 * (NCH // 2 + 1))
            attention(SA)

            def attention_out(c):
                for m in range(KT):
                    act.wait_ge(op_ps, 2 * c + m + 1)
                    act.activation(attn_o[:, m, cols_of(c)], bank(2 * (c % 2) + m), ACT.Identity, bias=v_("bo", m))\
                        .then_inc(ctx_ready, 1)

            def first_state(c):
                for k in range(KT):
                    act.wait_ge(b1_set, 1)
                    act.wait_ge(ln2.scaled, 2 * c + k + 1)
                    act.activation(nrm[:, k, cols_of(c)], nrm[:, k, cols_of(c)], ACT.Identity,
                                   bias=b1_scaled[:, k:k + 1], scale=1 / (DT * DT)).then_inc(y_ready, 1)

            skewed((first_state, 5), (deviation(ln2), 3), (square(ln2), 2), (attention_out, 0))
            act.wait_ge(wff_in, 16)
            with act.Fori(0, NITER) as s:
                for u in range(2 * NCH):
                    at = slice((u // 2) * CH, (u // 2 + 1) * CH)
                    act.wait_ge(z_ps, 8 * s + 2 * (u // 2) + 2)
                    act.activation(act_u[:, u % 2, at], bank(u), ACT.Tanh, bias=v_("binl", u % 2))\
                        .then_inc(u_ready, 1)
                piece = bass.ds(s * WPIECE, WPIECE)
                act.activation(rounded(wff_hi[:, piece]), wff[:, piece], ACT.Copy).then_inc(wff_h, 1)
            for m in range(KT):
                act.wait_ge(xk_ps, m + 1)
                act.activation(xk_hi[:, m, :].bitcast(F32R), bank(4 + m, BATCH * CTXP), ACT.Identity,
                               bias=v_("xbk", m)).then_inc(xk_hi_s, 1)

            def third_high(c):
                for k in range(KT):
                    act.wait_ge(ln3.scaled, 2 * c + k + 1)
                    act.activation(rounded(nrm_hi[:, k, cols_of(c)]), nrm[:, k, cols_of(c)], ACT.Identity,
                                   bias=v_("b2", k)).then_inc(ln3.hi, 1)

            skewed((third_high, 4), (deviation(ln3), 2), (square(ln3), 1), chunks=2)
            act.sem_inc(gelu, 4)
            act.sem_inc(ff2_ps, 1)
            for c in range(NCH):
                norm, nc = norm_beside(c)
                for m in range(FT + 1):
                    if m < FT:
                        act.wait_ge(ff1_ps, FT * c + m + 1)
                        if m == 0:
                            act.wait_ge(ff2_ps, c + 1)
                        act.activation(hid[:, m, :], bank(m % 4), ACT.Gelu, bias=v_("ffb1", m)).then_inc(gelu, 1)
                    if m > 0:
                        act.wait_ge(gelu, FT * c + m + 4)
                        act.activation(rounded(hid_hi[:, m - 1, :]), hid[:, m - 1, :], ACT.Copy).then_inc(hid_h, 1)
                    if m == 3:
                        square(norm)(nc)
                deviation(norm)(nc)
                if c == 0:
                    third_high(2)
                    square(ln3)(3)
                    deviation(ln3)(3)
                    third_high(3)

            def xq_high(c):
                act.wait_ge(xq_st[c % 2], 16 * 6 * (c // 2) + 16 * 6)
                act.wait_ge(xk_st, 16 * 3 * KT)
                for m in range(KT):
                    act.wait_ge(xq_ps, 2 * c + m + 1)
                    act.activation(xpart_hi[:, c % 2, m, :].bitcast(F32R), bank(xq_bank(c) + m), ACT.Identity,
                                   bias=v_("xbq", m)).then_inc(xq_hi_s, 1)

            square(ln4)(NCH - 1)
            xq_high(0)
            deviation(ln4)(NCH - 1)
            for c in range(1, NCH):
                xq_high(c)
            attention(XA)

            def tree_high(c):
                act.wait_ge(ln5.out, 2 * c + 2)
                act.activation(rounded(tree_hi[:, :, cols_of(c)]), nrm[:, :, cols_of(c)], ACT.Copy)\
                    .then_inc(ln5.hi, 1)

            skewed((tree_high, 5), (deviation(ln5), 3), (square(ln5), 2))

            def activate(st):
                act.wait_ge(lg_ps, st.g + 1)
                act.wait_ge(dec_ready, st.g + 1)
                if not (isinstance(st.g, int) and st.g < 2):
                    act.wait_ge(msk_ready, st.g - 1)
                for half in range(2):
                    ins = act.activation(silu[:, st.buf, half, :], bank(2 * st.buf + half), ACT.Silu,
                                         bias=wt[:, st.tree, WT + half:WT + half + 1])
                ins.then_inc(silu_ready, 1)

            def high_part(st):
                act.wait_ge(msk_ready, st.g + 1)
                if not (isinstance(st.g, int) and st.g < 2):
                    act.wait_ge(out_ps, st.g - 1)
                act.activation(rounded(masked_hi[:, st.buf]), masked[:, st.buf], ACT.Copy).then_inc(msk_h, 1)

            tree_steps(act, activate, high_part, lambda st: None)

        @block.vector
        def _(dve):
            dve.sem_inc(qk_free, 3)

            def total(L):
                def chunk(c):
                    dve.wait_ge(*((x_in[c], 16) if L.ready is None else (L.ready, L.per * (c + 1) + L.plus)))
                    if L.at + c >= 2:
                        dve.wait_ge(L.mean, L.at + c - 1)
                    dve.tensor_tensor(L.sum_of(0, c), L.src[:, 0, cols_of(c)], L.src[:, 1, cols_of(c)], ALU.add)\
                        .then_inc(L.total, 1)
                return chunk

            def center(L):
                def chunk(c):
                    dve.wait_ge(L.mean, L.at + c + 1)
                    for k in range(KT):
                        dve.tensor_tensor(L.d[:, k, cols_of(c)], L.src[:, k, cols_of(c)], bank(L.bank(c)), ALU.subtract)\
                            .then_inc(L.d_ready, 1)
                return chunk

            def total_squares(L):
                def chunk(c):
                    dve.wait_ge(L.sq, L.at + c + 1)
                    if L.at + c >= 2:
                        dve.wait_ge(L.var, L.at + c - 1)
                    dve.tensor_tensor(L.sum_of(1, c), L.square(c)[:, 0], L.square(c)[:, 1], ALU.add).then_inc(L.sqs, 1)
                return chunk

            def invert(L):
                def chunk(c):
                    dve.wait_ge(L.sd, L.at + c + 1)
                    if L.at + c >= 2:
                        dve.wait_ge(L.bc, L.at + c - 1)
                    dve.reciprocal(rs[:, c % 2, 0, :], sd[:, c % 2, 0, :]).then_inc(L.rs, 1)
                return chunk

            def scale(L):
                def chunk(c):
                    dve.wait_ge(L.bc, L.at + c + 1)
                    for k in range(KT):
                        at, r = nrm[:, k, cols_of(c)], bank(L.bank(c))
                        if L.gain:
                            dve.scalar_tensor_tensor(at, at, v_(L.gain, k), r, ALU.mult, ALU.mult).then_inc(L.scaled, 1)
                        else:
                            dve.tensor_tensor(at, at, r, ALU.mult).then_inc(L.out, 1)
                return chunk

            dve.wait_ge(c_in, 64)
            dve.tensor_scalar(b1_scaled[:], vec[:, VEC["b1"][0]:VEC["b1"][0] + KT], 1 / (DT * DT), None, ALU.mult)\
                .then_inc(b1_set, 1)

            def invert_first(c):
                r, r2 = rs[:, c % 2, 0, :], rs[:, c % 2, 1, :]
                dve.wait_ge(ln1.sd, c + 1)
                if c >= 2:
                    dve.wait_ge(ln1.bc, c - 1)
                dve.reciprocal(r, sd[:, c % 2, 0, :]).then_inc(xl_ready, 1)
                dve.wait_ge(xl_ready, c + 1)
                dve.tensor_tensor(r2, r, r, ALU.mult).then_inc(r1sq, 1)
                dve.wait_ge(r1sq, c + 1)
                dve.tensor_tensor(sd[:, c % 2, 1, :], r2, bank(ln1.bank(c), TPC), ALU.mult).then_inc(v2, 1)

            def invert_second(c):
                dve.wait_ge(sd2, c + 1)
                dve.reciprocal(rs[:, c % 2, 1, :], sd[:, c % 2, 1, :]).then_inc(ln1.rs, 1)

            def scale_twice(c):
                dve.wait_ge(ln1.bc, c + 1)
                for k in range(KT):
                    at = res[:, k, cols_of(c)]
                    dve.tensor_tensor(at, at, bank(ln1.bank(c)), ALU.mult).then_inc(rs2, 1)
                dve.wait_ge(rs2, 2 * c + 2)
                for k in range(KT):
                    dve.scalar_tensor_tensor(nrm[:, k, cols_of(c)], res[:, k, cols_of(c)], v_("g_attn", k), bank(4),
                                             ALU.mult, ALU.mult).then_inc(ln1.scaled, 1)

            def qk_low(c, tiles=range(4)):
                dve.wait_ge(qk_st[c % 2], 16 * 12 * (c // 2) + 16 * 12)
                for m in tiles:
                    dve.wait_ge(qk_hi, 4 * c + m + 1)
                    dve.scalar_tensor_tensor(part_lo[:, c % 2, m, :].bitcast(F32R), qk_bank(c, m), v_("bqk", m),
                                             part_hi[:, c % 2, m, :], ALU.add, ALU.subtract).then_inc(qk_free, 1)

            skewed((scale_twice, 5), (invert_second, 4), (invert_first, 3), (total_squares(ln1), 2), (center(ln1), 1),
                   (total(ln1), 0))
            for c in by_batch[0]:
                qk_low(c)
            dve.wait_ge(w_in3, 32)
            for u in range(8):
                dve.wait_ge(v_ps, u + 1)
                for t in range(2):
                    b, tt = u // 4, 2 * (u % 4) + t
                    dve.tensor_tensor(values[:, b::2, tt, :],
                                      psum[:, u % 4, t * D:(t + 1) * D].rearrange("p (k f) -> p k f", k=KT),
                                      vbias[:].rearrange("p (k f) -> p k f", k=KT), ALU.add).then_inc(v_done, 1)

            def qk_beside(u):
                if u % 3 == 0 and u // 3 in range(3, 11):
                    qk_low(by_batch[1][(u // 3 - 3) // 4], [(u // 3 - 3) % 4])

            def attention(A, ready, beside=None):
                dve.sem_inc(A.s1_free, A.nbanks)
                dve.sem_inc(A.neg, 1)

                dve.sem_inc(A.rec_free, 2)
                if A.causal:
                    dve.sem_inc(A.sums_in, 16)
                dve.wait_ge(consts, 1 if A.causal else 4)

                def maximum(it, qd, u):
                    n = 2 * it + qd
                    h, i, k0, nk, diag = A.units[u]
                    row = 16 * (h % 2) + 8 * (h // 2) + i
                    dve.wait_ge(A.s1_ps, n * A.nunits + u + 1)
                    if A.causal and u == 0 and not (isinstance(n, int) and n == 0):
                        dve.wait_ge(A.mx, n)
                    if A.causal:
                        at = 2 * row + k0 // CH
                        dve.tensor_reduce(part_max[:, at:at + 1], psum[:, 5 + u % A.nbanks, 0:nk], AX_X, ALU.max)\
                            .then_inc(A.s1_free, 1)
                    else:
                        dve.tensor_reduce(row_max[:].rearrange("q (j p i) -> q p j i", j=2, p=2)[:, :, :, i],
                                          psum[:, 5 + u % A.nbanks, 0:nk].rearrange("q (p j k) -> q p j k", p=2, j=2),
                                          AX_X, ALU.max).then_inc(A.s1_free, 1)

                def gather(it, qd):
                    n = 2 * it + qd
                    if A.causal:
                        dve.wait_ge(A.s1_free, (n + 1) * A.nunits + A.nbanks)
                        dve.wait_ge(A.mx_ps, n + 2)
                        dve.tensor_reduce(row_max[:], part_max[:].rearrange("p (r h) -> p r h", h=2), AX_X, ALU.max)\
                            .then_inc(A.mx, 1)

                def negate(it, qd):
                    n = 2 * it + qd
                    dve.wait_ge(A.mx_ps, n + 1 + 2)
                    dve.wait_ge(A.mrow[qd], 16 * it + 16)
                    dve.tensor_scalar(neg_max[:, qd, :], psum[0:32, 7, 0:P], -1.0, None, ALU.mult).then_inc(A.neg, 1)

                def invert_sums(it):
                    if A.causal:
                        dve.wait_ge(A.sums_in, 16 * it + 16)
                    elif not (isinstance(it, int) and it == 0):
                        sums_done, before = A.nth("sums_in", it - 1)
                        dve.wait_ge(sums_done, 16 * before + 16)
                    dve.wait_ge(A.rec_free, it + 1)
                    dve.reciprocal(A.recip[:], A.sums[:]).then_inc(A.rec, 1)

                for u in range(A.nunits):
                    if beside:
                        beside(u)
                    maximum(0, 0, u)
                gather(0, 0)
                negate(0, 0)
                for u in range(A.lead):
                    maximum(0, 1, u)
                if A.lead == A.nunits:
                    negate(0, 1)

                def quad(it, qd, more):
                    todo = [(d, u) for step in A.plan for d, u in step]
                    if not A.causal and more and not (isinstance(it, int) and it == qd == 0):
                        negate(*after(it, qd, 1))
                    if more == 0 and qd == A.recip_qd:
                        invert_sums(it)
                    for k, (d, u) in enumerate(todo):
                        if d <= more:
                            maximum(*after(it, qd, d), u)
                        if k == len(todo) // 2 and qd == A.recip_qd and more:
                            invert_sums(it)
                        if (d, u) == (1, A.nunits - 1) and more:
                            gather(*after(it, qd, 1))
                        if (d, u) == (2, 1) and A.causal and more:
                            negate(*after(it, qd, 1))

                over_iterations(dve, quad, not A.causal)

                def normalize(c):
                    its = ITS if c in by_batch[1] else ITS - 1
                    dve.wait_ge(A.num, 16 * (QUADS * (ITS - 1) - ("num1" in A.late)))
                    if A.late:
                        dve.wait_ge(A.late["num1"], 16)
                    if its == ITS:
                        dve.wait_ge(A.num_last, 16 if A.late else 16 * QUADS)
                        if A.late:
                            dve.wait_ge(A.num, 16 * QUADS * (ITS - 1))
                    if A.late:
                        dve.wait_ge(A.den_in, 16 * (ITS - 2))
                    den_done, before = A.nth("den_in", its - 1)
                    dve.wait_ge(den_done, 16 * before + 16)
                    num, den = A.out[:, :, cols_of(c)], A.den[:, :, cols_of(c)]
                    dve.tensor_tensor(num, num, den, ALU.mult).then_inc(ready, 1)

                def normalize_late(c):
                    if c in by_batch[1]:
                        normalize(c)

                for c in by_batch[0]:
                    normalize(c)
                invert_sums(ITS)
                return normalize_late

            def add_attention(c):
                dve.wait_ge(ctx_ready, 2 * c + 2)
                at = cols_of(c)
                dve.tensor_tensor(res[:, :, at], attn_o[:, :, at], res[:, :, at], ALU.add).then_inc(res1, 1)

            normalize_late = attention(SA, attn_ready, qk_beside)
            skewed((normalize_late, 0), (scale(ln2), 5), (invert(ln2), 4), (total_squares(ln2), 3), (center(ln2), 2),
                   (add_attention, 1), (total(ln2), 1))
            dve.wait_ge(scan_init, 1)
            with dve.Fori(0, NITER) as s:
                for u in range(2 * NCH):
                    at = slice((u // 2) * CH, (u // 2 + 1) * CH)
                    dve.wait_ge(u_ready, 8 * s + u + 1)
                    dve.wait_ge(y_ready, 8 * s + u + 1)
                    dve.scalar_tensor_tensor(act_u[:, u % 2, at], nrm[:, u % 2, at], -DT * DT, act_u[:, u % 2, at],
                                             ALU.mult, ALU.add).then_inc(a_ready, 1)
                    dve.wait_ge(a_ready, 8 * s + u + 1)
                    dve.scalar_tensor_tensor(vel[:, u % 2, at], vel[:, u % 2, at], 1 - DT, act_u[:, u % 2, at],
                                             ALU.mult, ALU.add).then_inc(vel_ready, 1)
                piece = bass.ds(s * WPIECE, WPIECE)
                dve.wait_ge(wff_h, s + 1)
                dve.tensor_tensor(rounded(wff_lo[:, piece]), wff[:, piece], wff_hi[:, piece], ALU.subtract)\
                    .then_inc(wff_l, 1)
            for m in range(KT):
                dve.wait_ge(xk_hi_s, m + 1)
                dve.scalar_tensor_tensor(xk_lo[:, m, :].bitcast(F32R), bank(4 + m, BATCH * CTXP), v_("xbk", m),
                                         xk_hi[:, m, :], ALU.add, ALU.subtract).then_inc(xk_free, 1)
            dve.wait_ge(w_late, 16 * 4)
            for b in range(BATCH):
                dve.wait_ge(xv_ps, b + 1)
                dve.tensor_tensor(xvals[0:CTX, b::2, :], bank(6 + b, D)[0:CTX].rearrange("p (k f) -> p k f", k=KT),
                                  xvbias[0:CTX, :].rearrange("p (k f) -> p k f", k=KT), ALU.add).then_inc(xv_done, 1)

            def add_state(c):
                for m in range(KT):
                    dve.wait_ge(y_ready, 2 * NCH * NITER + 2 * c + m + 1)
                    at = res[:, m, cols_of(c)]
                    dve.scalar_tensor_tensor(at, nrm[:, m, cols_of(c)], DT * DT, at, ALU.mult, ALU.add).then_inc(res2, 1)

            def third_low(c):
                for k in range(KT):
                    dve.wait_ge(ln3.hi, 2 * c + k + 1)
                    dve.scalar_tensor_tensor(rounded(nrm_lo[:, k, cols_of(c)]), nrm[:, k, cols_of(c)], v_("b2", k),
                                             nrm_hi[:, k, cols_of(c)], ALU.add, ALU.subtract).then_inc(ln3.out, 1)

            skewed((third_low, 5), (scale(ln3), 4), (invert(ln3), 3), (total_squares(ln3), 2), (center(ln3), 1),
                   (add_state, 0), (total(ln3), 0), chunks=2)
            dve.sem_inc(res4, 2)
            for c in range(NCH):
                norm, nc = norm_beside(c)
                if c == 0:
                    add_state(2)
                total(norm)(nc)
                if c == 1:
                    third_low(3)
                for m in range(FT):
                    dve.wait_ge(hid_h, FT * c + m + 1)
                    dve.tensor_tensor(rounded(hid_lo[:, m, :]), hid[:, m, :], hid_hi[:, m, :], ALU.subtract)\
                        .then_inc(hid_l, 1)
                    if m == 1:
                        center(norm)(nc)
                    if m == 4:
                        total_squares(norm)(nc)
                invert(norm)(nc)
                if c == 0:
                    add_state(3)
                    total(ln3)(3)
                scale(norm)(nc)
                if c == 0:
                    center(ln3)(3)
                    third_low(2)
                    for stage in (total_squares, invert, scale):
                        stage(ln3)(3)
                dve.wait_ge(ff2_ps, c + 2)
                dve.wait_ge(x0_added, 2 * c + 2)
                for m in range(KT):
                    at = res[:, m, cols_of(c)]
                    dve.scalar_tensor_tensor(at, bank(4 + m), v_("ffb2", m), at, ALU.add, ALU.add).then_inc(res4, 1)

            def xq_low(c):
                dve.wait_ge(xq_st[c % 2], 16 * 6 * (c // 2) + 16 * 6)
                dve.wait_ge(xk_st, 16 * 3 * KT)
                for m in range(KT):
                    dve.wait_ge(xq_hi_s, 2 * c + m + 1)
                    dve.scalar_tensor_tensor(xpart_lo[:, c % 2, m, :].bitcast(F32R), bank(xq_bank(c) + m),
                                             v_("xbq", m), xpart_hi[:, c % 2, m, :], ALU.add, ALU.subtract)\
                        .then_inc(xq_free, 1)

            total(ln4)(NCH - 1)
            center(ln4)(NCH - 1)
            total_squares(ln4)(NCH - 1)
            xq_low(0)
            invert(ln4)(NCH - 1)
            xq_low(1)
            scale(ln4)(NCH - 1)
            for c in range(2, NCH):
                xq_low(c)

            def add_cross(c):
                for m in range(KT):
                    dve.wait_ge(xo_ps, 2 * c + m + 1)
                    at = res[:, m, cols_of(c)]
                    dve.scalar_tensor_tensor(at, bank(2 * (c % 2) + m), v_("xbo", m), at, ALU.add, ALU.add)\
                        .then_inc(res5, 1)

            def tree_low(c):
                dve.wait_ge(ln5.hi, c + 1)
                at = cols_of(c)
                dve.tensor_tensor(rounded(nrm_lo[:, :, at]), nrm[:, :, at], tree_hi[:, :, at], ALU.subtract)\
                    .then_inc(ln5.scaled, 1)

            normalize_late = attention(XA, xattn_ready)
            skewed((normalize_late, 0), (tree_low, 6), (scale(ln5), 5), (invert(ln5), 4), (total_squares(ln5), 3),
                   (center(ln5), 2), (add_cross, 1), (total(ln5), 1))
            dve.sem_inc(tree_out, 1)

            def decisions(st):
                dve.wait_ge(lg_ps, st.g + 1)
                if not (isinstance(st.g, int) and st.g < 2):
                    dve.wait_ge(cnt_ps, st.g - 1)
                dve.tensor_scalar(decide[:, st.buf, :], bank(2 * st.buf), wt[:, st.tree, WT:WT + 1], 0.0,
                                  ALU.add, ALU.is_gt).then_inc(dec_ready, 1)

            def mask(st):
                dve.wait_ge(cnt_ps, st.g + 1)
                dve.wait_ge(silu_ready, st.g + 1)
                if not (isinstance(st.g, int) and st.g < 2):
                    dve.wait_ge(out_ps, st.g - 1)
                dve.scalar_tensor_tensor(masked[:, st.buf], psum[:, 4:6, :], 0.0, silu[:, st.buf],
                                         ALU.is_equal, ALU.mult).then_inc(msk_ready, 1)
                dve.wait_ge(msk_h, st.g + 1)
                dve.tensor_tensor(rounded(masked_lo[:, st.buf]), masked[:, st.buf], masked_hi[:, st.buf], ALU.subtract)\
                    .then_inc(msk_l, 1)

            def add_out(st):
                dve.wait_ge(out_ps, st.g + 1)
                dve.tensor_tensor(res[:, :, st.at], psum[:, 6:8, :], res[:, :, st.at], ALU.add).then_inc(tree_out, 1)

            tree_steps(dve, decisions, mask, add_out)

        @block.tensor
        def _(pe):
            pe.wait_ge(c_in, 64)

            def mean(L):
                def chunk(c):
                    pe.wait_ge(L.total, L.at + c + 1)
                    pe.matmul(bank(L.bank(c)), mean_w[:], L.sum_of(0, c), start=True, stop=True).then_inc(L.mean, 1)
                return chunk

            def variance(L):
                def chunk(c):
                    pe.wait_ge(L.sqs, L.at + c + 1)
                    for t in range(TPC):
                        mm = pe.matmul(bank(L.bank(c))[:, t:t + 1], L.sum_of(1, c)[:, t * P:(t + 1) * P],
                                       mean_w[:, 0:1], start=True, stop=True)
                    mm.then_inc(L.var, 1)
                return chunk

            def spread_out(L):
                def chunk(c):
                    pe.wait_ge(L.rs, L.at + c + 1)
                    if L is ln1 and c >= 1:
                        pe.wait_ge(L.scaled, 2 * c)
                    for i in range(2 if L is ln1 else 1):
                        for t in range(TPC):
                            mm = pe.matmul(bank((L.bank(c), 4)[i])[:, t * P:(t + 1) * P],
                                           rs[:, c % 2, i, t:t + 1].to_broadcast([P, P]), ident[:],
                                           start=True, stop=True)
                    mm.then_inc(L.bc, 1)
                return chunk

            def qk_projection(c, tiles=range(4)):
                pe.wait_ge(w_in3, 32)
                pe.wait_ge(ln1.out, 2 * c + 2)
                for m in tiles:
                    pe.wait_ge(qk_free, 4 * c + m + 1)
                    for k in range(KT):
                        mm = pe.matmul(qk_bank(c, m), w3[:, k, m * P:(m + 1) * P], nrm[:, k, cols_of(c)],
                                       start=k == 0, stop=k == 1)
                    mm.then_inc(qk_ps, 1)

            skewed((spread_out(ln1), 4), (variance(ln1), 2), (mean(ln1), 0))
            for c in by_batch[0]:
                qk_projection(c)
            for u in range(8):
                if u >= 4:
                    pe.wait_ge(v_done, 2 * (u - 3))
                for t in range(2):
                    for k in range(KT):
                        at = (2 * u + t) * P
                        mm = pe.matmul(psum[:, u % 4, t * D:(t + 1) * D], nrm[:, k, at:at + P],
                                       w3[:, k, 2 * D:3 * D], start=k == 0, stop=k == 1)
                mm.then_inc(v_ps, 1)

            def qk_beside(u):
                if u == 0:
                    pe.wait_ge(v_done, 16)
                if u % 3 == 0 and u // 3 in range(2, 10):
                    qk_projection(by_batch[1][(u // 3 - 2) // 4], [(u // 3 - 2) % 4])
                if u == 36:
                    pe.wait_ge(qk_free, 3 + 4 * NCH)

            def attention(A, beside=None):
                pe.sem_inc(A.mx_ps, 2)
                pe.sem_inc(A.pv_ps, 4)

                def unit(it, qd, u):
                    n = 2 * it + qd
                    h, i, k0, nk, diag = A.units[u]
                    if u == 0:
                        pe.wait_ge(A.ld1[qd], A.ld1_n * (it + 1))
                    pe.wait_ge(A.s1_free, n * A.nunits + u + 1)
                    if A.nbanks == 3 and u == 2:
                        pe.wait_ge(A.neg, n + 1)
                    if A.causal:
                        mm = pe.matmul(psum[:, 5 + u % A.nbanks, 0:nk], A.q1[:, qd, i * P:(i + 1) * P],
                                       A.k1[:, qd, h, k0:k0 + nk], start=True, stop=not diag)
                        if diag:
                            mm = pe.matmul(psum[:, 5 + u % A.nbanks, nk - P:nk], ident_b[:], causal_b[:], start=False, stop=True)
                    else:
                        pe.sem_inc(passed, 1)
                        mm = pe.matmul(psum[:, 5 + u % A.nbanks, 0:nk].rearrange("q (h k) -> q h k", h=4),
                                       A.q1[:, qd, i * P:(i + 1) * P], A.k1[:, qd, :, bass.ds(it * CTXP, CTXP)],
                                       start=True, stop=True)
                    mm.then_inc(A.s1_ps, 1)

                def turn(it, qd):
                    n = 2 * it + qd
                    if A.causal:
                        pe.wait_ge(A.mx, n + 1)
                    else:
                        pe.wait_ge(A.s1_free, (n + 1) * A.nunits + A.nbanks)
                    pe.wait_ge(A.neg, n + 1)
                    pe.transpose(psum[0:32, 7, 0:P], row_max[:], ident[:]).then_inc(A.mx_ps, 1)

                def scores(it, qd, s, p):
                    n = 2 * it + qd
                    c, kt, q0, diag, first, last = A.steps[s]
                    g = n * A.nsteps + s
                    pe.wait_ge(A.prob_ready, 2 * g + p + 1)
                    for j in range(2):
                        mm = pe.matmul(psum[0:A.keys, 2 * p + j, q0:CH],
                                       A.k2[:, qd, p, j, kt * P:kt * P + A.keys],
                                       A.q2[:, qd, p, c * CH + q0:(c + 1) * CH], start=True, stop=True)
                    mm.then_inc(A.st_ps, 1)

                def weigh(it, qd, s):
                    n = 2 * it + qd
                    c, kt, q0, diag, first, last = A.steps[s]
                    g = n * A.nsteps + s
                    if s == 0:
                        pe.wait_ge(A.vq_ready, n + 1)
                    if first:
                        pe.wait_ge(A.o_done, 2 * n + c + 1)
                    if diag:
                        k = sum(st[3] for st in A.steps[:s + 1])
                        pe.wait_ge(A.prob_masked, 2 * (n * A.ndiag + k))
                    pe.wait_ge(A.prob_ready, 2 * g + 2 + 2)
                    for h in range(4):
                        mm = pe.matmul(psum[32 * h:32 * h + 32, 4, q0:CH], A.vq[:, qd, kt, h, :],
                                       A.prob[:, s % 2, h // 2, h % 2, q0:CH], start=first, stop=last)
                    if last:
                        mm.then_inc(A.pv_ps, 1)

                for u in range(A.nunits):
                    if beside:
                        beside(u)
                    unit(0, 0, u)
                turn(0, 0)
                for u in range(A.lead):
                    unit(0, 1, u)
                if A.lead == A.nunits:
                    turn(0, 1)

                def ahead(it, qd, units, more):
                    for d, u in units:
                        if d <= more:
                            unit(*after(it, qd, d), u)
                        if (d, u) == (2, 1) and A.causal and more:
                            turn(*after(it, qd, 1))

                def quad(it, qd, more):
                    n = 2 * it + qd
                    pe.wait_ge(A.ld2[qd], A.ld2_n * (it + 1))
                    pe.wait_ge(A.mrow[qd], 16 * (it + 1) + 16)
                    for s in range(A.nsteps):
                        scores(it, qd, s, 0)
                        if s == 0 and not A.causal and more and not (isinstance(n, int) and n == 0):
                            turn(*after(it, qd, 1))
                        ahead(it, qd, A.share(s, 0), more)
                        scores(it, qd, s, 1)
                        ahead(it, qd, A.share(s, 1), more)
                        if s > 0:
                            weigh(it, qd, s - 1)
                        elif not (isinstance(n, int) and n == 0):
                            weigh(*after(it, qd, -1), A.nsteps - 1)
                        ahead(it, qd, A.share(s, 2) + A.share(s, 3), more)

                over_iterations(pe, quad, True)
                weigh(ITS - 1, QUADS - 1, A.nsteps - 1)

            pe.wait_ge(qk_free, 3 + 4 * NCH // BATCH)
            pe.wait_ge(consts, 1)
            attention(SA, qk_beside)

            def project(w, at, src, ready, per, done, bank_of, read):
                def chunk(c):
                    pe.wait_ge(ready, per * (c + 1))
                    if c >= 2:
                        pe.wait_ge(read, 2 * c - 2)
                    for m in range(KT):
                        for k in range(KT):
                            mm = pe.matmul(bank(bank_of(c) + m), w[:, k, at + m * P:at + (m + 1) * P],
                                           src[:, k, cols_of(c)], start=k == 0, stop=k == 1)
                        mm.then_inc(done, 1)
                return chunk

            pe.wait_ge(w_out3, 48)
            skewed((project(w3, 0, nrm, attn_ready, 1, op_ps, lambda c: 2 * (c % 2), ctx_ready), 0),
                   (spread_out(ln2), 4), (variance(ln2), 3), (mean(ln2), 1))
            pe.wait_ge(wx01_ready, 1)
            for c in range(NCH):
                at = slice(c * CH, (c + 1) * CH)
                pe.wait_ge(y_ready, 2 * c + 2)
                for m in range(KT):
                    mo = slice(m * P, (m + 1) * P)
                    for k in range(KT):
                        pe.matmul(bank(2 * c + m), w3[:, k, D + m * P:D + (m + 1) * P], attn_o[:, k, at],
                                  start=k == 0, stop=False, skip_group_check=True)
                    for k in range(KT):
                        mm = pe.matmul(bank(2 * c + m), wx01[:, k, mo], nrm[:, k, at], start=False, stop=k == 1,
                                       skip_group_check=True)
                    mm.then_inc(z_ps, 1)
            with pe.Fori(0, NITER - 1) as s:
                for c in range(NCH):
                    at = slice(c * CH, (c + 1) * CH)
                    pe.wait_ge(vel_ready, 8 * s + 2 * c + 2)
                    for m in range(KT):
                        for k in range(KT):
                            mm = pe.matmul(bank(2 * c + m), wx01[:, k, m * P:(m + 1) * P], vel[:, k, at],
                                           start=False, stop=k == 1, skip_group_check=True)
                        mm.then_inc(z_ps, 1)
            pe.wait_ge(u_ready, 2 * NCH * NITER)
            pe.wait_ge(w_late, 16 * 4)
            for m in range(KT):
                for k in range(KT):
                    mm = pe.matmul(bank(4 + m, BATCH * CTXP), wx4[:, k, D + m * P:D + (m + 1) * P], ctx_t[:, k, :],
                                   start=k == 0, stop=k == 1)
                mm.then_inc(xk_ps, 1)
            for b in range(BATCH):
                for k in range(KT):
                    mm = pe.matmul(bank(6 + b, D)[0:CTX], ctx_t[:, k, b * CTXP:b * CTXP + CTX], wx4[:, k, 2 * D:3 * D],
                                   start=k == 0, stop=k == 1)
                mm.then_inc(xv_ps, 1)
            pe.wait_ge(xv_done, 2)
            pe.wait_ge(xk_free, 2)
            skewed((spread_out(ln3), 3), (variance(ln3), 2), (mean(ln3), 0), chunks=2)
            pe.wait_ge(wff_l, NITER)
            for c in range(NCH):
                norm, nc = norm_beside(c)
                pe.wait_ge(ln3.out, 2 * c + 2)
                for m in range(FT):
                    pe.wait_ge(gelu, FT * c + m + 1)
                    for k in range(KT):
                        at = slice(k * FF + m * P, k * FF + (m + 1) * P)
                        mm = three(pe, bank(m % 4), wff_hi[:, at], wff_lo[:, at], nrm_hi[:, k, cols_of(c)],
                                   nrm_lo[:, k, cols_of(c)], k == 0, k == KT - 1)
                    mm.then_inc(ff1_ps, 1)
                    if m == 1:
                        mean(norm)(nc)
                pe.wait_ge(res4, 2 * c + 2)
                for k in range(FT):
                    pe.wait_ge(hid_l, FT * c + k + 1)
                    for m in range(KT):
                        at = slice(KT * FF + k * D + m * P, KT * FF + k * D + (m + 1) * P)
                        mm = three(pe, bank(4 + m), wff_hi[:, at], wff_lo[:, at], hid_hi[:, k, :], hid_lo[:, k, :],
                                   k == 0, k == FT - 1)
                    if k == 0:
                        variance(norm)(nc)
                    if k == 2:
                        spread_out(norm)(nc)
                    if c == 0 and k in (3, 5, 7):
                        (mean, variance, spread_out)[(k - 3) // 2](ln3)(3)
                mm.then_inc(ff2_ps, 1)
            xq_projection = project(wx4, 0, nrm, ln4.out, 2, xq_ps, xq_bank, xq_free)
            mean(ln4)(NCH - 1)
            xq_projection(0)
            variance(ln4)(NCH - 1)
            xq_projection(1)
            spread_out(ln4)(NCH - 1)
            for c in range(2, NCH):
                xq_projection(c)
            pe.wait_ge(xq_free, 2 * NCH)
            pe.wait_ge(xk_in, 16 * 4 * QUADS)
            attention(XA)
            skewed((project(wx4, 3 * D, wide, xattn_ready, 1, xo_ps, lambda c: 2 * (c % 2), res5), 0),
                   (spread_out(ln5), 4), (variance(ln5), 3), (mean(ln5), 1))
            pe.wait_ge(consts, 3)

            def logits(st):
                if not (isinstance(st.g, int) and st.g < 2):
                    pe.wait_ge(silu_ready, st.g - 1)
                else:
                    pe.wait_ge(ln5.scaled, st.g + 1)
                if st.chunk == 0:
                    pe.wait_ge(wt_l, st.trees + 1)
                for half in range(2):
                    for k in range(KT):
                        o = k * 2 * P + half * P
                        mm = three(pe, bank(2 * st.buf + half), wt_hi[:, st.tree, o:o + P], wt_lo[:, st.tree, o:o + P],
                                   tree_hi[:, k, st.at], nrm_lo[:, k, st.at], k == 0, k == KT - 1)
                mm.then_inc(lg_ps, 1)

            def counts(st):
                pe.wait_ge(dec_ready, st.g + 1)
                if isinstance(st.g, int) and st.g == 0:
                    pe.wait_ge(ln5.scaled, NCH)
                else:
                    pe.wait_ge(msk_ready, st.g)
                for half in range(2):
                    mm = pe.matmul(bank(4 + half), sel[:, half * P:(half + 1) * P], decide[:, st.buf, :],
                                   start=True, stop=True)
                mm.then_inc(cnt_ps, 1)

            def outputs(st):
                pe.wait_ge(msk_l, st.g + 1)
                pe.wait_ge(tree_out, st.g + 1)
                for m in range(KT):
                    for half in range(2):
                        o = 2 * P * KT + half * D + m * P
                        mm = three(pe, bank(6 + m), wt_hi[:, st.tree, o:o + P], wt_lo[:, st.tree, o:o + P],
                                   masked_hi[:, st.buf, half, :], masked_lo[:, st.buf, half, :], half == 0, half == 1)
                mm.then_inc(out_ps, 1)

            tree_steps(pe, logits, counts, outputs)


INS = ["xT", "vec", "ident", "causal", "mean_w", "wqkv", "vbias", "wo", "wctx", "wx", "wff", "wx4", "wt",
       "sel", "ctxT", "xvbias"]


def kernel(**inp):
    import numpy as np
    import concourse.bacc as bacc
    from concourse.bass_utils import run_bass_kernel_spmd

    f = {k: np.asarray(v) for k, v in inp.items()}

    def tiles(w):
        return w.reshape(-1, P, w.shape[1]).transpose(1, 0, 2)

    def cols(v):
        return v.reshape(-1, P).T

    A, X, T = "L0_attn_", "L0_xattn_", "L0_ffn_"
    bin2 = f[T + "b_in"].reshape(TREES, NODES)
    turn = np.zeros((P, NODES), np.float32)
    for node in range(NODES):
        child = node
        while child:
            turn[(child - 1) // 2, node] = 1.0 if child % 2 == 0 else -1.0
            child = (child - 1) // 2
    turn[INNER] = -(turn > 0).sum(0)
    sel = np.ones((P, 2 * P), np.float32)
    sel[:, :INNER], sel[:, P:] = turn[:, :INNER], turn[:, INNER:]
    qkv_b = f[A + "qkv_b"]
    vec = {"bqk": cols(qkv_b[:2 * D]), "bo": cols(f[A + "out_b"]), "binl": cols(f[A + "b_inl"]),
           "ffb1": cols(f[A + "ff_b1"]), "ffb2": cols(f[A + "ff_b2"]), "xbq": cols(f[X + "bq"]),
           "xbk": cols(f[X + "bk"]), "xbo": cols(f[X + "bo"]),
           "eps": np.full((P, 1), EPS, np.float32)}
    for n in ("g_attn", "b_attn", "g1", "b1", "g2", "b2"):
        vec[n] = cols(f[A + n])
    win = f[T + "W_in"].reshape(TREES, NODES, KT, P).transpose(0, 3, 2, 1)
    wout = f[T + "W_out"].T.reshape(TREES, NODES, D)
    wt = np.zeros((TREES, P, WT + 2), np.float32)
    wt[..., WT:] = 1.0
    wt[:, :INNER, WT], wt[:, :, WT + 1] = bin2[:, :INNER], bin2[:, INNER:]
    into = wt[:, :, :2 * P * KT].reshape(TREES, P, KT, 2 * P)
    into[..., :INNER], into[..., P:] = win[..., :INNER], win[..., INNER:]
    wt[:, :INNER, 2 * P * KT:2 * P * KT + D], wt[:, :, 2 * P * KT + D:WT] = wout[:, :INNER], wout[:, INNER:]
    context = np.concatenate([f["ctx_1024"], f["ctx_1024"][:, -1:]], 1).reshape(BATCH * CTXP, D)
    q, k = np.arange(P)[:, None], np.arange(P)[None]
    arrays = {
        "xT": tiles(f["x"].reshape(TOK, D).T),
        "vec": np.concatenate([vec[n] for n in VEC], 1),
        "ident": np.eye(P, dtype=np.float32),
        "causal": np.where(k <= q, 0.0, LOW).astype(np.float32),
        "mean_w": np.full((P, P), 1.0 / D, np.float32),
        "wqkv": tiles(f[A + "qkv_w"]),
        "vbias": np.tile(qkv_b[None, 2 * D:], (P, 1)),
        "wo": tiles(f[A + "out_w"]), "wctx": tiles(f[A + "w_ctx"]), "wx": tiles(f[A + "w_x"]),
        "wff": np.concatenate([tiles(f[A + n]).reshape(P, -1) for n in ("ff_w1", "ff_w2")], 1),
        "wx4": np.concatenate([tiles(f[X + n].T) for n in ("Wq", "Wk", "Wv", "Wo")], 2),
        "wt": wt,
        "sel": sel, "ctxT": tiles(context.T), "xvbias": np.tile(f[X + "bv"][None], (P, 1)),
    }
    nc = bacc.Bacc("TRN2", target_bir_lowering=False, num_devices=1)
    aps, feed = {}, {}
    for n in INS:
        arr = np.ascontiguousarray(arrays[n])
        feed[f"in_{n}"] = arr
        aps[n] = nc.dram_tensor(f"in_{n}", arr.shape, mybir.dt.from_np(arr.dtype), kind="ExternalInput").ap()
    out = nc.dram_tensor("out_t", (P, KT, TOK), F32, kind="ExternalOutput").ap()
    layer(nc, aps, out)
    r = run_bass_kernel_spmd(nc, [feed], core_ids=[0])
    return np.ascontiguousarray(r.results[0]["out_t"].transpose(2, 1, 0).reshape(BATCH, SEQ, D))
```
